# Optimizing a Trainium2 kernel written in Bass

```python
import numpy as np
import jax
import jax.numpy as jnp

def _softmax(x, axis=-1):
    return jax.nn.softmax(x, axis=axis)

def _gelu(x):
    return jax.nn.gelu(x, approximate=True)

def _silu(x):
    return jax.nn.silu(x)

def _sigmoid(x):
    return jax.nn.sigmoid(x)

def _layernorm(x, axis=-1, eps=1e-05):
    m = jnp.mean(x, axis=axis, keepdims=True)
    v = jnp.var(x, axis=axis, keepdims=True)
    return (x - m) / jnp.sqrt(v + eps)

def _scatter_add(tgt, idx, src, axis=0):
    return tgt.at[idx].add(src)

def _segment_sum(src, seg, n):
    return jax.ops.segment_sum(src, seg, n)
kernel_name = 'mk_gnn_ffn_d4_gnn_r32_4434ad'

def setup_inputs(seed: int=0):
    np.random.seed(seed)
    _w = jnp.asarray

    def _rec_inputs():
        import jax
        import jax.numpy as jnp
        _gk = jax.random.key(seed)
        x = -6.415e-05 + 1 * jax.random.normal(jax.random.fold_in(_gk, 1), (625, 512), jnp.float32)
        src = jax.random.randint(jax.random.fold_in(_gk, 2), (20000,), 0, 625, jnp.int32)
        dst = jax.random.randint(jax.random.fold_in(_gk, 3), (20000,), 0, 625, jnp.int32)
        _o = jnp.argsort(dst, stable=True)
        src = src[_o]
        dst = dst[_o]
        edge_type_2 = jax.random.randint(jax.random.fold_in(_gk, 12), (20000,), 0, 2, jnp.int32)
        return (x, src, dst, edge_type_2)
    x, src, dst, edge_type_2 = _rec_inputs()

    def _L0_gnn_setup():
        import jax, jax.numpy as jnp
        import numpy as np
        N, E, H = (625, 5000, 512)
        EPS = 1e-07

        def _ln(x, g, b, eps=1e-05):
            mu = jnp.mean(x, axis=-1, keepdims=True)
            var = jnp.mean((x - mu) ** 2, axis=-1, keepdims=True)
            return (x - mu) * jax.lax.rsqrt(var + eps) * g + b

        def _genconv(x, src, dst, t, w1, b1, lg, lb, w2, b2):
            m = jax.nn.relu(x[src]) + EPS
            z = m * t
            zmax = jax.lax.stop_gradient(jax.ops.segment_max(z, dst, num_segments=N))
            zmax = jnp.where(jnp.isfinite(zmax), zmax, 0.0)
            e = jnp.exp(z - zmax[dst])
            denom = jax.ops.segment_sum(e, dst, num_segments=N)
            alpha = e / (denom[dst] + 1e-16)
            agg = jax.ops.segment_sum(alpha * m, dst, num_segments=N)
            h = agg + x
            h = jax.nn.relu(_ln(h @ w1 + b1, lg, lb))
            return h @ w2 + b2

        def _forward(x, edge_index, p):
            src, dst = (edge_index[0], edge_index[1])
            x1 = _genconv(x, src, dst, *p['c0'])
            x2 = x1 + jax.nn.relu(_ln(_genconv(x1, src, dst, *p['c1']), p['lng_1'], p['lnb_1']))
            x3 = x2 + jax.nn.relu(_ln(_genconv(x2, src, dst, *p['c2']), p['lng_2'], p['lnb_2']))
            return jnp.concatenate([x1, x2, x3], axis=1) @ p['cw'] + p['cb']
        key = jax.random.key(seed)
        ks = iter(jax.random.split(key, 16))
        s = 0.05
        d = {'x': jax.random.normal(next(ks), (N, H), jnp.float32), 'edge_index': jax.random.randint(next(ks), (2, E), 0, N, jnp.int32)}
        for i in range(3):
            d[f't{i}'] = jnp.ones((1,), jnp.float32)
            d[f'mw1_{i}'] = jax.random.normal(next(ks), (H, 2 * H), jnp.float32) * s
            d[f'mb1_{i}'] = jnp.zeros((2 * H,), jnp.float32)
            d[f'mlg_{i}'] = jnp.ones((2 * H,), jnp.float32)
            d[f'mlb_{i}'] = jnp.zeros((2 * H,), jnp.float32)
            d[f'mw2_{i}'] = jax.random.normal(next(ks), (2 * H, H), jnp.float32) * s
            d[f'mb2_{i}'] = jnp.zeros((H,), jnp.float32)
        for i in (1, 2):
            d[f'lng_{i}'] = jnp.ones((H,), jnp.float32)
            d[f'lnb_{i}'] = jnp.zeros((H,), jnp.float32)
        d['cw'] = jax.random.normal(next(ks), (3 * H, H), jnp.float32) * s
        d['cb'] = jnp.zeros((H,), jnp.float32)
        return d
    _L0_gnn_all = _L0_gnn_setup()
    _L0_gnn_in = {k: v for k, v in _L0_gnn_all.items() if k in ('t0', 'mw1_0', 'mb1_0', 'mlg_0', 'mlb_0', 'mw2_0', 'mb2_0', 't1', 'mw1_1', 'mb1_1', 'mlg_1', 'mlb_1', 'mw2_1', 'mb2_1', 't2', 'mw1_2', 'mb1_2', 'mlg_2', 'mlb_2', 'mw2_2', 'mb2_2', 'lng_1', 'lnb_1', 'lng_2', 'lnb_2', 'cw', 'cb')}
    del _L0_gnn_all

    def _L0_ffn_setup():
        import jax, jax.numpy as jnp
        import numpy as np
        MAX_THRESHOLD = 0.25
        B, S, D, E = (8, 128, 512, 8)
        key = jax.random.key(seed)
        ks = jax.random.split(key, 5)
        scale = 1.0 / np.sqrt(D)
        return {'inputs': jax.random.normal(ks[0], (B, S, D), dtype=jnp.float32), 'W_gate': jax.random.normal(ks[1], (D, E), dtype=jnp.float32) * scale, 'b_gate': jnp.zeros((E,), dtype=jnp.float32), 'W_thr': jax.random.normal(ks[2], (D, 1), dtype=jnp.float32) * scale, 'b_thr': jnp.zeros((1,), dtype=jnp.float32), 'W_exp': jax.random.normal(ks[3], (E, D, D), dtype=jnp.float32) * scale, 'b_exp': jnp.zeros((E, D), dtype=jnp.float32)}
    _L0_ffn_all = _L0_ffn_setup()
    _L0_ffn_in = {k: v for k, v in _L0_ffn_all.items() if k in ('W_gate', 'b_gate', 'W_thr', 'b_thr', 'W_exp', 'b_exp')}
    del _L0_ffn_all

    def _L1_gnn_setup():
        import jax, jax.numpy as jnp
        import numpy as np
        D = 512
        H = 8
        DH = D // H
        F = 64
        L = 2
        N = 625
        E = 10000
        EPS = 1e-05

        def _xavier(key, shape):
            fan_out, fan_in = (shape[-2], shape[-1])
            lim = float(np.sqrt(6.0 / (fan_in + fan_out)))
            return jax.random.uniform(key, shape, jnp.float32, -lim, lim)

        def _batchnorm(x, g, b):
            mu = jnp.mean(x, axis=0)
            var = jnp.mean(jnp.square(x - mu), axis=0)
            return (x - mu) * jax.lax.rsqrt(var + EPS) * g + b

        def _layernorm(x, g, b):
            mu = jnp.mean(x, axis=-1, keepdims=True)
            var = jnp.mean(jnp.square(x - mu), axis=-1, keepdims=True)
            return (x - mu) * jax.lax.rsqrt(var + EPS) * g + b
        key = jax.random.key(seed)
        ks = jax.random.split(key, 12)
        src = jax.random.normal(ks[0], (N, D), jnp.float32)
        edge_index = jax.random.randint(ks[1], (2, E), 0, N)
        return {'src': src, 'edge_index': edge_index, 'Wq': _xavier(ks[2], (L, D, D)), 'bq': jnp.zeros((L, D), jnp.float32), 'Wk': _xavier(ks[3], (L, D, D)), 'Wv': _xavier(ks[4], (L, D, D)), 'Wo': _xavier(ks[5], (L, D, D)), 'bo': jnp.zeros((L, D), jnp.float32), 'W1': _xavier(ks[6], (L, F, D)), 'b1': jnp.zeros((L, F), jnp.float32), 'W2': _xavier(ks[7], (L, D, F)), 'b2': jnp.zeros((L, D), jnp.float32), 'g1': jnp.ones((L, D), jnp.float32), 'beta1': jnp.zeros((L, D), jnp.float32), 'g2': jnp.ones((L, D), jnp.float32), 'beta2': jnp.zeros((L, D), jnp.float32), 'ln_g': jnp.ones((D,), jnp.float32), 'ln_b': jnp.zeros((D,), jnp.float32)}
    _L1_gnn_all = _L1_gnn_setup()
    _L1_gnn_in = {k: v for k, v in _L1_gnn_all.items() if k in ('Wq', 'bq', 'Wk', 'Wv', 'Wo', 'bo', 'W1', 'b1', 'W2', 'b2', 'g1', 'beta1', 'g2', 'beta2', 'ln_g', 'ln_b')}
    del _L1_gnn_all

    def _L1_ffn_setup():
        import jax, jax.numpy as jnp
        import numpy as np
        SINKHORN_ITERS = 8
        TEMPERATURE = 1.0
        EPS = 1e-10

        def sinkhorn(gates):
            t = jnp.log(jnp.clip(gates, EPS)) / TEMPERATURE

            def body(t, _):
                t = t - jax.nn.logsumexp(t, axis=-2, keepdims=True)
                t = t - jax.nn.logsumexp(t, axis=-1, keepdims=True)
                return (t, None)
            t, _ = jax.lax.scan(body, t, None, length=SINKHORN_ITERS)
            return jnp.exp(t)
        key = jax.random.key(seed)
        k1, k2, k3 = jax.random.split(key, 3)
        b, n, d, e, h = (4, 256, 512, 8, 1)
        x = jax.random.normal(k1, (b, n, d), dtype=jnp.float32)
        gate_w = jax.random.normal(k2, (h, d, e), dtype=jnp.float32)
        experts = jax.random.normal(k3, (e, d, d), dtype=jnp.float32) / np.sqrt(d)
        return {'x': x, 'gate_w': gate_w, 'experts': experts}
    _L1_ffn_all = _L1_ffn_setup()
    _L1_ffn_in = {k: v for k, v in _L1_ffn_all.items() if k in ('gate_w', 'experts')}
    del _L1_ffn_all

    def _L2_gnn_setup():
        import jax, jax.numpy as jnp
        import numpy as np
        NUM_RELATIONS = 2
        NUM_BASES = 30
        HIDDEN = 512
        N_NODES = 10000
        N_EDGES = 5000

        def rgcn_gate_layer(x, row, col, edge_type, basis, att, gate_w, root, bias):
            H = x.shape[1]
            w = jnp.einsum('rb,bio->rio', att, basis)
            x_j = x[col]
            msgs = []
            for r in range(NUM_RELATIONS):
                gate = jax.nn.sigmoid(x_j @ gate_w[r, :, 0])
                msgs.append(gate[:, None] * x_j @ w[r])
            msg = jnp.where((edge_type == 0)[:, None], msgs[0], msgs[1])
            agg = jax.ops.segment_sum(msg, row, num_segments=x.shape[0])
            return agg + x @ root + bias
        key = jax.random.key(seed)
        ks = jax.random.split(key, 16)
        H, R, B = (HIDDEN, NUM_RELATIONS, NUM_BASES)
        bound = 1.0 / np.sqrt(B * H)
        u = lambda k, shape: jax.random.uniform(k, shape, jnp.float32, -bound, bound)
        inp = {'x': jax.random.normal(ks[0], (N_NODES, H), jnp.float32), 'edge_index': jax.random.randint(ks[1], (2, N_EDGES), 0, N_NODES, jnp.int32), 'edge_type': jax.random.randint(ks[2], (N_EDGES,), 0, R, jnp.int32), 'basis1': u(ks[3], (B, H, H)), 'att1': u(ks[4], (R, B)), 'gate_w1': u(ks[5], (R, H, 1)), 'root1': u(ks[6], (H, H)), 'bias1': u(ks[7], (H,)), 'basis2': u(ks[8], (B, H, H)), 'att2': u(ks[9], (R, B)), 'gate_w2': u(ks[10], (R, H, 1)), 'root2': u(ks[11], (H, H)), 'bias2': u(ks[12], (H,))}
        return inp
    _L2_gnn_all = _L2_gnn_setup()
    _L2_gnn_in = {k: v for k, v in _L2_gnn_all.items() if k in ('basis1', 'att1', 'gate_w1', 'root1', 'bias1', 'basis2', 'att2', 'gate_w2', 'root2', 'bias2')}
    del _L2_gnn_all

    def _L2_ffn_setup():
        import jax, jax.numpy as jnp
        import numpy as np
        K = 2
        EPS = 1e-06

        def _layernorm(x, gamma, beta):
            mu = jnp.mean(x, axis=-1, keepdims=True)
            var = jnp.mean(jnp.square(x - mu), axis=-1, keepdims=True)
            return (x - mu) * jax.lax.rsqrt(var + EPS) * gamma + beta
        key = jax.random.key(seed)
        ks = jax.random.split(key, 5)
        B, S, D, F, E = (8, 64, 512, 64, 8)
        x = jax.random.normal(ks[0], (B, S, D), dtype=jnp.float32)
        router_w = jax.random.normal(ks[1], (D, E), dtype=jnp.float32) * 0.02
        w1 = jax.random.normal(ks[2], (E, D, F), dtype=jnp.float32) * 0.02
        b1 = jnp.zeros((E, F), dtype=jnp.float32)
        w2 = jax.random.normal(ks[3], (E, F, D), dtype=jnp.float32) * 0.02
        b2 = jnp.zeros((E, D), dtype=jnp.float32)
        gamma = jnp.ones((E, D), dtype=jnp.float32)
        beta = jnp.zeros((E, D), dtype=jnp.float32)
        return {'x': x, 'router_w': router_w, 'w1': w1, 'b1': b1, 'w2': w2, 'b2': b2, 'gamma': gamma, 'beta': beta}
    _L2_ffn_all = _L2_ffn_setup()
    _L2_ffn_in = {k: v for k, v in _L2_ffn_all.items() if k in ('router_w', 'w1', 'b1', 'w2', 'b2', 'gamma', 'beta')}
    del _L2_ffn_all

    def _L3_gnn_setup():
        import jax, jax.numpy as jnp
        import numpy as np
        N_NODES = 10000
        N_EDGES = 5000
        D = 512
        key = jax.random.key(seed)
        k_h, k_e, k_w1, k_w2 = jax.random.split(key, 4)
        h = jax.random.normal(k_h, (N_NODES, D), dtype=jnp.float32)
        edge_index = jax.random.randint(k_e, (2, N_EDGES), 0, N_NODES, dtype=jnp.int64)
        scale = 1.0 / np.sqrt(D)
        W1 = jax.random.normal(k_w1, (D, D), dtype=jnp.float32) * scale
        b1 = jnp.zeros((D,), dtype=jnp.float32)
        W2 = jax.random.normal(k_w2, (D, D), dtype=jnp.float32) * scale
        b2 = jnp.zeros((D,), dtype=jnp.float32)
        return {'h': h, 'edge_index': edge_index, 'W1': W1, 'b1': b1, 'W2': W2, 'b2': b2}
    _L3_gnn_all = _L3_gnn_setup()
    _L3_gnn_in = {k: v for k, v in _L3_gnn_all.items() if k in ('W1', 'b1', 'W2', 'b2')}
    del _L3_gnn_all

    def _L3_ffn_setup():
        import jax, jax.numpy as jnp
        import numpy as np
        B, T, H = (8, 256, 512)
        E, R = (4, 16)
        SCALE = 0.04
        key = jax.random.key(seed)
        ks = jax.random.split(key, 7)
        return {'x': jax.random.normal(ks[0], (B, T, H), jnp.float32), 'gate_w': jax.random.normal(ks[1], (E, H), jnp.float32) * SCALE, 'thr_w': jax.random.normal(ks[2], (1, H), jnp.float32) * SCALE, 'fc1_w': jax.random.normal(ks[3], (E, H, H), jnp.float32) * SCALE, 'lora_A': jax.random.normal(ks[4], (E, H, R), jnp.float32) * SCALE, 'lora_B': jax.random.normal(ks[5], (E, R, H), jnp.float32) * SCALE, 'fc2_w': jax.random.normal(ks[6], (E, H, H), jnp.float32) * SCALE}
    _L3_ffn_all = _L3_ffn_setup()
    _L3_ffn_in = {k: v for k, v in _L3_ffn_all.items() if k in ('gate_w', 'thr_w', 'fc1_w', 'lora_A', 'lora_B', 'fc2_w')}
    del _L3_ffn_all
    return {'x': x, 'src': src, 'dst': dst, 'edge_type_2': edge_type_2, 'L0_gnn_t0': _L0_gnn_in['t0'], 'L0_gnn_mw1_0': _L0_gnn_in['mw1_0'], 'L0_gnn_mb1_0': _L0_gnn_in['mb1_0'], 'L0_gnn_mlg_0': _L0_gnn_in['mlg_0'], 'L0_gnn_mlb_0': _L0_gnn_in['mlb_0'], 'L0_gnn_mw2_0': _L0_gnn_in['mw2_0'], 'L0_gnn_mb2_0': _L0_gnn_in['mb2_0'], 'L0_gnn_t1': _L0_gnn_in['t1'], 'L0_gnn_mw1_1': _L0_gnn_in['mw1_1'], 'L0_gnn_mb1_1': _L0_gnn_in['mb1_1'], 'L0_gnn_mlg_1': _L0_gnn_in['mlg_1'], 'L0_gnn_mlb_1': _L0_gnn_in['mlb_1'], 'L0_gnn_mw2_1': _L0_gnn_in['mw2_1'], 'L0_gnn_mb2_1': _L0_gnn_in['mb2_1'], 'L0_gnn_t2': _L0_gnn_in['t2'], 'L0_gnn_mw1_2': _L0_gnn_in['mw1_2'], 'L0_gnn_mb1_2': _L0_gnn_in['mb1_2'], 'L0_gnn_mlg_2': _L0_gnn_in['mlg_2'], 'L0_gnn_mlb_2': _L0_gnn_in['mlb_2'], 'L0_gnn_mw2_2': _L0_gnn_in['mw2_2'], 'L0_gnn_mb2_2': _L0_gnn_in['mb2_2'], 'L0_gnn_lng_1': _L0_gnn_in['lng_1'], 'L0_gnn_lnb_1': _L0_gnn_in['lnb_1'], 'L0_gnn_lng_2': _L0_gnn_in['lng_2'], 'L0_gnn_lnb_2': _L0_gnn_in['lnb_2'], 'L0_gnn_cw': _L0_gnn_in['cw'], 'L0_gnn_cb': _L0_gnn_in['cb'], 'L0_ffn_W_gate': _L0_ffn_in['W_gate'], 'L0_ffn_b_gate': _L0_ffn_in['b_gate'], 'L0_ffn_W_thr': _L0_ffn_in['W_thr'], 'L0_ffn_b_thr': _L0_ffn_in['b_thr'], 'L0_ffn_W_exp': _L0_ffn_in['W_exp'], 'L0_ffn_b_exp': _L0_ffn_in['b_exp'], 'L1_gnn_Wq': _L1_gnn_in['Wq'], 'L1_gnn_bq': _L1_gnn_in['bq'], 'L1_gnn_Wk': _L1_gnn_in['Wk'], 'L1_gnn_Wv': _L1_gnn_in['Wv'], 'L1_gnn_Wo': _L1_gnn_in['Wo'], 'L1_gnn_bo': _L1_gnn_in['bo'], 'L1_gnn_W1': _L1_gnn_in['W1'], 'L1_gnn_b1': _L1_gnn_in['b1'], 'L1_gnn_W2': _L1_gnn_in['W2'], 'L1_gnn_b2': _L1_gnn_in['b2'], 'L1_gnn_g1': _L1_gnn_in['g1'], 'L1_gnn_beta1': _L1_gnn_in['beta1'], 'L1_gnn_g2': _L1_gnn_in['g2'], 'L1_gnn_beta2': _L1_gnn_in['beta2'], 'L1_gnn_ln_g': _L1_gnn_in['ln_g'], 'L1_gnn_ln_b': _L1_gnn_in['ln_b'], 'L1_ffn_gate_w': _L1_ffn_in['gate_w'], 'L1_ffn_experts': _L1_ffn_in['experts'], 'L2_gnn_basis1': _L2_gnn_in['basis1'], 'L2_gnn_att1': _L2_gnn_in['att1'], 'L2_gnn_gate_w1': _L2_gnn_in['gate_w1'], 'L2_gnn_root1': _L2_gnn_in['root1'], 'L2_gnn_bias1': _L2_gnn_in['bias1'], 'L2_gnn_basis2': _L2_gnn_in['basis2'], 'L2_gnn_att2': _L2_gnn_in['att2'], 'L2_gnn_gate_w2': _L2_gnn_in['gate_w2'], 'L2_gnn_root2': _L2_gnn_in['root2'], 'L2_gnn_bias2': _L2_gnn_in['bias2'], 'L2_ffn_router_w': _L2_ffn_in['router_w'], 'L2_ffn_w1': _L2_ffn_in['w1'], 'L2_ffn_b1': _L2_ffn_in['b1'], 'L2_ffn_w2': _L2_ffn_in['w2'], 'L2_ffn_b2': _L2_ffn_in['b2'], 'L2_ffn_gamma': _L2_ffn_in['gamma'], 'L2_ffn_beta': _L2_ffn_in['beta'], 'L3_gnn_W1': _L3_gnn_in['W1'], 'L3_gnn_b1': _L3_gnn_in['b1'], 'L3_gnn_W2': _L3_gnn_in['W2'], 'L3_gnn_b2': _L3_gnn_in['b2'], 'L3_ffn_gate_w': _L3_ffn_in['gate_w'], 'L3_ffn_thr_w': _L3_ffn_in['thr_w'], 'L3_ffn_fc1_w': _L3_ffn_in['fc1_w'], 'L3_ffn_lora_A': _L3_ffn_in['lora_A'], 'L3_ffn_lora_B': _L3_ffn_in['lora_B'], 'L3_ffn_fc2_w': _L3_ffn_in['fc2_w']}

def reference(x, src, dst, edge_type_2, L0_gnn_t0, L0_gnn_mw1_0, L0_gnn_mb1_0, L0_gnn_mlg_0, L0_gnn_mlb_0, L0_gnn_mw2_0, L0_gnn_mb2_0, L0_gnn_t1, L0_gnn_mw1_1, L0_gnn_mb1_1, L0_gnn_mlg_1, L0_gnn_mlb_1, L0_gnn_mw2_1, L0_gnn_mb2_1, L0_gnn_t2, L0_gnn_mw1_2, L0_gnn_mb1_2, L0_gnn_mlg_2, L0_gnn_mlb_2, L0_gnn_mw2_2, L0_gnn_mb2_2, L0_gnn_lng_1, L0_gnn_lnb_1, L0_gnn_lng_2, L0_gnn_lnb_2, L0_gnn_cw, L0_gnn_cb, L0_ffn_W_gate, L0_ffn_b_gate, L0_ffn_W_thr, L0_ffn_b_thr, L0_ffn_W_exp, L0_ffn_b_exp, L1_gnn_Wq, L1_gnn_bq, L1_gnn_Wk, L1_gnn_Wv, L1_gnn_Wo, L1_gnn_bo, L1_gnn_W1, L1_gnn_b1, L1_gnn_W2, L1_gnn_b2, L1_gnn_g1, L1_gnn_beta1, L1_gnn_g2, L1_gnn_beta2, L1_gnn_ln_g, L1_gnn_ln_b, L1_ffn_gate_w, L1_ffn_experts, L2_gnn_basis1, L2_gnn_att1, L2_gnn_gate_w1, L2_gnn_root1, L2_gnn_bias1, L2_gnn_basis2, L2_gnn_att2, L2_gnn_gate_w2, L2_gnn_root2, L2_gnn_bias2, L2_ffn_router_w, L2_ffn_w1, L2_ffn_b1, L2_ffn_w2, L2_ffn_b2, L2_ffn_gamma, L2_ffn_beta, L3_gnn_W1, L3_gnn_b1, L3_gnn_W2, L3_gnn_b2, L3_ffn_gate_w, L3_ffn_thr_w, L3_ffn_fc1_w, L3_ffn_lora_A, L3_ffn_lora_B, L3_ffn_fc2_w):
    import jax
    import jax.numpy as jnp

    def _L0_gnn_ref(x, edge_index, t0, mw1_0, mb1_0, mlg_0, mlb_0, mw2_0, mb2_0, t1, mw1_1, mb1_1, mlg_1, mlb_1, mw2_1, mb2_1, t2, mw1_2, mb1_2, mlg_2, mlb_2, mw2_2, mb2_2, lng_1, lnb_1, lng_2, lnb_2, cw, cb):
        import jax, jax.numpy as jnp
        import numpy as np
        N, E, H = (625, 5000, 512)
        EPS = 1e-07

        def _ln(x, g, b, eps=1e-05):
            mu = jnp.mean(x, axis=-1, keepdims=True)
            var = jnp.mean((x - mu) ** 2, axis=-1, keepdims=True)
            return (x - mu) * jax.lax.rsqrt(var + eps) * g + b

        def _genconv(x, src, dst, t, w1, b1, lg, lb, w2, b2):
            m = jax.nn.relu(x[src]) + EPS
            z = m * t
            zmax = jax.lax.stop_gradient(jax.ops.segment_max(z, dst, num_segments=N))
            zmax = jnp.where(jnp.isfinite(zmax), zmax, 0.0)
            e = jnp.exp(z - zmax[dst])
            denom = jax.ops.segment_sum(e, dst, num_segments=N)
            alpha = e / (denom[dst] + 1e-16)
            agg = jax.ops.segment_sum(alpha * m, dst, num_segments=N)
            h = agg + x
            h = jax.nn.relu(_ln(h @ w1 + b1, lg, lb))
            return h @ w2 + b2

        def _forward(x, edge_index, p):
            src, dst = (edge_index[0], edge_index[1])
            x1 = _genconv(x, src, dst, *p['c0'])
            x2 = x1 + jax.nn.relu(_ln(_genconv(x1, src, dst, *p['c1']), p['lng_1'], p['lnb_1']))
            x3 = x2 + jax.nn.relu(_ln(_genconv(x2, src, dst, *p['c2']), p['lng_2'], p['lnb_2']))
            return jnp.concatenate([x1, x2, x3], axis=1) @ p['cw'] + p['cb']
        p = {'c0': (t0, mw1_0, mb1_0, mlg_0, mlb_0, mw2_0, mb2_0), 'c1': (t1, mw1_1, mb1_1, mlg_1, mlb_1, mw2_1, mb2_1), 'c2': (t2, mw1_2, mb1_2, mlg_2, mlb_2, mw2_2, mb2_2), 'lng_1': lng_1, 'lnb_1': lnb_1, 'lng_2': lng_2, 'lnb_2': lnb_2, 'cw': cw, 'cb': cb}
        return _forward(x, edge_index, p)

    def _L0_ffn_ref(inputs, W_gate, b_gate, W_thr, b_thr, W_exp, b_exp):
        import jax, jax.numpy as jnp
        import numpy as np
        MAX_THRESHOLD = 0.25
        B, S, D, E = (8, 128, 512, 8)
        d = inputs.shape[-1]
        x = inputs.reshape(-1, d)
        gate_logits = jax.nn.softmax(x @ W_gate + b_gate, axis=-1)
        thresholds = jax.nn.sigmoid(x @ W_thr + b_thr) * MAX_THRESHOLD
        adapted = gate_logits - thresholds
        selected = (adapted >= 0).astype(x.dtype)
        weights = adapted * selected
        wsum = jnp.sum(weights, axis=-1, keepdims=True)
        wsum = jnp.where(wsum == 0, jnp.ones_like(wsum), wsum)
        weights = weights / wsum
        ex_out = jnp.einsum('td,edf->etf', x, W_exp) + b_exp[:, None, :]
        results = jnp.einsum('etf,te->tf', ex_out, weights)
        return results.reshape(inputs.shape[:-1] + (results.shape[-1],))

    def _L1_gnn_ref(src, edge_index, Wq, bq, Wk, Wv, Wo, bo, W1, b1, W2, b2, g1, beta1, g2, beta2, ln_g, ln_b):
        import jax, jax.numpy as jnp
        import numpy as np
        D = 512
        H = 8
        DH = D // H
        F = 64
        L = 2
        N = 625
        E = 10000
        EPS = 1e-05

        def _xavier(key, shape):
            fan_out, fan_in = (shape[-2], shape[-1])
            lim = float(np.sqrt(6.0 / (fan_in + fan_out)))
            return jax.random.uniform(key, shape, jnp.float32, -lim, lim)

        def _batchnorm(x, g, b):
            mu = jnp.mean(x, axis=0)
            var = jnp.mean(jnp.square(x - mu), axis=0)
            return (x - mu) * jax.lax.rsqrt(var + EPS) * g + b

        def _layernorm(x, g, b):
            mu = jnp.mean(x, axis=-1, keepdims=True)
            var = jnp.mean(jnp.square(x - mu), axis=-1, keepdims=True)
            return (x - mu) * jax.lax.rsqrt(var + EPS) * g + b
        n = src.shape[0]
        scaling = float(DH) ** (-0.5)
        tgt = edge_index[1]
        srcidx = edge_index[0]
        x = src
        for l in range(L):
            q = ((x @ Wq[l].T + bq[l]) * scaling).reshape(n, H, DH)
            k = (x @ Wk[l].T).reshape(n, H, DH)
            v = (x @ Wv[l].T).reshape(n, H, DH)
            scores = jnp.einsum('ehd,ehd->eh', q[tgt], k[srcidx])
            m = jax.ops.segment_max(scores, tgt, num_segments=n)
            p = jnp.exp(scores - m[tgt])
            s = jax.ops.segment_sum(p, tgt, num_segments=n)
            w = p / (s[tgt] + 1e-16)
            agg = jax.ops.segment_sum(w[:, :, None] * v[srcidx], tgt, num_segments=n)
            attn = agg.reshape(n, D) @ Wo[l].T + bo[l]
            x = _batchnorm(x + attn, g1[l], beta1[l])
            ff = jax.nn.relu(x @ W1[l].T + b1[l]) @ W2[l].T + b2[l]
            x = _batchnorm(x + ff, g2[l], beta2[l])
        return _layernorm(x, ln_g, ln_b)

    def _L1_ffn_ref(x, gate_w, experts):
        import jax, jax.numpy as jnp
        import numpy as np
        SINKHORN_ITERS = 8
        TEMPERATURE = 1.0
        EPS = 1e-10

        def sinkhorn(gates):
            t = jnp.log(jnp.clip(gates, EPS)) / TEMPERATURE

            def body(t, _):
                t = t - jax.nn.logsumexp(t, axis=-2, keepdims=True)
                t = t - jax.nn.logsumexp(t, axis=-1, keepdims=True)
                return (t, None)
            t, _ = jax.lax.scan(body, t, None, length=SINKHORN_ITERS)
            return jnp.exp(t)
        b, n, d = x.shape
        h = gate_w.shape[0]
        e = experts.shape[0]
        N = b * n
        m = n // e
        x4 = x[:, None]
        gates = jnp.einsum('bhnd,hde->bhne', x4, gate_w)
        xf = jnp.transpose(x4, (1, 0, 2, 3)).reshape(h, N, d)
        gf = jnp.transpose(gates, (1, 0, 2, 3)).reshape(h, N, e)
        cg = sinkhorn(gf)
        vals, idx = jax.lax.top_k(jnp.transpose(cg, (0, 2, 1)), m)
        gate_values = (vals > 0.5).astype(x.dtype)
        gate_values = jnp.transpose(gate_values, (0, 2, 1))
        idx = jnp.transpose(idx, (0, 2, 1))
        routed = xf[jnp.arange(h)[:, None, None], idx]
        outputs = jnp.einsum('hmei,eio->hmeo', routed, experts)
        outputs = outputs * gate_values[..., None]
        o_dim = outputs.shape[-1]
        src = outputs.reshape(h, m * e, o_dim)
        idx_flat = idx.reshape(h, m * e)

        def combine(idxf, srcf):
            s = jnp.zeros((N, o_dim), srcf.dtype).at[idxf].add(srcf)
            c = jnp.zeros((N,), srcf.dtype).at[idxf].add(1.0)
            return s / (c + 1.0)[:, None]
        out = jax.vmap(combine)(idx_flat, src)
        out = out.reshape(h, b, n, o_dim)
        out = jnp.transpose(out, (1, 0, 2, 3))[:, 0]
        return out

    def _L2_gnn_ref(x, edge_index, edge_type, basis1, att1, gate_w1, root1, bias1, basis2, att2, gate_w2, root2, bias2):
        import jax, jax.numpy as jnp
        import numpy as np
        NUM_RELATIONS = 2
        NUM_BASES = 30
        HIDDEN = 512
        N_NODES = 10000
        N_EDGES = 5000

        def rgcn_gate_layer(x, row, col, edge_type, basis, att, gate_w, root, bias):
            H = x.shape[1]
            w = jnp.einsum('rb,bio->rio', att, basis)
            x_j = x[col]
            msgs = []
            for r in range(NUM_RELATIONS):
                gate = jax.nn.sigmoid(x_j @ gate_w[r, :, 0])
                msgs.append(gate[:, None] * x_j @ w[r])
            msg = jnp.where((edge_type == 0)[:, None], msgs[0], msgs[1])
            agg = jax.ops.segment_sum(msg, row, num_segments=x.shape[0])
            return agg + x @ root + bias
        row, col = (edge_index[0], edge_index[1])
        h = jax.nn.relu(rgcn_gate_layer(x, row, col, edge_type, basis1, att1, gate_w1, root1, bias1))
        out = rgcn_gate_layer(h, row, col, edge_type, basis2, att2, gate_w2, root2, bias2)
        return out

    def _L2_ffn_ref(x, router_w, w1, b1, w2, b2, gamma, beta):
        import jax, jax.numpy as jnp
        import numpy as np
        K = 2
        EPS = 1e-06

        def _layernorm(x, gamma, beta):
            mu = jnp.mean(x, axis=-1, keepdims=True)
            var = jnp.mean(jnp.square(x - mu), axis=-1, keepdims=True)
            return (x - mu) * jax.lax.rsqrt(var + EPS) * gamma + beta
        B, S, D = x.shape
        E = w1.shape[0]
        xf = x.reshape(-1, D)
        logits = xf @ router_w
        gate_vals, idx = jax.lax.top_k(logits, K)
        gates = jax.nn.softmax(gate_vals, axis=-1)
        out = jnp.zeros_like(xf)
        for e in range(E):
            h = jax.nn.relu(xf @ w1[e] + b1[e]) @ w2[e] + b2[e]
            y = _layernorm(xf + h, gamma[e], beta[e])
            w = jnp.sum(jnp.where(idx == e, gates, 0.0), axis=-1)
            out = out + w[:, None] * y
        return out.reshape(B, S, D)

    def _L3_gnn_ref(h, edge_index, W1, b1, W2, b2):
        import jax, jax.numpy as jnp
        import numpy as np
        N_NODES = 10000
        N_EDGES = 5000
        D = 512
        send, rec = (edge_index[0], edge_index[1])
        agg = jax.ops.segment_sum(h[send], rec, num_segments=h.shape[0])
        x = h + agg
        x = jax.nn.relu(x @ W1 + b1)
        x = x @ W2 + b2
        return x

    def _L3_ffn_ref(x, gate_w, thr_w, fc1_w, lora_A, lora_B, fc2_w):
        import jax, jax.numpy as jnp
        import numpy as np
        B, T, H = (8, 256, 512)
        E, R = (4, 16)
        SCALE = 0.04
        b, t, h = x.shape
        e = gate_w.shape[0]
        xf = x.reshape(-1, h)
        gate_logits = jax.nn.softmax(xf @ gate_w.T, axis=-1)
        thresholds = jax.nn.sigmoid(xf @ thr_w.T) * (1.0 / e)
        adapted = gate_logits - thresholds
        selected = (adapted >= 0).astype(xf.dtype)
        weights = adapted * selected
        wsum = jnp.sum(weights, axis=-1, keepdims=True)
        wsum = jnp.where(wsum == 0, jnp.ones_like(wsum), wsum)
        weights = weights / wsum
        hidden = jax.nn.relu(jnp.einsum('ni,ehi->neh', xf, fc1_w))
        lo = jnp.einsum('neh,ehr->ner', hidden, lora_A)
        lo = jnp.einsum('ner,ero->neo', lo, lora_B)
        expert_out = jnp.einsum('neo,edo->ned', lo, fc2_w)
        out = jnp.einsum('ne,ned->nd', weights, expert_out)
        return out.reshape(b, t, h)
    edge_index = jnp.stack([src, dst])
    x = x + _L0_gnn_ref(_layernorm(x, axis=-1), edge_index, L0_gnn_t0, L0_gnn_mw1_0, L0_gnn_mb1_0, L0_gnn_mlg_0, L0_gnn_mlb_0, L0_gnn_mw2_0, L0_gnn_mb2_0, L0_gnn_t1, L0_gnn_mw1_1, L0_gnn_mb1_1, L0_gnn_mlg_1, L0_gnn_mlb_1, L0_gnn_mw2_1, L0_gnn_mb2_1, L0_gnn_t2, L0_gnn_mw1_2, L0_gnn_mb1_2, L0_gnn_mlg_2, L0_gnn_mlb_2, L0_gnn_mw2_2, L0_gnn_mb2_2, L0_gnn_lng_1, L0_gnn_lnb_1, L0_gnn_lng_2, L0_gnn_lnb_2, L0_gnn_cw, L0_gnn_cb)
    x = x + _L0_ffn_ref(_layernorm(x, axis=-1)[None], L0_ffn_W_gate, L0_ffn_b_gate, L0_ffn_W_thr, L0_ffn_b_thr, L0_ffn_W_exp, L0_ffn_b_exp)[0]
    x = x + _L1_gnn_ref(_layernorm(x, axis=-1), edge_index, L1_gnn_Wq, L1_gnn_bq, L1_gnn_Wk, L1_gnn_Wv, L1_gnn_Wo, L1_gnn_bo, L1_gnn_W1, L1_gnn_b1, L1_gnn_W2, L1_gnn_b2, L1_gnn_g1, L1_gnn_beta1, L1_gnn_g2, L1_gnn_beta2, L1_gnn_ln_g, L1_gnn_ln_b)
    x = x + _L1_ffn_ref(_layernorm(x, axis=-1)[None], L1_ffn_gate_w, L1_ffn_experts)[0]
    x = x + _L2_gnn_ref(_layernorm(x, axis=-1), edge_index, edge_type_2, L2_gnn_basis1, L2_gnn_att1, L2_gnn_gate_w1, L2_gnn_root1, L2_gnn_bias1, L2_gnn_basis2, L2_gnn_att2, L2_gnn_gate_w2, L2_gnn_root2, L2_gnn_bias2)
    x = x + _L2_ffn_ref(_layernorm(x, axis=-1)[None], L2_ffn_router_w, L2_ffn_w1, L2_ffn_b1, L2_ffn_w2, L2_ffn_b2, L2_ffn_gamma, L2_ffn_beta)[0]
    x = x + _L3_gnn_ref(_layernorm(x, axis=-1), edge_index, L3_gnn_W1, L3_gnn_b1, L3_gnn_W2, L3_gnn_b2)
    x = x + _L3_ffn_ref(_layernorm(x, axis=-1)[None], L3_ffn_gate_w, L3_ffn_thr_w, L3_ffn_fc1_w, L3_ffn_lora_A, L3_ffn_lora_B, L3_ffn_fc2_w)[0]
    return x

_drawn_inputs = setup_inputs


def setup_inputs(seed=0):
    import zlib

    import numpy as np

    out = dict(_drawn_inputs(seed))
    spreads = {'L0_gnn_mb1_0': (0.0, 0.1),
     'L0_gnn_mlg_0': (1.0, 0.2),
     'L0_gnn_mlb_0': (0.0, 0.1),
     'L0_gnn_mb2_0': (0.0, 0.1),
     'L0_gnn_mb1_1': (0.0, 0.34),
     'L0_gnn_mlg_1': (1.0, 0.2),
     'L0_gnn_mlb_1': (0.0, 0.1),
     'L0_gnn_mb2_1': (0.0, 0.1),
     'L0_gnn_mb1_2': (0.0, 0.701),
     'L0_gnn_mlg_2': (1.0, 0.2),
     'L0_gnn_mlb_2': (0.0, 0.276),
     'L0_gnn_mb2_2': (0.0, 0.301),
     'L0_gnn_lng_1': (1.0, 0.2),
     'L0_gnn_lnb_1': (0.0, 0.1),
     'L0_gnn_lng_2': (1.0, 0.2),
     'L0_gnn_lnb_2': (0.0, 0.1),
     'L0_gnn_cb': (0.0, 0.1),
     'L0_ffn_b_gate': (0.0, 0.8),
     'L0_ffn_b_exp': (0.0, 0.457),
     'L1_gnn_bq': (0.0, 0.8),
     'L1_gnn_bo': (0.0, 0.8),
     'L1_gnn_b1': (0.0, 0.8),
     'L1_gnn_b2': (0.0, 0.8),
     'L1_gnn_g1': (1.0, 0.6),
     'L1_gnn_beta1': (0.0, 0.8),
     'L1_gnn_g2': (1.0, 0.55),
     'L1_gnn_beta2': (0.0, 0.1),
     'L1_gnn_ln_g': (1.0, 0.567),
     'L1_gnn_ln_b': (0.0, 0.1),
     'L2_ffn_b1': (0.0, 0.8),
     'L2_ffn_b2': (0.0, 0.603),
     'L2_ffn_gamma': (1.0, 0.6),
     'L2_ffn_beta': (0.0, 0.593),
     'L3_gnn_b1': (0.0, 0.8),
     'L3_gnn_b2': (0.0, 0.8)}
    factors = {'L2_gnn_basis1': 8.0,
     'L2_gnn_att1': 8.0,
     'L2_gnn_gate_w1': 8.0,
     'L2_gnn_root1': 8.0,
     'L2_gnn_bias1': 8.0,
     'L2_gnn_basis2': 8.0,
     'L2_gnn_att2': 8.0,
     'L2_gnn_gate_w2': 8.0,
     'L2_gnn_root2': 8.0,
     'L2_gnn_bias2': 8.0,
     'L2_ffn_router_w': 2.835,
     'L2_ffn_w1': 8.0,
     'L2_ffn_w2': 8.0,
     'L3_ffn_gate_w': 8.0,
     'L3_ffn_thr_w': 8.0,
     'L3_ffn_fc1_w': 8.0,
     'L3_ffn_lora_A': 7.833,
     'L3_ffn_lora_B': 7.251,
     'L3_ffn_fc2_w': 6.915}
    for name, (base, spread) in spreads.items():
        noise = np.random.default_rng([zlib.crc32(name.encode()), seed]).standard_normal(out[name].shape)
        drawn = base * np.exp(spread * noise) if base else spread * noise
        out[name] = jnp.asarray(drawn.astype(out[name].dtype))
    for name, factor in factors.items():
        out[name] = (out[name] * factor).astype(out[name].dtype)
    return out
```

```python
from contextlib import ExitStack

import concourse.bass as bass
from concourse import mybir
from concourse.alu_op_type import AluOpType as ALU

ACT = mybir.ActivationFunctionType
AX = mybir.AxisListType
F32 = mybir.dt.float32
BF16 = mybir.dt.bfloat16
FP16 = mybir.dt.float16
I32 = mybir.dt.int32

NODES = 625
P = 125
TILES = NODES // P
PADDED = 626
HALF = PADDED // 2
EDGES = 20000
CHUNKS = EDGES // P
D = 512
K = D // 128
D2 = 2 * D
BASES = 30
ROWS4 = 4
MIX = BASES * ROWS4
GROUP = 16
STEPS = D // (ROWS4 * GROUP)
BANK = 512
BIG = 1e30


class Semaphores:

    def __init__(self, nc, part):
        self.nc, self.part, self.known = nc, part, {}

    def __getitem__(self, name):
        if name not in self.known:
            self.known[name] = self.nc.alloc_semaphore(f"{self.part}_{name}")
        return self.known[name]


def accumulate(pe, out, pairs):
    for n, (lhsT, rhs) in enumerate(pairs):
        last = pe.matmul(out, lhsT, rhs, start=(n == 0), stop=(n == len(pairs) - 1))
    return last


def tile_of(columns, k, m):
    return columns[:, k, m * P:(m + 1) * P]


def halves(row):
    return row.rearrange("p (h n) -> p h n", h=2)


def spread(ap, n):
    return ap.unsqueeze(2).to_broadcast([ap.shape[0], ap.shape[1], n])



def count_edges(nc, b, t, load_next):
    S = Semaphores(nc, b.part)
    PS = b.psum
    flat = PS.rearrange("p b n -> p (b n)")
    SLOTS = 4
    PASS = CHUNKS // STEPS
    LAYERS = 2

    def sb(name, shape, dt=F32):
        return nc.alloc_sbuf_tensor(name, shape, dt)

    ids_i = sb("ids_i", [P, 3, CHUNKS], I32)
    ids = sb("ids", [P, 3, CHUNKS])
    iota = sb("iota", [P, NODES], FP16)
    hot_dst = sb("hot_dst", [P, SLOTS, NODES], BF16)
    hot_src = sb("hot_src", [P, SLOTS, NODES], BF16)
    zeros = sb("zeros", [1, BANK], BF16)
    att = sb("att", [MIX, LAYERS, 2])
    quarter = sb("quarter", [MIX, ROWS4])
    ones = sb("ones16", [MIX, GROUP])
    mixer = sb("mixer", [MIX, LAYERS, GROUP * 128])
    mixed = sb("mixed", [128, STEPS, D])
    counts = sb("counts", [P, TILES, PADDED])
    counts_1 = b.V[1][0:P, 0:TILES * PADDED].rearrange("p (m n) -> p m n", m=TILES)
    counts_of = (counts, counts_1)

    pieces = []
    for m in range(TILES):
        at = m * NODES
        while at < (m + 1) * NODES:
            end = min((m + 1) * NODES, (at // BANK + 1) * BANK)
            pieces.append((m, at, end))
            at = end
    count_banks = -(-TILES * NODES // BANK)
    mix_bank = PS[:, count_banks, :]

    with nc.Block() as block:
        @block.sync
        def _(sp):
            for n, name in enumerate(("src", "dst", "edge_type_2")):
                sp.dma_start(ids_i[:, n, :], t[name].rearrange("(p c) -> p c", p=P)).then_inc(S["ids_in"], 16)
            sp.dma_start(iota[:, :], t["iota"]).then_inc(S["ids_in"], 16)
            sp.dma_start(quarter[:, :], t["quarter"]).then_inc(S["att_in"], 16)
            sp.dma_start(att[:, :, :], t["atts"]).then_inc(S["att_in"], 16)
            sp.dma_start(b.ident[:, :], t["ident"]).then_inc(S["ident_in"], 16)
            sp.dma_start(b.X[:, :, :], t["x"].rearrange("(m p) f -> p m f", p=P)).then_inc(S["ident_in"], 16)
            for layer in range(LAYERS):
                rows = t[f"L2_gnn_basis{layer + 1}"].rearrange("b (t q j) o -> t b q (j o)", t=STEPS, q=ROWS4)
                with sp.Fori(0, STEPS // 2) as i:
                    for h in range(2):
                        sp.wait_ge(S["mixed_full"], STEPS * layer + 2 * i + h + 1)
                        sp.dma_start(b.W[h][0:MIX, :], rows[bass.ds(2 * i + h, 1)].rearrange("a b q n -> (a b) q n")
                                     ).then_inc(S[f"basis_in{h}"], 16)
            sp.wait_ge(S["mixed_full"], 2 + LAYERS * STEPS)
            load_next(sp)
            sp.wait_ge(S["ident_in"], 32)

        @block.gpsimd
        def _(pool):
            for layer in range(LAYERS):
                pool.wait_ge(S["mixed_out"], 1 + STEPS * (layer + 1))
                pool.dma_start(b.mixed_dram[layer], mixed[:, :, :].rearrange("p a n -> p (a n)")).then_inc(S["stored"], 16)
                if layer == 0:
                    pool.wait_ge(S["stored"], 16)
                    pool.sem_inc(S["mixed_free"], 1)
            for n in range(2):
                pool.wait_ge(S["counted"], n + 1)
                pool.dma_start(b.counts_dram[n], counts_of[n][:, :, :].rearrange("p m n -> p (m n)")).then_inc(S["stored"], 16)
            pool.wait_ge(S["stored"], 64)

        @block.vector
        def _(dve):
            dve.memset(zeros[:, :], 0.0).then_inc(S["zeros"], 1)
            dve.memset(mixer[:, :, :], 0.0).then_inc(S["blank"], 1)
            dve.memset(ones[:, :], 1.0).then_inc(S["blank"], 1)
            dve.memset(counts[:, :, :], 0.0).then_inc(S["blank"], 1)
            dve.memset(counts_1[:, :, :], 0.0).then_inc(S["blank"], 1)
            dve.memset(b.CT[:, :, :], 0.0).then_inc(S["blank"], 1)
            dve.memset(b.XT[:, :, :], 0.0).then_inc(S["blank"], 1)
            dve.memset(b.ones[:, :], 1.0).then_inc(S["blank"], 1)
            dve.wait_ge(S["ids_in"], 64)
            dve.tensor_copy(ids[:, 0:2, :], ids_i[:, 0:2, :]).then_inc(S["ids_cast"], 1)
            dve.tensor_scalar(ids[:, 2, :], ids_i[:, 2, :], 0.0, None, ALU.not_equal).then_inc(S["ids_cast"], 1)
            dve.wait_ge(S["att_in"], 32)
            dve.wait_ge(S["blank"], 7)
            for layer in range(LAYERS):
                for r in range(2):
                    for q in range(ROWS4):
                        first = r * ROWS4 * GROUP + q * GROUP
                        dve.tensor_scalar(mixer[:, layer, first:first + 129 * (GROUP - 1) + 1:129], ones[:, :],
                                          quarter[:, q:q + 1], att[:, layer, r:r + 1], ALU.mult, ALU.mult
                                          ).then_inc(S["mixer_made"], 1)
            dve.wait_ge(S["ids_cast"], 2)
            for n in range(2):
                with dve.Fori(0, CHUNKS // SLOTS) as i:
                    for slot in range(SLOTS):
                        c = SLOTS * i + slot
                        dve.wait_ge(S["hot_free"], CHUNKS * n + c + 1)
                        dve.tensor_scalar(hot_dst[:, slot, :], iota[:, :], ids[:, 1, bass.ds(c, 1)], None,
                                          ALU.is_equal).then_inc(S["hot_ready"], 1)
                        if n == 0:
                            dve.tensor_scalar(hot_src[:, slot, :], iota[:, :], ids[:, 0, bass.ds(c, 1)], None,
                                              ALU.is_equal).then_inc(S["hot_ready"], 1)
                        else:
                            dve.tensor_scalar(hot_src[:, slot, :], iota[:, :], ids[:, 0, bass.ds(c, 1)],
                                              ids[:, 2, bass.ds(c, 1)], ALU.is_equal, ALU.mult
                                              ).then_inc(S["hot_ready"], 1)
                dve.wait_ge(S["pass_done"], n + 1)
                dve.tensor_copy(counts_of[n][:, :, 0:NODES],
                                flat[0:P, 0:TILES * NODES].rearrange("p (m n) -> p m n", m=TILES)
                                ).then_inc(S["counted"], 1)
            for s in range(TILES):
                dve.wait_ge(S["turned"], s + 1)
                dve.tensor_copy(b.CT[:, s, 0:4 * P], PS[0:P, s, 0:4 * P]).then_inc(S["ct_out"], 1)
            dve.wait_ge(S["turned"], 2 * TILES)
            dve.tensor_copy(b.CT[:, 0:4, 4 * P:5 * P], PS[0:P, TILES, 0:4 * P].rearrange("p (s n) -> p s n", s=4)
                            ).then_inc(S["ct_out"], 1)
            dve.tensor_copy(b.CT[:, 4, 4 * P:5 * P], PS[0:P, TILES + 1, 0:P]).then_inc(S["ct_out"], 1)

        @block.scalar
        def _(act):
            for layer in range(LAYERS):
                if layer == 1:
                    act.wait_ge(S["mixed_free"], 1)
                with act.Fori(0, STEPS) as i:
                    act.wait_ge(S["mixed_full"], 2 + STEPS * layer + i + 1)
                    act.activation(mixed[:, bass.ds(i, 1), :], PS[:, count_banks:count_banks + 1, :], ACT.Copy
                                   ).then_inc(S["mixed_out"], 1)

        @block.tensor
        def _(pe):
            pe.sem_inc(S["hot_free"], SLOTS)
            pe.sem_inc(S["mixed_full"], 2)
            pe.sem_inc(S["mixed_out"], 1)
            pe.wait_ge(S["zeros"], 1)
            pe.wait_ge(S["mixer_made"], LAYERS * 2 * ROWS4)
            for n in range(2):
                if n == 1:
                    pe.wait_ge(S["counted"], 1)
                for bank in range(count_banks):
                    pe.matmul(PS[:, bank, :], zeros[0:1, 0:128], zeros[0:1, :], start=True, stop=False,
                              skip_group_check=True)
                with pe.Fori(0, STEPS // 2) as i:
                    for h in range(2):
                        step = 2 * i + h
                        for j in range(PASS):
                            c = PASS * step + j
                            slot = (PASS * h + j) % SLOTS
                            pe.wait_ge(S["hot_ready"], 2 * (CHUNKS * n + c + 1))
                            for m, at, end in pieces:
                                last = pe.matmul(flat[0:P, at:end], hot_dst[:, slot, m * P:(m + 1) * P],
                                                 hot_src[:, slot, at - m * NODES:end - m * NODES],
                                                 start=False, stop=False, skip_group_check=True)
                            last.then_inc(S["hot_free"], 1)
                            if j < GROUP:
                                if j == 0:
                                    pe.wait_ge(S[f"basis_in{h}"], 16 * (STEPS // 2 * n + i + 1))
                                    pe.wait_ge(S["mixed_out"], 1 + STEPS * n + step)
                                last = pe.matmul(mix_bank, mixer[:, n, j * 128:(j + 1) * 128],
                                                 b.W[h][0:MIX, j * D:(j + 1) * D], start=(j == 0),
                                                 stop=(j == GROUP - 1))
                                if j == GROUP - 1:
                                    last.then_inc(S["mixed_full"], 1)
                for bank in range(count_banks):
                    last = pe.matmul(PS[:, bank, :], zeros[0:1, 0:128], zeros[0:1, :], start=False, stop=True,
                                     skip_group_check=True)
                last.then_inc(S["pass_done"], 1)
            pe.wait_ge(S["ident_in"], 32)
            pe.wait_ge(S["counted"], 2)
            for s in range(TILES):
                for d in range(4):
                    last = pe.transpose(PS[0:P, s, d * P:(d + 1) * P], counts[:, d, s * P:(s + 1) * P], b.ident[0:P, 0:P])
                last.then_inc(S["turned"], 1)
            for s in range(TILES):
                pe.transpose(PS[0:P, TILES + s // 4, (s % 4) * P:(s % 4 + 1) * P], counts[:, 4, s * P:(s + 1) * P],
                             b.ident[0:P, 0:P]).then_inc(S["turned"], 1)


def prenorm_vector(dve, b, S):
    row_stats(dve, b, S, "pre", [[b.X[:, m, :]] for m in range(TILES)])
    for m in range(TILES):
        dve.tensor_scalar(b.XN[:, m, :], b.X[:, m, :], b.mv[:, m, 0:1], b.rstd[:, m:m + 1], ALU.subtract, ALU.mult
                          ).then_inc(S["pre_rows"], 1)


def prenorm_tensor(pe, b, S):
    for m in range(TILES):
        pe.wait_ge(S["pre_rows"], m + 1)
        for k in range(K):
            last = pe.transpose(b.psum[:, m, k * P:(k + 1) * P], b.XN[:, m, k * 128:(k + 1) * 128], b.ident[0:P, 0:P])
        last.then_inc(S["pre_turned"], 1)


def prenorm_scalar(act, b, S):
    row_root(act, b, S, "pre")
    for m in range(TILES):
        act.wait_ge(S["pre_turned"], m + 1)
        act.activation(b.XT[:, :, m * P:(m + 1) * P], b.psum[:, m, 0:K * P].rearrange("p (k n) -> p k n", k=K), ACT.Copy
                       ).then_inc(S["pre_columns"], 1)


def row_stats(dve, b, S, tag, views):
    n = len(views[0])
    for m in range(TILES):
        for h in range(n):
            dve.bn_stats(b.stats[:, m, h, :], views[m][h]).then_inc(S[tag + "_stats"], 1)
    dve.wait_ge(S[tag + "_stats"], n * TILES)
    for m in range(TILES):
        dve.bn_aggr(b.mv[:, m, :], b.stats[:, m, 0:n, :].rearrange("p h s -> p (h s)")).then_inc(S[tag + "_aggr"], 1)
    dve.wait_ge(S[tag + "_aggr"], TILES)
    dve.tensor_scalar(b.var[:, :], b.mv[:, :, 1], 1e-5, None, ALU.add).then_inc(S[tag + "_var"], 1)
    dve.wait_ge(S[tag + "_root"], 1)
    dve.reciprocal(b.rstd[:, :], b.root[:, :]).then_inc(S[tag + "_rstd"], 1)
    dve.wait_ge(S[tag + "_rstd"], 1)


def row_root(act, b, S, tag):
    act.wait_ge(S[tag + "_var"], 1)
    act.activation(b.root[:, :], b.var[:, :], ACT.Sqrt).then_inc(S[tag + "_root"], 1)


def column_vectors(b, slot, names):
    out, at = {}, 0
    for name, n in names:
        out[name] = b.U[slot][:, at:at + n]
        at += n
    return out



def load_conv(sp, b, t, slot, done, layer):
    W, V = b.W[slot], b.V[slot]
    sp.dma_start(W[:, 0:K * D2].rearrange("p (k n) -> p k n", k=K),
                 t[f"L0_gnn_mw1_{layer}"].rearrange("(k p) n -> p k n", p=128)).then_inc(done, 16)
    sp.dma_start(W[:, K * D2:].rearrange("p (k n) -> p k n", k=2 * K),
                 t[f"L0_gnn_mw2_{layer}"].rearrange("(k p) n -> p k n", p=128)).then_inc(done, 16)
    sp.dma_start(b.U[slot][:, 0:17], t[f"conv_columns{layer}"]).then_inc(done, 16)
    rows = [(f"L0_gnn_mb1_{layer}", 0), (f"L0_gnn_mb2_{layer}", D2)]
    rows += [("L0_gnn_cb", D2 + D)] if layer == 0 else [(f"L0_gnn_lng_{layer}", D2 + D), (f"L0_gnn_lnb_{layer}", D2 + 2 * D)]
    for name, at in rows:
        sp.dma_start(V[:, at:at + t[name].shape[0]], t[name].partition_broadcast(128)).then_inc(done, 16)
    return 3 + len(rows)


def load_experts(sp, b, t, slot, done, weights, columns, rows, bias=None):
    for e in range(4):
        sp.dma_start(b.W[slot][:, e * K * D:(e + 1) * K * D].rearrange("p (k n) -> p k n", k=K),
                     t[weights][e].rearrange("(k p) n -> p k n", p=128)).then_inc(done, 16)
    sp.dma_start(b.U[slot][:, 0:t[columns].shape[1]], t[columns]).then_inc(done, 16)
    n = 5
    if rows:
        sp.dma_start(b.V[slot][:, 0:t[rows].shape[0]], t[rows].partition_broadcast(128)).then_inc(done, 16)
        n += 1
    if bias:
        sp.dma_start(b.V[slot][0:8, D:2 * D], t[bias]).then_inc(done, 16)
        n += 1
    return n


def load_attention(sp, b, t, slot, done, layer):
    W, V = b.W[slot], b.V[slot]
    for n, name in enumerate(("q", "k", "v", "o")):
        sp.dma_start(W[:, n * K * D:(n + 1) * K * D].rearrange("p (k n) -> p k n", k=K),
                     t[f"att_W{name}"][layer].rearrange("(k p) n -> p k n", p=128)).then_inc(done, 16)
    sp.dma_start(V[:, 0:256].rearrange("p (k n) -> p k n", k=K),
                 t["att_W1"][layer].rearrange("(k p) n -> p k n", p=128)).then_inc(done, 16)
    sp.dma_start(V[0:64, 256:768], t["att_W2"][layer]).then_inc(done, 16)
    sp.dma_start(b.U[slot][:, 0:29], t["att_columns"][layer]).then_inc(done, 16)
    for name, at in (("L1_gnn_ln_g", 1024), ("L1_gnn_ln_b", 1536)):
        sp.dma_start(V[:, at:at + D], t[name].partition_broadcast(128)).then_inc(done, 16)
    return 9


def load_relations(sp, b, t, slot, done, layer):
    W = b.W[slot]
    sp.dma_start(W[:, 0:STEPS * D], b.mixed_dram[layer]).then_inc(done, 16)
    sp.dma_start(W[:, STEPS * D:STEPS * D + K * D].rearrange("p (k n) -> p k n", k=K),
                 t[f"L2_gnn_root{layer + 1}"].rearrange("(k p) n -> p k n", p=128)).then_inc(done, 16)
    sp.dma_start(b.U[slot][:, 0:2 * K], t[f"rel_columns{layer}"]).then_inc(done, 16)
    sp.dma_start(b.V[slot][:, 0:D], t[f"L2_gnn_bias{layer + 1}"].partition_broadcast(128)).then_inc(done, 16)
    return 4


def load_top2(sp, b, t, slot, done):
    W = b.W[slot]
    sp.dma_start(W[:, 0:K * D].rearrange("p (k n) -> p k n", k=K),
                 t["top2_w1"].rearrange("(k p) n -> p k n", p=128)).then_inc(done, 16)
    sp.dma_start(W[:, K * D:2 * K * D].rearrange("p (k n) -> p k n", k=K),
                 t["L2_ffn_w2"].rearrange("(a c) f o -> (c f) a o", c=2)).then_inc(done, 16)
    sp.dma_start(W[:, 2 * K * D:4 * K * D], t["L2_ffn_b2"].rearrange("e n -> (e n)").partition_broadcast(128)
                 ).then_inc(done, 16)
    sp.dma_start(b.V[slot][:, :], t["L2_ffn_gamma"].rearrange("e n -> (e n)").partition_broadcast(128)
                 ).then_inc(done, 16)
    sp.dma_start(b.U[slot][:, 0:9 * K], t["top2_columns"]).then_inc(done, 16)
    return 5


def load_isomorphism(sp, b, t, slot, done):
    for n in range(2):
        sp.dma_start(b.W[slot][:, n * K * D:(n + 1) * K * D].rearrange("p (k n) -> p k n", k=K),
                     t[f"L3_gnn_W{n + 1}"].rearrange("(k p) n -> p k n", p=128)).then_inc(done, 16)
    sp.dma_start(b.U[slot][:, 0:K], t["gin_columns"]).then_inc(done, 16)
    sp.dma_start(b.V[slot][:, 0:D], t["L3_gnn_b2"].partition_broadcast(128)).then_inc(done, 16)
    return 4


def load_lora(sp, b, t, slot, done):
    for e in range(4):
        sp.dma_start(b.W[slot][:, e * K * D:(e + 1) * K * D].rearrange("p (k n) -> p k n", k=K),
                     t["lora_fc1"][e].rearrange("(k p) n -> p k n", p=128)).then_inc(done, 16)
    sp.dma_start(b.U[slot][:, 0:5 * K], t["lora_gate"]).then_inc(done, 16)
    sp.dma_start(b.V[slot][:, 0:256], t["lora_down"]).then_inc(done, 16)
    sp.dma_start(b.V[slot][:, 256:512], t["lora_up"]).then_inc(done, 16)
    return 7



def conv(nc, b, t, layer, slot, loaded, loads, load_next):
    S = Semaphores(nc, b.part)
    PS = b.psum
    W, V = b.W[slot], b.V[slot]
    w1 = W[:, 0:K * D2].rearrange("p (k n) -> p k n", k=K)
    w2 = W[:, K * D2:].rearrange("p (k n) -> p k n", k=2 * K)
    b1, b2 = V[0:P, 0:D2], V[0:P, D2:D2 + D]
    cb = lng = V[0:P, D2 + D:D2 + 2 * D]
    lnb = V[0:P, D2 + 2 * D:D2 + 3 * D]
    cols = column_vectors(b, slot, [("g", 2 * K), ("b", 2 * K), ("t", 1)])
    temperature = cols["t"][0:P, :]

    M = b.sb("messages", [P, TILES, D])
    EE = b.sb("weights_and_weighted", [P, TILES, D2])
    hT = b.sb("h_columns", [128, K, PADDED])
    H2T = b.sb("hidden_columns", [128, 2 * K, NODES])
    den = V[:, 6 * D:6 * D + PADDED]
    cw = b.sb("cw", [128, K, D])
    ext = b.sb("extremes", [P, 8])
    H1 = EE

    with nc.Block() as block:
        @block.sync
        def _(sp):
            sp.dma_start(cw[:, :, :], t["L0_gnn_cw"][layer * D:(layer + 1) * D, :].rearrange("(k p) n -> p k n", p=128)
                         ).then_inc(S["cw_in"], 16)
            load_next(sp)

        @block.vector
        def _(dve):
            if layer == 0:
                prenorm_vector(dve, b, S)
                dve.wait_ge(S["pre_rows"], TILES)
            dve.tensor_scalar(M[:, :, :], b.XN[:, :, :], 0.0, 1e-7, ALU.max, ALU.add).then_inc(S["messages"], 1)
            dve.wait_ge(S["messages"], 1)
            dve.tensor_reduce(ext[:, 0:1], M[:, :, :], AX.XY, ALU.max).then_inc(S["ext"], 1)
            dve.tensor_reduce(ext[:, 1:2], M[:, :, :], AX.XY, ALU.min).then_inc(S["ext"], 1)
            dve.wait_ge(loaded, loads)
            dve.wait_ge(S["ext"], 2)
            dve.tensor_scalar(ext[:, 2:4], ext[:, 0:2], temperature, None, ALU.mult).then_inc(S["ext"], 1)
            dve.wait_ge(S["ext"], 3)
            dve.tensor_tensor(ext[:, 4:5], ext[:, 2:3], ext[:, 3:4], ALU.max).then_inc(S["ext_tile"], 1)
            dve.wait_ge(S["ext_turned"], 1)
            dve.tensor_reduce(ext[0:1, 5:6], PS[0:1, 7, 0:P], AX.X, ALU.max).then_inc(S["ext_all"], 1)
            dve.wait_ge(S["ext_everywhere"], 1)
            dve.tensor_scalar(ext[:, 6:7], PS[0:P, 7, 256:257], -1.0, None, ALU.mult).then_inc(S["shift"], 1)
            for m in range(TILES):
                dve.wait_ge(S["weights"], m + 1)
                dve.tensor_tensor(EE[:, m, D:], EE[:, m, 0:D], M[:, m, :], ALU.mult).then_inc(S["weighted"], 1)
            if layer == 0:
                dve.wait_ge(S["pre_columns"], TILES)
            for c in range(K):
                bank = 4 * (c % 2)
                dve.wait_ge(S["aggregated"], c + 1)
                dve.tensor_scalar(halves(den), PS[:, bank:bank + 2, 0:HALF], 1e-37, None, ALU.max
                                  ).then_inc(S["den"], 1)
                dve.wait_ge(S["den"], 2 * c + 1)
                dve.reciprocal(den, den).then_inc(S["den"], 1)
                dve.wait_ge(S["den"], 2 * c + 2)
                dve.tensor_tensor(halves(hT[:, c, :]), PS[:, bank + 2:bank + 4, 0:HALF], halves(den), ALU.mult
                                  ).then_inc(S["agg"], 1)
                dve.wait_ge(S["agg"], c + 1)
                dve.tensor_tensor(hT[:, c, :], hT[:, c, :], b.XT[:, c, :], ALU.add).then_inc(S["h"], 1)
            for m in range(TILES):
                dve.wait_ge(S["up"], m + 1)
                bank = 2 * (m % 4)
                dve.tensor_tensor(H1[:, m, :].rearrange("p (a n) -> p a n", a=2), PS[0:P, bank:bank + 2, :],
                                  b1.rearrange("p (a n) -> p a n", a=2), ALU.add).then_inc(S["up_out"], 1)
            dve.wait_ge(S["up_out"], TILES)
            row_stats(dve, b, S, "mid", [[H1[:, m, 0:D], H1[:, m, D:]] for m in range(TILES)])
            dve.scalar_tensor_tensor(b.nmr[:, :], b.mv[:, :, 0], -1.0, b.rstd[:, :], ALU.mult, ALU.mult
                                     ).then_inc(S["mid_nmr"], 1)
            if layer == 0:
                for m in range(TILES):
                    dve.wait_ge(S["down"], m + 1)
                    dve.tensor_tensor(b.XN[:, m, :], PS[0:P, m, :], b2, ALU.add).then_inc(S["x_rows"], 1)
            else:
                G = [H1[:, m, 0:D] for m in range(TILES)]
                for m in range(TILES):
                    dve.wait_ge(S["down"], m + 1)
                    dve.tensor_tensor(G[m], PS[0:P, m, :], b2, ALU.add).then_inc(S["down_out"], 1)
                dve.wait_ge(S["down_out"], TILES)
                row_stats(dve, b, S, "out", [[g] for g in G])
                for m in range(TILES):
                    dve.tensor_scalar(G[m], G[m], b.mv[:, m, 0:1], b.rstd[:, m:m + 1], ALU.subtract, ALU.mult
                                      ).then_inc(S["out_norm"], 1)
                for m in range(TILES):
                    dve.wait_ge(S["out_norm"], m + 1)
                    dve.tensor_tensor(G[m], G[m], lng, ALU.mult).then_inc(S["out_gain"], 1)
                for m in range(TILES):
                    dve.wait_ge(S["out_gain"], m + 1)
                    dve.tensor_tensor(G[m], G[m], lnb, ALU.add).then_inc(S["out_shift"], 1)
                for m in range(TILES):
                    dve.wait_ge(S["out_shift"], m + 1)
                    dve.scalar_tensor_tensor(b.XN[:, m, :], G[m], 0.0, b.XN[:, m, :], ALU.max, ALU.add
                                             ).then_inc(S["x_rows"], 1)
            if layer == 0:
                for m in range(TILES):
                    dve.tensor_tensor(b.X[:, m, :], b.X[:, m, :], cb, ALU.add).then_inc(S["cb"], 1)
                dve.wait_ge(S["cb"], TILES)
            for m in range(TILES):
                dve.wait_ge(S["share"], m + 1)
                dve.tensor_tensor(b.X[:, m, :], PS[0:P, 5 + m % 3, :], b.X[:, m, :], ALU.add).then_inc(S["share_out"], 1)

        @block.scalar
        def _(act):
            if layer == 0:
                prenorm_scalar(act, b, S)
            act.wait_ge(S["shift"], 1)
            act.wait_ge(loaded, loads)
            for m in range(TILES):
                act.activation(EE[:, m, 0:D], M[:, m, :], ACT.Exp, bias=ext[:, 6:7], scale=temperature
                               ).then_inc(S["weights"], 1)
            row_root(act, b, S, "mid")
            act.wait_ge(S["mid_nmr"], 1)
            for m in range(TILES):
                act.activation(H1[:, m, :], H1[:, m, :], ACT.Identity, bias=b.nmr[:, m:m + 1], scale=b.rstd[:, m:m + 1]
                               ).then_inc(S["mid_norm"], 1)
            for k in range(2 * K):
                bank = 2 * (k % 4)
                act.wait_ge(S["mid_turned"], k + 1)
                act.activation(H2T[:, k, 0:4 * P], PS[:, bank, 0:4 * P], ACT.Relu, bias=cols["b"][:, k:k + 1],
                               scale=cols["g"][:, k:k + 1]).then_inc(S["hidden"], 1)
                act.activation(H2T[:, k, 4 * P:], PS[:, bank + 1, 0:P], ACT.Relu, bias=cols["b"][:, k:k + 1],
                               scale=cols["g"][:, k:k + 1]).then_inc(S["hidden"], 1)
            if layer > 0:
                row_root(act, b, S, "out")
            for m in range(TILES):
                act.wait_ge(S["x_turned"], m + 1)
                act.activation(b.XT[:, :, m * P:(m + 1) * P], PS[:, m, 0:K * P].rearrange("p (k n) -> p k n", k=K),
                               ACT.Copy).then_inc(S["x_columns"], 1)

        @block.tensor
        def _(pe):
            if layer == 0:
                prenorm_tensor(pe, b, S)
            pe.wait_ge(S["ext_tile"], 1)
            pe.transpose(PS[0:1, 7, 0:P], ext[:, 4:5], b.ident[0:P, 0:P]).then_inc(S["ext_turned"], 1)
            pe.wait_ge(S["ext_all"], 1)
            pe.matmul(PS[0:P, 7, 256:257], b.ones[0:1, 0:P], ext[0:1, 5:6], start=True, stop=True
                      ).then_inc(S["ext_everywhere"], 1)
            if layer == 0:
                pe.wait_ge(S["pre_columns"], TILES)
            pe.wait_ge(S["weighted"], TILES)
            for c in range(K):
                if c >= 2:
                    pe.wait_ge(S["h"], c - 1)
                for part in range(2):
                    at = part * D + c * 128
                    for h in range(2):
                        last = accumulate(pe, PS[:, 4 * (c % 2) + 2 * part + h, 0:HALF],
                                          [(EE[:, s, at:at + 128], b.CT[:, s, h * HALF:(h + 1) * HALF])
                                           for s in range(TILES)])
                last.then_inc(S["aggregated"], 1)
            pe.wait_ge(S["h"], K)
            pe.wait_ge(loaded, loads)
            for m in range(TILES):
                if m >= 4:
                    pe.wait_ge(S["up_out"], m - 3)
                for h in range(2):
                    last = accumulate(pe, PS[0:P, 2 * (m % 4) + h, :],
                                      [(tile_of(hT, k, m), w1[:, k, h * D:(h + 1) * D]) for k in range(K)])
                last.then_inc(S["up"], 1)
            pe.wait_ge(S["mid_norm"], TILES)
            for k in range(2 * K):
                if k >= 4:
                    pe.wait_ge(S["hidden"], 2 * (k - 3))
                for m in range(TILES):
                    last = pe.transpose(PS[:, 2 * (k % 4) + m // 4, (m % 4) * P:(m % 4 + 1) * P],
                                        H1[:, m, k * 128:(k + 1) * 128], b.ident[0:P, 0:P])
                last.then_inc(S["mid_turned"], 1)
            pe.wait_ge(S["hidden"], 4 * K)
            for m in range(TILES):
                accumulate(pe, PS[0:P, m, :], [(tile_of(H2T, k, m), w2[:, k, :]) for k in range(2 * K)]
                           ).then_inc(S["down"], 1)
            for m in range(TILES):
                pe.wait_ge(S["x_rows"], m + 1)
                for k in range(K):
                    last = pe.transpose(PS[:, m, k * P:(k + 1) * P], b.XN[:, m, k * 128:(k + 1) * 128], b.ident[0:P, 0:P])
                last.then_inc(S["x_turned"], 1)
            pe.wait_ge(S["cw_in"], 16)
            for m in range(TILES):
                pe.wait_ge(S["x_columns"], m + 1)
                if m >= 3:
                    pe.wait_ge(S["share_out"], m - 2)
                accumulate(pe, PS[0:P, 5 + m % 3, :], [(tile_of(b.XT, k, m), cw[:, k, :]) for k in range(K)]
                           ).then_inc(S["share"], 1)



def threshold_gates_vector(dve, b, S, G, E, bias, cap):
    lg = G["lg"]
    dve.wait_ge(S["logits"], 1)
    logits = b.psum[0:P, 7, 0:TILES * (E + 1)].rearrange("p (m e) -> p m e", m=TILES)
    if bias is not None:
        dve.tensor_tensor(lg[:, :, :], logits, bias.unsqueeze(1).to_broadcast([P, TILES, E + 1]), ALU.add
                          ).then_inc(S["gate"], 1)
    else:
        dve.tensor_copy(lg[:, :, :], logits).then_inc(S["gate"], 1)
    dve.wait_ge(S["gate"], 1)
    dve.tensor_reduce(G["s"][:, :], lg[:, :, 0:E], AX.X, ALU.max).then_inc(S["gate"], 1)
    dve.wait_ge(S["gate"], 2)
    dve.tensor_tensor(lg[:, :, 0:E], lg[:, :, 0:E], spread(G["s"][:, :], E), ALU.subtract).then_inc(S["gate_shifted"], 1)
    dve.wait_ge(S["gate_exp"], 2)
    dve.tensor_reduce(G["s"][:, :], G["w"][:, :, :], AX.X, ALU.add).then_inc(S["gate"], 1)
    dve.tensor_scalar(G["t"][:, :], G["t"][:, :], 1.0, None, ALU.add).then_inc(S["gate"], 1)
    dve.wait_ge(S["gate"], 4)
    dve.reciprocal(G["s"][:, :], G["s"][:, :]).then_inc(S["gate"], 1)
    dve.reciprocal(G["t"][:, :], G["t"][:, :]).then_inc(S["gate"], 1)
    dve.wait_ge(S["gate"], 6)
    dve.tensor_tensor(G["w"][:, :, :], G["w"][:, :, :], spread(G["s"][:, :], E), ALU.mult).then_inc(S["gate"], 1)
    dve.tensor_scalar(G["t"][:, :], G["t"][:, :], cap, None, ALU.mult).then_inc(S["gate"], 1)
    dve.wait_ge(S["gate"], 8)
    dve.tensor_tensor(G["w"][:, :, :], G["w"][:, :, :], spread(G["t"][:, :], E), ALU.subtract).then_inc(S["gate"], 1)
    dve.wait_ge(S["gate"], 9)
    dve.tensor_scalar(G["w"][:, :, :], G["w"][:, :, :], 0.0, None, ALU.max).then_inc(S["gate"], 1)
    dve.wait_ge(S["gate"], 10)
    dve.tensor_reduce(G["s"][:, :], G["w"][:, :, :], AX.X, ALU.add).then_inc(S["gate"], 1)
    dve.wait_ge(S["gate"], 11)
    dve.scalar_tensor_tensor(G["t"][:, :], G["s"][:, :], 0.0, G["s"][:, :], ALU.is_equal, ALU.add).then_inc(S["gate"], 1)
    dve.wait_ge(S["gate"], 12)
    dve.reciprocal(G["t"][:, :], G["t"][:, :]).then_inc(S["gate"], 1)
    dve.wait_ge(S["gate"], 13)
    dve.tensor_tensor(G["w"][:, :, :], G["w"][:, :, :], spread(G["t"][:, :], E), ALU.mult).then_inc(S["gates"], 1)


def threshold_gates_scalar(act, b, S, G, E):
    act.wait_ge(S["gate_shifted"], 1)
    act.activation(G["w"][:, :, :], G["lg"][:, :, 0:E], ACT.Exp).then_inc(S["gate_exp"], 1)
    act.activation(G["t"][:, :], G["lg"][:, :, E], ACT.Exp, scale=-1.0).then_inc(S["gate_exp"], 1)


def logits_tensor(pe, b, S, weights, n):
    for m in range(TILES):
        last = accumulate(pe, b.psum[0:P, 7, m * n:(m + 1) * n],
                          [(tile_of(b.XT, k, m), weights[:, k, :]) for k in range(K)])
    last.then_inc(S["logits"], 1)


def gate_buffers(b, E):
    return {"lg": b.sb("gate_logits", [P, TILES, E + 1]),
            "w": b.sb("gate_weights", [P, TILES, E]),
            "s": b.sb("gate_sums", [P, TILES]),
            "t": b.sb("gate_thresholds", [P, TILES])}


def experts_vector(dve, b, S, w, first, E):
    for n in range(E * TILES):
        e, m = divmod(n, TILES)
        dve.wait_ge(S["expert"], n + 1)
        if n >= TILES:
            dve.wait_ge(S["expert_out"], n - TILES + 1)
        dve.scalar_tensor_tensor(b.X[:, m, :], b.psum[0:P, (first + n) % 7, :], w[:, m, e:e + 1], b.X[:, m, :],
                                 ALU.mult, ALU.add).then_inc(S["expert_out"], 1)


def experts_tensor(pe, b, S, W, first, E):
    for n in range(E * TILES):
        e, m = divmod(n, TILES)
        if e >= 4 and m == 0:
            pe.wait_ge(S[f"ring_in{e % 4}"], 16)
        if n >= 7:
            pe.wait_ge(S["expert_out"], n - 6)
        accumulate(pe, b.psum[0:P, (first + n) % 7, :],
                   [(tile_of(b.XT, k, m), W[:, ((e % 4) * K + k) * D:((e % 4) * K + k + 1) * D]) for k in range(K)]
                   ).then_inc(S["expert"], 1)


def experts_sync(sp, b, S, t, weights, W, E):
    for e in range(4, E):
        sp.wait_ge(S["expert"], TILES * (e - 3))
        sp.dma_start(W[:, (e - 4) * K * D:(e - 3) * K * D].rearrange("p (k n) -> p k n", k=K),
                     t[weights][e].rearrange("(k p) n -> p k n", p=128)).then_inc(S[f"ring_in{e % 4}"], 16)


def ffn_threshold(nc, b, t, slot, loaded, loads, load_next):
    S = Semaphores(nc, b.part)
    E = 8
    W, V = b.W[slot], b.V[slot]
    gate = b.U[slot][:, 0:K * (E + 1)].rearrange("p (k e) -> p k e", k=K)
    G = gate_buffers(b, E)
    wT = b.sb("gates_columns", [E, NODES])
    bias = V[0:E, D:2 * D]

    with nc.Block() as block:
        @block.sync
        def _(sp):
            experts_sync(sp, b, S, t, "L0_ffn_W_exp", W, E)
            load_next(sp)

        @block.vector
        def _(dve):
            prenorm_vector(dve, b, S)
            dve.wait_ge(loaded, loads)
            threshold_gates_vector(dve, b, S, G, E, V[0:P, 0:E + 1], 0.25)
            dve.wait_ge(S["gates_turned"], 1)
            dve.tensor_copy(wT[:, 0:4 * P], b.psum[0:E, 0, 0:4 * P]).then_inc(S["gates_out"], 1)
            dve.tensor_copy(wT[:, 4 * P:], b.psum[0:E, 1, 0:P]).then_inc(S["gates_out"], 1)
            for m in range(TILES):
                dve.wait_ge(S["bias"], m + 1)
                dve.tensor_tensor(b.X[:, m, :], b.psum[0:P, 2 + m, :], b.X[:, m, :], ALU.add).then_inc(S["bias_out"], 1)
            dve.wait_ge(S["bias_out"], TILES)
            experts_vector(dve, b, S, G["w"], 0, E)

        @block.scalar
        def _(act):
            prenorm_scalar(act, b, S)
            threshold_gates_scalar(act, b, S, G, E)

        @block.tensor
        def _(pe):
            prenorm_tensor(pe, b, S)
            pe.wait_ge(S["pre_columns"], TILES)
            pe.wait_ge(loaded, loads)
            logits_tensor(pe, b, S, gate, E + 1)
            pe.wait_ge(S["gates"], 1)
            for m in range(TILES):
                last = pe.transpose(b.psum[0:E, m // 4, (m % 4) * P:(m % 4 + 1) * P], G["w"][:, m, :], b.ident[0:P, 0:P])
            last.then_inc(S["gates_turned"], 1)
            pe.wait_ge(S["gates_out"], 2)
            for m in range(TILES):
                pe.matmul(b.psum[0:P, 2 + m, :], wT[:, m * P:(m + 1) * P], bias, start=True, stop=True
                          ).then_inc(S["bias"], 1)
            pe.wait_ge(S["bias_out"], TILES)
            experts_tensor(pe, b, S, W, 0, E)


def ffn_sinkhorn(nc, b, t, slot, loaded, loads, load_next):
    S = Semaphores(nc, b.part)
    E, ROUNDS = 8, 8
    TOP = NODES // E
    PICKS = -(-TOP // 8)
    SENTINELS = 8 * PICKS - TOP
    W = b.W[slot]
    PS = b.psum
    gate = b.U[slot][:, 0:K * E].rearrange("p (k e) -> p k e", k=K)
    T = b.sb("balanced", [P, TILES, E])
    T2 = b.sb("column_scaled", [P, TILES, E])
    rc = b.sb("column_factor", [P, E])
    rr = b.sb("row_factor", [P, TILES])
    rank = [b.sb(f"ranked{n}", [E, NODES + SENTINELS]) for n in range(2)]
    top8 = b.sb("top8", [E, 8])
    picked = b.sb("picked_columns", [E, NODES])
    sel = b.sb("picked", [P, TILES, E])
    w = b.sb("combine", [P, TILES, E])

    with nc.Block() as block:
        @block.sync
        def _(sp):
            experts_sync(sp, b, S, t, "L1_ffn_experts", W, E)
            load_next(sp)

        @block.vector
        def _(dve):
            prenorm_vector(dve, b, S)
            dve.wait_ge(S["logits"], 1)
            dve.tensor_scalar(T[:, :, :], PS[0:P, 7, 0:TILES * E].rearrange("p (m e) -> p m e", m=TILES), 1e-10, None,
                              ALU.max).then_inc(S["balanced"], 1)
            for i in range(ROUNDS):
                dve.wait_ge(S["column_sums"], i + 1)
                dve.reciprocal(rc[:, :], PS[0:P, 6, 0:E]).then_inc(S["bal"], 1)
                dve.wait_ge(S["bal"], 4 * i + 1)
                dve.tensor_tensor(T2[:, :, :], T[:, :, :], rc[:, :].unsqueeze(1).to_broadcast([P, TILES, E]), ALU.mult
                                  ).then_inc(S["bal"], 1)
                dve.wait_ge(S["bal"], 4 * i + 2)
                dve.tensor_reduce(rr[:, :], T2[:, :, :], AX.X, ALU.add).then_inc(S["bal"], 1)
                dve.wait_ge(S["bal"], 4 * i + 3)
                dve.reciprocal(rr[:, :], rr[:, :]).then_inc(S["bal"], 1)
                dve.wait_ge(S["bal"], 4 * i + 4)
                dve.tensor_tensor(T[:, :, :], T2[:, :, :], spread(rr[:, :], E), ALU.mult).then_inc(S["balanced"], 1)
            for n in range(SENTINELS):
                dve.memset(rank[0][:, NODES + n:NODES + n + 1], 4.0 + n).then_inc(S["ranked"], 1)
            dve.wait_ge(S["ranks_turned"], 1)
            dve.tensor_copy(rank[0][:, 0:4 * P], PS[0:E, 0, 0:4 * P]).then_inc(S["ranked"], 1)
            dve.tensor_copy(rank[0][:, 4 * P:NODES], PS[0:E, 1, 0:P]).then_inc(S["ranked"], 1)
            dve.wait_ge(S["ranked"], SENTINELS + 2)
            for n in range(PICKS):
                dve.max(top8[:, :], rank[n % 2][:, :]).then_inc(S["top8"], 1)
                dve.wait_ge(S["top8"], n + 1)
                dve.match_replace(rank[1 - n % 2][:, :], top8[:, :], rank[n % 2][:, :], -1.0).then_inc(S["taken"], 1)
                dve.wait_ge(S["taken"], n + 1)
            dve.tensor_scalar(picked[:, :], rank[PICKS % 2][:, 0:NODES], -1.0, None, ALU.is_equal).then_inc(S["picked"], 1)
            dve.wait_ge(S["picked_turned"], 1)
            dve.tensor_copy(sel[:, :, :], PS[0:P, 5, 0:TILES * E].rearrange("p (m e) -> p m e", m=TILES)
                            ).then_inc(S["comb"], 1)
            dve.wait_ge(S["comb"], 1)
            dve.tensor_reduce(rr[:, :], sel[:, :, :], AX.X, ALU.add).then_inc(S["comb"], 1)
            dve.scalar_tensor_tensor(w[:, :, :], T[:, :, :], 0.5, sel[:, :, :], ALU.is_gt, ALU.mult).then_inc(S["comb"], 1)
            dve.wait_ge(S["comb"], 3)
            dve.tensor_scalar(rr[:, :], rr[:, :], 1.0, None, ALU.add).then_inc(S["comb"], 1)
            dve.wait_ge(S["comb"], 4)
            dve.reciprocal(rr[:, :], rr[:, :]).then_inc(S["comb"], 1)
            dve.wait_ge(S["comb"], 5)
            dve.tensor_tensor(w[:, :, :], w[:, :, :], spread(rr[:, :], E), ALU.mult).then_inc(S["comb"], 1)
            dve.wait_ge(S["comb"], 6)
            experts_vector(dve, b, S, w, 0, E)

        @block.scalar
        def _(act):
            prenorm_scalar(act, b, S)

        @block.tensor
        def _(pe):
            prenorm_tensor(pe, b, S)
            pe.wait_ge(S["pre_columns"], TILES)
            pe.wait_ge(loaded, loads)
            logits_tensor(pe, b, S, gate, E)
            for i in range(ROUNDS):
                pe.wait_ge(S["balanced"], i + 1)
                accumulate(pe, PS[0:P, 6, 0:E], [(b.ones[0:P, 0:P], T[:, m, :]) for m in range(TILES)]
                           ).then_inc(S["column_sums"], 1)
            pe.wait_ge(S["balanced"], ROUNDS + 1)
            for m in range(TILES):
                last = pe.transpose(PS[0:E, m // 4, (m % 4) * P:(m % 4 + 1) * P], T[:, m, :], b.ident[0:P, 0:P])
            last.then_inc(S["ranks_turned"], 1)
            pe.wait_ge(S["picked"], 1)
            for m in range(TILES):
                last = pe.transpose(PS[0:P, 5, m * E:(m + 1) * E], picked[:, m * P:(m + 1) * P], b.ident[0:E, 0:E])
            last.then_inc(S["picked_turned"], 1)
            pe.wait_ge(S["comb"], 1)
            experts_tensor(pe, b, S, W, 0, E)


def attention(nc, b, t, layer, slot, loaded, loads, load_next, C, edged):
    S = Semaphores(nc, b.part)
    PS = b.psum
    HEADS, DH = 8, 64
    W, V = b.W[slot], b.V[slot]
    wq, wk, wv, wo = (W[:, n * K * D:(n + 1) * K * D].rearrange("p (k n) -> p k n", k=K) for n in range(4))
    w1 = V[:, 0:256].rearrange("p (k n) -> p k n", k=K)
    w2 = V[0:64, 256:768]
    ln_g, ln_b = V[0:P, 1024:1536], V[0:P, 1536:2048]
    cols = column_vectors(b, slot, [(n, K) for n in ("bq", "bo", "b2", "g1", "beta1", "g2", "beta2")] + [("b1", 1)])
    ITEMS = TILES * HEADS

    qT = b.sb("q_columns", [128, K, PADDED])
    kT = b.sb("k_columns", [128, K, PADDED])
    v = b.sb("v_rows", [P, TILES, D])
    bqs = b.sb("bq_scaled", [128, K])
    sc = V[0:P, 4 * D:4 * D + 2 * PADDED].rearrange("p (a n) -> p a n", a=2)
    pr = b.sb("probabilities", [P, 2, PADDED])
    pT = b.sb("probabilities_turned", [P, 2, TILES, P])
    top = b.sb("score_max", [P, ITEMS])
    ntop = b.sb("minus_max", [P, ITEMS])
    total = b.sb("prob_sum", [P, ITEMS])
    inv = b.sb("inverse_sum", [P, TILES, HEADS])
    att = b.sb("attended", [P, D])
    aT = b.sb("attended_columns", [128, K, PADDED])
    fT = V[0:64, 4 * D + 2 * PADDED:4 * D + 3 * PADDED]
    bs = b.sb("batch_stats", [128, K, 2, 6])
    bm = b.sb("batch_mean", [128, K, 2])
    bv = b.sb("batch_scale", [128, 4, K])
    z = qT

    def batch_norm_vector(dve, tag, gain, shift):
        for c in range(K):
            dve.bn_stats(bs[:, c, 0, :], z[:, c, 0:HALF]).then_inc(S[tag + "_stats"], 1)
            dve.bn_stats(bs[:, c, 1, :], z[:, c, HALF:NODES]).then_inc(S[tag + "_stats"], 1)
        dve.wait_ge(S[tag + "_stats"], 2 * K)
        for c in range(K):
            dve.bn_aggr(bm[:, c, :], bs[:, c, :, :].rearrange("p h s -> p (h s)")).then_inc(S[tag + "_aggr"], 1)
        dve.wait_ge(S[tag + "_aggr"], K)
        dve.tensor_scalar(bv[:, 0, :], bm[:, :, 1], 1e-5, None, ALU.add).then_inc(S[tag + "_var"], 1)
        dve.wait_ge(S[tag + "_root"], 1)
        dve.reciprocal(bv[:, 1, :], bv[:, 1, :]).then_inc(S[tag], 1)
        dve.wait_ge(S[tag], 1)
        dve.tensor_tensor(bv[:, 2, :], bv[:, 1, :], gain, ALU.mult).then_inc(S[tag], 1)
        dve.wait_ge(S[tag], 2)
        dve.tensor_tensor(bv[:, 3, :], bm[:, :, 0], bv[:, 2, :], ALU.mult).then_inc(S[tag], 1)
        dve.wait_ge(S[tag], 3)
        dve.tensor_tensor(bv[:, 3, :], shift, bv[:, 3, :], ALU.subtract).then_inc(S[tag], 1)
        dve.wait_ge(S[tag], 4)
        for c in range(K):
            dve.tensor_scalar(b.XT[:, c, 0:NODES], z[:, c, 0:NODES], bv[:, 2, c:c + 1], bv[:, 3, c:c + 1], ALU.mult, ALU.add
                              ).then_inc(S[tag + "_out"], 1)

    def batch_norm_scalar(act, tag):
        act.wait_ge(S[tag + "_var"], 1)
        act.activation(bv[:, 1, :], bv[:, 0, :], ACT.Sqrt).then_inc(S[tag + "_root"], 1)

    with nc.Block() as block:
        @block.sync
        def _(sp):
            load_next(sp)

        @block.vector
        def _(dve):
            def turned_copy(dve, n):
                dve.wait_ge(S["turned"], n + 1)
                if n >= 2:
                    dve.wait_ge(S["pv"], n - 1)
                dve.tensor_copy(pT[:, n % 2, 0:4, :], PS[0:P, 4, 0:4 * P].rearrange("p (s d) -> p s d", s=4)
                                ).then_inc(S["turned_out"], 1)
                dve.tensor_copy(pT[:, n % 2, 4, :], PS[0:P, 5, 0:P]).then_inc(S["turned_out"], 1)

            def normalise(dve, m):
                dve.wait_ge(S["probs"], HEADS * (m + 1))
                dve.reciprocal(inv[:, m, :], total[:, HEADS * m:HEADS * (m + 1)]).then_inc(S["inv"], 1)
                dve.wait_ge(S["inv"], 2 * m + 1)
                dve.tensor_scalar(inv[:, m, :], inv[:, m, :], edged[:, m:m + 1], None, ALU.mult).then_inc(S["inv"], 1)
                dve.wait_ge(S["inv"], 2 * m + 2)
                dve.wait_ge(S["pv"], HEADS * (m + 1))
                if m >= 1:
                    dve.wait_ge(S["att_turned"], m)
                dve.tensor_tensor(att[:, :].rearrange("p (h n) -> p h n", h=HEADS),
                                  PS[0:P, 6 + m % 2, :].rearrange("p (h n) -> p h n", h=HEADS),
                                  spread(inv[:, m, :], DH), ALU.mult).then_inc(S["att"], 1)

            if layer == 0:
                prenorm_vector(dve, b, S)
                dve.wait_ge(b.counts_loaded, 16)
                dve.tensor_reduce(edged[:, :], C[:, :, :], AX.X, ALU.max).then_inc(S["edged"], 1)
                dve.wait_ge(S["edged"], 1)
                dve.tensor_scalar(edged[:, :], edged[:, :], 0.0, None, ALU.is_gt).then_inc(S["edged"], 1)
                dve.tensor_scalar(v[:, :, :], C[:, :, 0:D], 0.0, None, ALU.is_equal).then_inc(S["none"], 1)
                dve.tensor_scalar(aT[0:P, 0:1, 0:TILES * (PADDED - D)].rearrange("p a (m n) -> p (a m) n", m=TILES),
                                  C[:, :, D:], 0.0, None, ALU.is_equal).then_inc(S["none"], 1)
                dve.wait_ge(S["none"], 2)
                dve.tensor_tensor(C[:, :, 0:D], C[:, :, 0:D], v[:, :, :], ALU.add).then_inc(S["none"], 1)
                dve.tensor_tensor(C[:, :, D:], C[:, :, D:],
                                  aT[0:P, 0:1, 0:TILES * (PADDED - D)].rearrange("p a (m n) -> p (a m) n", m=TILES),
                                  ALU.add).then_inc(S["counts_safe"], 1)
                dve.wait_ge(S["counts_log"], 1)
                dve.scalar_tensor_tensor(C[:, :, 0:D], v[:, :, :], -BIG, C[:, :, 0:D], ALU.mult, ALU.add
                                         ).then_inc(S["log_counts"], 1)
                dve.scalar_tensor_tensor(C[:, :, D:],
                                         aT[0:P, 0:1, 0:TILES * (PADDED - D)].rearrange("p a (m n) -> p (a m) n", m=TILES),
                                         -BIG, C[:, :, D:], ALU.mult, ALU.add).then_inc(S["log_counts"], 1)
                dve.wait_ge(S["log_counts"], 2)
            dve.memset(aT[:, :, NODES:], 0.0).then_inc(S["padding"], 1)
            dve.wait_ge(loaded, loads)
            dve.tensor_scalar(bqs[:, :], cols["bq"], float(DH) ** -0.5, None, ALU.mult).then_inc(S["bq"], 1)
            for c in range(K):
                dve.wait_ge(S["qk"], 2 * c + 2)
                bank = 4 * (c % 2) + 2
                dve.tensor_copy(halves(kT[:, c, :]), PS[:, bank:bank + 2, 0:HALF]).then_inc(S["k_out"], 1)
            for m in range(TILES):
                dve.wait_ge(S["v"], m + 1)
                dve.tensor_copy(v[:, m, :], PS[0:P, m, :]).then_inc(S["v_out"], 1)
            for n in range(ITEMS):
                m, h = divmod(n, HEADS)
                dve.wait_ge(S["scores"], n + 1)
                if n >= 2:
                    dve.wait_ge(S["probs"], n - 1)
                dve.tensor_tensor_reduce(halves(sc[:, n % 2, :]), PS[0:P, 2 * (n % 2):2 * (n % 2) + 2, 0:HALF],
                                         halves(C[:, m, :]), 1.0, -3e38, ALU.add, ALU.max, top[:, n:n + 1]
                                         ).then_inc(S["scored"], 1)
                dve.wait_ge(S["scored"], n + 1)
                dve.tensor_scalar(ntop[:, n:n + 1], top[:, n:n + 1], -1.0, None, ALU.mult).then_inc(S["ntop"], 1)
                if n >= 1:
                    turned_copy(dve, n - 1)
                if h == 1 and m >= 1:
                    normalise(dve, m - 1)
            turned_copy(dve, ITEMS - 1)
            normalise(dve, TILES - 1)
            for c in range(K):
                bank = 2 * (c % 4)
                dve.wait_ge(S["wo"], c + 1)
                dve.scalar_tensor_tensor(halves(z[:, c, :]), PS[:, bank:bank + 2, 0:HALF], cols["bo"][:, c:c + 1],
                                         halves(b.XT[:, c, :]), ALU.add, ALU.add).then_inc(S["z1"], 1)
            dve.wait_ge(S["z1"], K)
            batch_norm_vector(dve, "bn1", cols["g1"], cols["beta1"])
            for c in range(K):
                bank = 2 * (c % 4)
                dve.wait_ge(S["ff2"], c + 1)
                dve.scalar_tensor_tensor(halves(z[:, c, :]), PS[:, bank:bank + 2, 0:HALF], cols["b2"][:, c:c + 1],
                                         halves(b.XT[:, c, :]), ALU.add, ALU.add).then_inc(S["z2"], 1)
            dve.wait_ge(S["z2"], K)
            batch_norm_vector(dve, "bn2", cols["g2"], cols["beta2"])
            if layer == 1:
                for m in range(TILES):
                    dve.wait_ge(S["rows"], m + 1)
                    dve.tensor_copy(b.XN[:, m, :], PS[0:P, m, :]).then_inc(S["rows_out"], 1)
                dve.wait_ge(S["rows_out"], TILES)
                row_stats(dve, b, S, "last", [[b.XN[:, m, :]] for m in range(TILES)])
                for m in range(TILES):
                    dve.tensor_scalar(b.XN[:, m, :], b.XN[:, m, :], b.mv[:, m, 0:1], b.rstd[:, m:m + 1],
                                      ALU.subtract, ALU.mult).then_inc(S["last_norm"], 1)
                    dve.tensor_tensor(b.X[:, m, :], b.X[:, m, :], ln_b, ALU.add).then_inc(S["last_shift"], 1)
                for m in range(TILES):
                    dve.wait_ge(S["last_norm"], m + 1)
                    dve.tensor_tensor(b.XN[:, m, :], b.XN[:, m, :], ln_g, ALU.mult).then_inc(S["last_gain"], 1)
                dve.wait_ge(S["last_shift"], TILES)
                for m in range(TILES):
                    dve.wait_ge(S["last_gain"], m + 1)
                    dve.tensor_tensor(b.X[:, m, :], b.X[:, m, :], b.XN[:, m, :], ALU.add).then_inc(S["last_sum"], 1)

        @block.scalar
        def _(act):
            def att_columns(act, m):
                act.wait_ge(S["att_turned"], m + 1)
                act.activation(aT[:, :, m * P:(m + 1) * P], PS[:, 6 + m % 2, 0:K * P].rearrange("p (k n) -> p k n", k=K),
                               ACT.Copy).then_inc(S["att_columns"], 1)

            if layer == 0:
                prenorm_scalar(act, b, S)
                act.wait_ge(S["counts_safe"], 1)
                act.wait_ge(S["none"], 3)
                act.activation(C[:, :, :], C[:, :, :], ACT.Ln).then_inc(S["counts_log"], 1)
            act.wait_ge(S["bq"], 1)
            for c in range(K):
                act.wait_ge(S["qk"], 2 * c + 1)
                bank = 4 * (c % 2)
                act.activation(halves(qT[:, c, :]), PS[:, bank:bank + 2, 0:HALF], ACT.Identity, bias=bqs[:, c:c + 1],
                               scale=float(DH) ** -0.5).then_inc(S["q_out"], 1)
            for n in range(ITEMS):
                m, h = divmod(n, HEADS)
                act.wait_ge(S["ntop"], n + 1)
                if n >= 2:
                    act.wait_ge(S["turned"], n - 1)
                act.activation(pr[:, n % 2, :], sc[:, n % 2, :], ACT.Exp, bias=ntop[:, n:n + 1], scale=1.0,
                               accum_out=total[:, n:n + 1]).then_inc(S["probs"], 1)
                if h == 3 and m >= 1:
                    att_columns(act, m - 1)
            att_columns(act, TILES - 1)
            batch_norm_scalar(act, "bn1")
            act.wait_ge(S["ff1"], 1)
            act.activation(halves(fT), PS[0:64, 0:2, 0:HALF], ACT.Relu, bias=cols["b1"][0:64, :]).then_inc(S["ff"], 1)
            batch_norm_scalar(act, "bn2")
            if layer == 1:
                row_root(act, b, S, "last")

        @block.tensor
        def _(pe):
            if layer == 0:
                prenorm_tensor(pe, b, S)
                pe.wait_ge(S["pre_columns"], TILES)
            pe.wait_ge(loaded, loads)
            for c in range(K):
                for part, w in enumerate((wq, wk)):
                    if c >= 2:
                        pe.wait_ge(S[("q_out", "k_out")[part]], c - 1)
                    for h in range(2):
                        last = accumulate(pe, PS[:, 4 * (c % 2) + 2 * part + h, 0:HALF],
                                          [(w[:, k, c * 128:(c + 1) * 128], b.XT[:, k, h * HALF:(h + 1) * HALF])
                                           for k in range(K)])
                    last.then_inc(S["qk"], 1)
            pe.wait_ge(S["q_out"], K)
            pe.wait_ge(S["k_out"], K)
            for m in range(TILES):
                accumulate(pe, PS[0:P, m, :], [(tile_of(b.XT, k, m), wv[:, k, :]) for k in range(K)]).then_inc(S["v"], 1)
            pe.wait_ge(S["v_out"], TILES)

            def scores(n):
                m, h = divmod(n, HEADS)
                rows = slice(DH * (h % 2), DH * (h % 2) + DH)
                if n >= 2:
                    pe.wait_ge(S["scored"], n - 1)
                for half in range(2):
                    last = pe.matmul(PS[0:P, 2 * (n % 2) + half, 0:HALF], qT[rows, h // 2, m * P:(m + 1) * P],
                                     kT[rows, h // 2, half * HALF:(half + 1) * HALF], start=True, stop=True)
                last.then_inc(S["scores"], 1)

            def turn(n):
                pe.wait_ge(S["probs"], n + 1)
                if n >= 1:
                    pe.wait_ge(S["turned_out"], 2 * n)
                for s in range(TILES):
                    last = pe.transpose(PS[0:P, 4 + s // 4, (s % 4) * P:(s % 4 + 1) * P], pr[:, n % 2, s * P:(s + 1) * P],
                                        b.ident[0:P, 0:P])
                last.then_inc(S["turned"], 1)

            def weigh(n):
                m, h = divmod(n, HEADS)
                if h == 0 and m >= 2:
                    pe.wait_ge(S["att_columns"], m - 1)
                pe.wait_ge(S["turned_out"], 2 * n + 2)
                for s in range(TILES):
                    last = pe.matmul(PS[0:P, 6 + m % 2, h * DH:(h + 1) * DH], pT[:, n % 2, s, :],
                                     v[:, s, h * DH:(h + 1) * DH], start=(s == 0), stop=(s == TILES - 1),
                                     skip_group_check=True)
                last.then_inc(S["pv"], 1)

            def turn_attended(m):
                pe.wait_ge(S["att"], m + 1)
                for k in range(K):
                    last = pe.transpose(PS[:, 6 + m % 2, k * P:(k + 1) * P], att[:, k * 128:(k + 1) * 128],
                                        b.ident[0:P, 0:P])
                last.then_inc(S["att_turned"], 1)

            scores(0)
            for n in range(ITEMS):
                m, h = divmod(n, HEADS)
                if n + 1 < ITEMS:
                    scores(n + 1)
                turn(n)
                if n >= 1:
                    weigh(n - 1)
                if h == 3 and m >= 1:
                    turn_attended(m - 1)
            weigh(ITEMS - 1)
            turn_attended(TILES - 1)
            pe.wait_ge(S["att_columns"], TILES)
            pe.wait_ge(S["padding"], 1)
            for c in range(K):
                for h in range(2):
                    last = accumulate(pe, PS[:, 2 * c + h, 0:HALF],
                                      [(wo[:, k, c * 128:(c + 1) * 128], aT[:, k, h * HALF:(h + 1) * HALF])
                                       for k in range(K)])
                last.then_inc(S["wo"], 1)
            pe.wait_ge(S["bn1_out"], K)
            for h in range(2):
                last = accumulate(pe, PS[0:64, h, 0:HALF],
                                  [(w1[:, k, :], b.XT[:, k, h * HALF:(h + 1) * HALF]) for k in range(K)])
            last.then_inc(S["ff1"], 1)
            pe.wait_ge(S["ff"], 1)
            for c in range(K):
                for h in range(2):
                    last = pe.matmul(PS[:, 2 * c + h, 0:HALF], w2[:, c * 128:(c + 1) * 128],
                                     fT[:, h * HALF:(h + 1) * HALF], start=True, stop=True)
                last.then_inc(S["ff2"], 1)
            if layer == 1:
                pe.wait_ge(S["bn2_out"], K)
                for m in range(TILES):
                    for k in range(K):
                        last = pe.transpose(PS[0:P, m, k * 128:(k + 1) * 128], tile_of(b.XT, k, m), b.ident[:, :])
                    last.then_inc(S["rows"], 1)



def relations(nc, b, t, layer, slot, loaded, loads, load_next, C2):
    S = Semaphores(nc, b.part)
    PS = b.psum
    W = b.W[slot]
    mixed = W[:, 0:STEPS * D].rearrange("p (a n) -> p a n", a=STEPS)
    root = W[:, STEPS * D:STEPS * D + K * D].rearrange("p (k n) -> p k n", k=K)
    bias = b.V[slot][0:P, 0:D]
    gate = b.U[slot][:, 0:2 * K].rearrange("p (k r) -> p k r", k=K)
    g = b.sb("gates", [P, TILES, 2])
    xg = b.sb("gated", [P, 2, TILES, D])
    yT = b.sb("gathered_columns", [128, STEPS, PADDED])

    with nc.Block() as block:
        @block.sync
        def _(sp):
            load_next(sp)

        @block.vector
        def _(dve):
            if layer == 0:
                prenorm_vector(dve, b, S)
                dve.wait_ge(b.relations_loaded, 32)
                dve.tensor_tensor(C2[:, 0, :, :], C2[:, 0, :, :], C2[:, 1, :, :], ALU.subtract).then_inc(S["count_0"], 1)
            dve.wait_ge(S["gate_exp"], 1)
            dve.tensor_scalar(g[:, :, :], g[:, :, :], 1.0, None, ALU.add).then_inc(S["gate"], 1)
            dve.wait_ge(S["gate"], 1)
            dve.reciprocal(g[:, :, :], g[:, :, :]).then_inc(S["gate"], 1)
            dve.wait_ge(S["gate"], 2)
            for m in range(TILES):
                dve.tensor_scalar(xg[:, 1, m, :], b.XN[:, m, :], g[:, m, 1:2], None, ALU.mult).then_inc(S["gated_1"], 1)
            for n in range(2 * K):
                c, r = divmod(n, 2)
                bank = 2 * (n % 4)
                dve.wait_ge(S["gathered"], n + 1)
                dve.tensor_copy(halves(yT[64 * r:64 * r + 64, 2 * c, :]), PS[0:64, bank:bank + 2, 0:HALF]
                                ).then_inc(S["y_low"], 1)
            dve.wait_ge(loaded, loads)
            for m in range(TILES):
                dve.wait_ge(S["sum"], m + 1)
                if layer == 0:
                    dve.tensor_tensor(xg[:, 0, m, :], PS[0:P, m, :], bias, ALU.add).then_inc(S["biased"], 1)
                else:
                    dve.tensor_tensor(xg[:, 0, m, :], PS[0:P, m, :], bias, ALU.add).then_inc(S["biased"], 1)
                    dve.wait_ge(S["biased"], m + 1)
                    dve.tensor_tensor(b.X[:, m, :], xg[:, 0, m, :], b.X[:, m, :], ALU.add).then_inc(S["added"], 1)

        @block.scalar
        def _(act):
            if layer == 0:
                prenorm_scalar(act, b, S)
            act.wait_ge(S["logits"], 1)
            act.activation(g[:, :, :], PS[0:P, 7, 0:2 * TILES].rearrange("p (m r) -> p m r", m=TILES), ACT.Exp, scale=-1.0
                           ).then_inc(S["gate_exp"], 1)
            act.wait_ge(S["gate"], 2)
            for m in range(TILES):
                act.activation(xg[:, 0, m, :], b.XN[:, m, :], ACT.Copy, scale=g[:, m, 0:1]).then_inc(S["gated_0"], 1)
            for n in range(2 * K):
                c, r = divmod(n, 2)
                bank = 2 * (n % 4)
                act.wait_ge(S["gathered"], n + 1)
                act.activation(halves(yT[64 * r:64 * r + 64, 2 * c + 1, :]), PS[64:128, bank:bank + 2, 0:HALF], ACT.Copy
                               ).then_inc(S["y_high"], 1)
            if layer == 0:
                for m in range(TILES):
                    act.wait_ge(S["biased"], m + 1)
                    act.activation(b.XN[:, m, :], xg[:, 0, m, :], ACT.Relu).then_inc(S["x_rows"], 1)
                for m in range(TILES):
                    act.wait_ge(S["x_turned"], m + 1)
                    act.activation(b.XT[:, :, m * P:(m + 1) * P], PS[:, m, 0:K * P].rearrange("p (k n) -> p k n", k=K),
                                   ACT.Copy).then_inc(S["x_columns"], 1)

        @block.tensor
        def _(pe):
            if layer == 0:
                prenorm_tensor(pe, b, S)
                pe.wait_ge(S["pre_columns"], TILES)
            pe.wait_ge(loaded, loads)
            logits_tensor(pe, b, S, gate, 2)
            if layer == 0:
                pe.wait_ge(S["count_0"], 1)
            pe.wait_ge(S["gated_0"], TILES)
            pe.wait_ge(S["gated_1"], TILES)
            for n in range(2 * K):
                c, r = divmod(n, 2)
                if n >= 4:
                    pe.wait_ge(S["y_low"], n - 3)
                    pe.wait_ge(S["y_high"], n - 3)
                for h in range(2):
                    last = accumulate(pe, PS[:, 2 * (n % 4) + h, 0:HALF],
                                      [(xg[:, r, m, c * 128:(c + 1) * 128], C2[:, r, m, h * HALF:(h + 1) * HALF])
                                       for m in range(TILES)])
                last.then_inc(S["gathered"], 1)
            pe.wait_ge(S["y_low"], 2 * K)
            pe.wait_ge(S["y_high"], 2 * K)
            for m in range(TILES):
                accumulate(pe, PS[0:P, m, :], [(tile_of(yT, a, m), mixed[:, a, :]) for a in range(STEPS)] +
                           [(tile_of(b.XT, k, m), root[:, k, :]) for k in range(K)]).then_inc(S["sum"], 1)
            if layer == 0:
                for m in range(TILES):
                    pe.wait_ge(S["x_rows"], m + 1)
                    for k in range(K):
                        last = pe.transpose(PS[:, m, k * P:(k + 1) * P], b.XN[:, m, k * 128:(k + 1) * 128],
                                            b.ident[0:P, 0:P])
                    last.then_inc(S["x_turned"], 1)



def ffn_top2(nc, b, t, slot, loaded, loads, load_next):
    S = Semaphores(nc, b.part)
    PS = b.psum
    E = 8
    FILL = 6
    W = b.W[slot]
    w1 = W[:, 0:K * D].rearrange("p (k n) -> p k n", k=K)
    w2 = W[:, K * D:2 * K * D].rearrange("p (k n) -> p k n", k=K)
    b2 = W[0:P, 2 * K * D:].rearrange("p (e n) -> p e n", e=E)
    gamma = b.V[slot][0:P, :].rearrange("p (e n) -> p e n", e=E)
    router = b.U[slot][:, 0:K * E].rearrange("p (k e) -> p k e", k=K)
    b1 = b.U[slot][:, K * E:K * E + K]
    lg = b.sb("router_logits", [P, TILES, E + FILL])
    lg2 = b.sb("router_taken", [P, TILES, E + FILL])
    top8 = b.sb("router_top8", [P, TILES, 8])
    sel = b.sb("router_sel", [P, TILES, E])
    w = b.sb("router_weights", [P, TILES, E])
    s = b.sb("router_sums", [P, TILES])
    wT = b.sb("router_columns", [E, NODES])
    beta = b.sb("beta", [E, D])
    fT = b.sb("hidden_columns", [128, K, PADDED])
    xb = b.sb("x_plus_b2", [P, 2, TILES, D])
    y = b.sb("y", [P, 2, TILES, D])
    st = b.sb("y_stats", [P, 2, TILES, 6])
    mv = b.sb("y_mean", [P, 2, TILES, 2])
    sd = b.sb("y_root", [P, 2, TILES])
    ws = b.sb("y_scale", [P, 2, TILES])
    nm = b.sb("y_shift", [P, 2, TILES])

    with nc.Block() as block:
        @block.sync
        def _(sp):
            sp.dma_start(beta[:, :], t["L2_ffn_beta"]).then_inc(S["beta_in"], 16)
            load_next(sp)

        @block.gpsimd
        def _(pool):
            pool.wait_ge(loaded, loads)
            pool.wait_ge(S["pre_rows"], TILES)
            for e in range(E):
                if e >= 2:
                    pool.wait_ge(S["y_sum"], TILES * (e - 1))
                for m in range(TILES):
                    pool.tensor_tensor(xb[:, e % 2, m, :], b.XN[:, m, :], b2[:, e, :], ALU.add).then_inc(S["xb"], 1)

        @block.vector
        def _(dve):
            prenorm_vector(dve, b, S)
            dve.memset(lg[:, :, E:], 3e38).then_inc(S["route"], 1)
            dve.wait_ge(S["logits"], 1)
            dve.tensor_copy(lg[:, :, 0:E], PS[0:P, 7, 0:TILES * E].rearrange("p (m e) -> p m e", m=TILES)
                            ).then_inc(S["route"], 1)
            dve.wait_ge(S["route"], 2)
            for m in range(TILES):
                dve.max(top8[:, m, :], lg[:, m, :]).then_inc(S["top8"], 1)
            for m in range(TILES):
                dve.wait_ge(S["top8"], m + 1)
                dve.match_replace(lg2[:, m, :], top8[:, m, :], lg[:, m, :], -3e38).then_inc(S["route"], 1)
            dve.wait_ge(S["route"], 2 + TILES)
            dve.tensor_tensor(sel[:, :, :], lg[:, :, 0:E], lg2[:, :, 0:E], ALU.not_equal).then_inc(S["route"], 1)
            dve.tensor_tensor(w[:, :, :], lg[:, :, 0:E], top8[:, :, FILL:FILL + 1].to_broadcast([P, TILES, E]),
                              ALU.subtract).then_inc(S["route_shifted"], 1)
            dve.wait_ge(S["route_exp"], 1)
            dve.wait_ge(S["route"], 3 + TILES)
            dve.tensor_tensor(w[:, :, :], w[:, :, :], sel[:, :, :], ALU.mult).then_inc(S["route"], 1)
            dve.wait_ge(S["route"], 4 + TILES)
            dve.tensor_reduce(s[:, :], w[:, :, :], AX.X, ALU.add).then_inc(S["route"], 1)
            dve.wait_ge(S["route"], 5 + TILES)
            dve.reciprocal(s[:, :], s[:, :]).then_inc(S["route"], 1)
            dve.wait_ge(S["route"], 6 + TILES)
            dve.tensor_tensor(w[:, :, :], w[:, :, :], spread(s[:, :], E), ALU.mult).then_inc(S["gates"], 1)
            dve.wait_ge(S["gates_turned"], 1)
            dve.tensor_copy(wT[:, 0:4 * P], PS[0:E, 0, 0:4 * P]).then_inc(S["gates_out"], 1)
            dve.tensor_copy(wT[:, 4 * P:], PS[0:E, 1, 0:P]).then_inc(S["gates_out"], 1)
            for m in range(TILES):
                dve.wait_ge(S["betas"], m + 1)
                dve.tensor_tensor(b.X[:, m, :], PS[0:P, 2 + m, :], b.X[:, m, :], ALU.add).then_inc(S["betas_out"], 1)
            for e in range(E + 1):
                if e < E:
                    for m in range(TILES):
                        n = e * TILES + m
                        dve.wait_ge(S["expert"], n + 1)
                        dve.wait_ge(S["xb"], n + 1)
                        if e >= 2:
                            dve.wait_ge(S["added"], (e - 2) * TILES + m + 1)
                        dve.tensor_tensor(y[:, e % 2, m, :], PS[0:P, n % 8, :], xb[:, e % 2, m, :], ALU.add
                                          ).then_inc(S["y_sum"], 1)
                    for m in range(TILES):
                        dve.wait_ge(S["y_sum"], e * TILES + m + 1)
                        dve.bn_stats(st[:, e % 2, m, :], y[:, e % 2, m, :]).then_inc(S["y_stats"], 1)
                    dve.wait_ge(S["y_stats"], TILES * (e + 1))
                    for m in range(TILES):
                        dve.bn_aggr(mv[:, e % 2, m, :], st[:, e % 2, m, :]).then_inc(S["y_aggr"], 1)
                    dve.wait_ge(S["y_aggr"], TILES * (e + 1))
                    dve.tensor_scalar(sd[:, e % 2, :], mv[:, e % 2, :, 1], 1e-6, None, ALU.add).then_inc(S["y_var"], 1)
                    dve.wait_ge(S["y_root"], e + 1)
                    dve.reciprocal(ws[:, e % 2, :], sd[:, e % 2, :]).then_inc(S["y_scale"], 1)
                    dve.wait_ge(S["y_scale"], 2 * e + 1)
                    dve.tensor_tensor(ws[:, e % 2, :], ws[:, e % 2, :], w[:, :, e], ALU.mult).then_inc(S["y_scale"], 1)
                    dve.wait_ge(S["y_scale"], 2 * e + 2)
                    dve.scalar_tensor_tensor(nm[:, e % 2, :], mv[:, e % 2, :, 0], -1.0, ws[:, e % 2, :], ALU.mult, ALU.mult
                                             ).then_inc(S["y_shift"], 1)
                if e >= 1:
                    f = e - 1
                    for m in range(TILES):
                        n = f * TILES + m
                        dve.wait_ge(S["y_norm"], n + 1)
                        dve.tensor_tensor(y[:, f % 2, m, :], y[:, f % 2, m, :], gamma[:, f, :], ALU.mult
                                          ).then_inc(S["y_gain"], 1)
                    for m in range(TILES):
                        dve.wait_ge(S["y_gain"], f * TILES + m + 1)
                        if f == 0:
                            dve.wait_ge(S["betas_out"], m + 1)
                        else:
                            dve.wait_ge(S["added"], (f - 1) * TILES + m + 1)
                        dve.tensor_tensor(b.X[:, m, :], b.X[:, m, :], y[:, f % 2, m, :], ALU.add).then_inc(S["added"], 1)

        @block.scalar
        def _(act):
            prenorm_scalar(act, b, S)
            for c in range(K):
                act.wait_ge(S["hidden"], c + 1)
                bank = 2 * (c % 3)
                act.activation(halves(fT[:, c, :]), PS[:, bank:bank + 2, 0:HALF], ACT.Relu, bias=b1[:, c:c + 1]
                               ).then_inc(S["hidden_out"], 1)
            act.wait_ge(S["route_shifted"], 1)
            act.activation(w[:, :, :], w[:, :, :], ACT.Exp).then_inc(S["route_exp"], 1)
            for e in range(E):
                act.wait_ge(S["y_var"], e + 1)
                act.activation(sd[:, e % 2, :], sd[:, e % 2, :], ACT.Sqrt).then_inc(S["y_root"], 1)
                act.wait_ge(S["y_shift"], e + 1)
                for m in range(TILES):
                    act.activation(y[:, e % 2, m, :], y[:, e % 2, m, :], ACT.Identity, bias=nm[:, e % 2, m:m + 1],
                                   scale=ws[:, e % 2, m:m + 1]).then_inc(S["y_norm"], 1)

        @block.tensor
        def _(pe):
            prenorm_tensor(pe, b, S)
            pe.wait_ge(S["pre_columns"], TILES)
            pe.wait_ge(loaded, loads)
            logits_tensor(pe, b, S, router, E)
            for c in range(K):
                if c >= 3:
                    pe.wait_ge(S["hidden_out"], c - 2)
                for h in range(2):
                    last = accumulate(pe, PS[:, 2 * (c % 3) + h, 0:HALF],
                                      [(w1[:, k, c * 128:(c + 1) * 128], b.XT[:, k, h * HALF:(h + 1) * HALF])
                                       for k in range(K)])
                last.then_inc(S["hidden"], 1)
            pe.wait_ge(S["hidden_out"], K)
            pe.wait_ge(S["gates"], 1)
            for m in range(TILES):
                last = pe.transpose(PS[0:E, m // 4, (m % 4) * P:(m % 4 + 1) * P], w[:, m, :], b.ident[0:P, 0:P])
            last.then_inc(S["gates_turned"], 1)
            pe.wait_ge(S["gates_out"], 2)
            pe.wait_ge(S["beta_in"], 16)
            for m in range(TILES):
                pe.matmul(PS[0:P, 2 + m, :], wT[:, m * P:(m + 1) * P], beta[:, :], start=True, stop=True
                          ).then_inc(S["betas"], 1)
            pe.wait_ge(S["betas_out"], TILES)
            for n in range(E * TILES):
                e, m = divmod(n, TILES)
                rows = slice(64 * (e % 2), 64 * (e % 2) + 64)
                if n >= 8:
                    pe.wait_ge(S["y_sum"], n - 7)
                pe.matmul(PS[0:P, n % 8, :], fT[rows, e // 2, m * P:(m + 1) * P], w2[rows, e // 2, :],
                          start=True, stop=True).then_inc(S["expert"], 1)



def isomorphism(nc, b, t, slot, loaded, loads, load_next):
    S = Semaphores(nc, b.part)
    PS = b.psum
    W = b.W[slot]
    w1 = W[:, 0:K * D].rearrange("p (k n) -> p k n", k=K)
    w2 = W[:, K * D:2 * K * D].rearrange("p (k n) -> p k n", k=K)
    b1 = b.U[slot][:, 0:K]
    b2 = b.V[slot][0:P, 0:D]
    hT = b.sb("h_columns", [128, K, PADDED])
    fT = b.sb("hidden_columns", [128, K, PADDED])

    with nc.Block() as block:
        @block.sync
        def _(sp):
            load_next(sp)

        @block.vector
        def _(dve):
            prenorm_vector(dve, b, S)
            dve.wait_ge(loaded, loads)
            for m in range(TILES):
                dve.tensor_tensor(b.X[:, m, :], b.X[:, m, :], b2, ALU.add).then_inc(S["b2"], 1)
            dve.wait_ge(S["pre_columns"], TILES)
            for c in range(K):
                dve.wait_ge(S["aggregated"], c + 1)
                dve.tensor_tensor(halves(hT[:, c, :]), PS[:, 2 * c:2 * c + 2, 0:HALF], halves(b.XT[:, c, :]), ALU.add
                                  ).then_inc(S["h"], 1)
            dve.wait_ge(S["b2"], TILES)
            for m in range(TILES):
                dve.wait_ge(S["down"], m + 1)
                dve.tensor_tensor(b.X[:, m, :], PS[0:P, m, :], b.X[:, m, :], ALU.add).then_inc(S["added"], 1)

        @block.scalar
        def _(act):
            prenorm_scalar(act, b, S)
            act.wait_ge(loaded, loads)
            for c in range(K):
                act.wait_ge(S["up"], c + 1)
                act.activation(halves(fT[:, c, :]), PS[:, 2 * c:2 * c + 2, 0:HALF], ACT.Relu, bias=b1[:, c:c + 1]
                               ).then_inc(S["up_out"], 1)

        @block.tensor
        def _(pe):
            prenorm_tensor(pe, b, S)
            pe.wait_ge(S["pre_columns"], TILES)
            for c in range(K):
                for h in range(2):
                    last = accumulate(pe, PS[:, 2 * c + h, 0:HALF],
                                      [(b.XN[:, m, c * 128:(c + 1) * 128], b.CT[:, m, h * HALF:(h + 1) * HALF])
                                       for m in range(TILES)])
                last.then_inc(S["aggregated"], 1)
            pe.wait_ge(S["h"], K)
            pe.wait_ge(loaded, loads)
            for c in range(K):
                for h in range(2):
                    last = accumulate(pe, PS[:, 2 * c + h, 0:HALF],
                                      [(w1[:, k, c * 128:(c + 1) * 128], hT[:, k, h * HALF:(h + 1) * HALF])
                                       for k in range(K)])
                last.then_inc(S["up"], 1)
            pe.wait_ge(S["up_out"], K)
            for m in range(TILES):
                accumulate(pe, PS[0:P, m, :], [(tile_of(fT, k, m), w2[:, k, :]) for k in range(K)]).then_inc(S["down"], 1)



def ffn_lora(nc, b, t, slot, loaded, loads, out):
    S = Semaphores(nc, b.part)
    PS = b.psum
    E, R = 4, 16
    W = b.W[slot]
    fc2 = b.W[1 - slot]
    gate = b.U[slot][:, 0:K * (E + 1)].rearrange("p (k e) -> p k e", k=K)
    down = b.V[slot][:, 0:E * K * R].rearrange("p (e k r) -> p e k r", e=E, k=K)
    up = b.V[slot][:, 256:256 + E * K * R].rearrange("p (e k r) -> p e k r", e=E, k=K)
    G = gate_buffers(b, E)
    up_wide = b.sb("up_wide", [128, E, K, E * R])
    up_fc2 = b.sb("up_times_fc2", [E * R, D])
    hT = b.sb("hidden_columns", [128, K, PADDED])
    lo = b.sb("low", [P, TILES, E, R])
    lw = b.sb("low_weighted", [P, TILES, E * R])
    lT = b.sb("low_columns", [E * R, NODES])

    with nc.Block() as block:
        @block.sync
        def _(sp):
            for e in range(E):
                sp.dma_start(fc2[:, e * K * D:(e + 1) * K * D].rearrange("p (k n) -> p k n", k=K),
                             t["lora_fc2"][e].rearrange("(k p) n -> p k n", p=128)).then_inc(S["fc2_in"], 16)
            for m in range(TILES):
                sp.wait_ge(S["added"], m + 1)
                sp.dma_start(out[m * P:(m + 1) * P, :], b.X[:, m, :]).then_inc(S["stored"], 16)
            sp.wait_ge(S["stored"], 16 * TILES)

        @block.vector
        def _(dve):
            prenorm_vector(dve, b, S)
            dve.memset(up_wide[:, :, :, :], 0.0).then_inc(S["wide"], 1)
            dve.wait_ge(loaded, loads)
            dve.wait_ge(S["wide"], 1)
            for e in range(E):
                dve.tensor_copy(up_wide[:, e, :, e * R:(e + 1) * R], up[:, e, :, :]).then_inc(S["wide"], 1)
            threshold_gates_vector(dve, b, S, G, E, None, 1.0 / E)
            for e in range(E):
                dve.wait_ge(S["low"], e + 1)
                dve.tensor_copy(lo[:, :, e, :], PS[0:P, 6, 0:TILES * R].rearrange("p (m r) -> p m r", m=TILES)
                                ).then_inc(S["low_out"], 1)
            dve.wait_ge(S["gates"], 1)
            dve.wait_ge(S["low_out"], E)
            for m in range(TILES):
                dve.tensor_tensor(lw[:, m, :].rearrange("p (e r) -> p e r", e=E), lo[:, m, :, :],
                                  spread(G["w"][:, m, :], R), ALU.mult).then_inc(S["weighted"], 1)
            dve.wait_ge(S["fused"], 1)
            dve.tensor_copy(up_fc2[:, :], PS[0:E * R, 7, :]).then_inc(S["fused_out"], 1)
            dve.wait_ge(S["low_turned"], 1)
            dve.tensor_copy(lT[:, 0:4 * P], PS[0:E * R, 0, 0:4 * P]).then_inc(S["low_columns"], 1)
            dve.tensor_copy(lT[:, 4 * P:], PS[0:E * R, 1, 0:P]).then_inc(S["low_columns"], 1)
            for m in range(TILES):
                dve.wait_ge(S["product"], m + 1)
                dve.tensor_tensor(b.X[:, m, :], PS[0:P, 2 + m % 4, :], b.X[:, m, :], ALU.add).then_inc(S["added"], 1)

        @block.scalar
        def _(act):
            prenorm_scalar(act, b, S)
            threshold_gates_scalar(act, b, S, G, E)
            for n in range(E * K):
                e, c = divmod(n, K)
                act.wait_ge(S["hidden"], n + 1)
                if e >= 1 and c == 0:
                    act.wait_ge(S["low"], e)
                act.activation(halves(hT[:, c, :]), PS[:, 2 * (n % 3):2 * (n % 3) + 2, 0:HALF], ACT.Relu
                               ).then_inc(S["hidden_out"], 1)

        @block.tensor
        def _(pe):
            prenorm_tensor(pe, b, S)
            pe.wait_ge(S["pre_columns"], TILES)
            pe.wait_ge(loaded, loads)
            logits_tensor(pe, b, S, gate, E + 1)

            def hidden(e):
                for c in range(K):
                    n = e * K + c
                    if n >= 3:
                        pe.wait_ge(S["hidden_out"], n - 2)
                    for h in range(2):
                        at = e * K * D + c * 128
                        last = accumulate(pe, PS[:, 2 * (n % 3) + h, 0:HALF],
                                          [(W[:, at + k * D:at + k * D + 128], b.XT[:, k, h * HALF:(h + 1) * HALF])
                                           for k in range(K)])
                    last.then_inc(S["hidden"], 1)

            def low(e):
                pe.wait_ge(S["hidden_out"], K * (e + 1))
                if e >= 1:
                    pe.wait_ge(S["low_out"], e)
                for m in range(TILES):
                    last = accumulate(pe, PS[0:P, 6, m * R:(m + 1) * R],
                                      [(tile_of(hT, k, m), down[:, e, k, :]) for k in range(K)])
                last.then_inc(S["low"], 1)

            for e in range(E):
                hidden(e)
                low(e)
            pe.wait_ge(S["fc2_in"], 16 * E)
            pe.wait_ge(S["wide"], E + 1)
            pe.wait_ge(S["gate_shifted"], 1)
            accumulate(pe, PS[0:E * R, 7, :],
                       [(up_wide[:, e, k, :], fc2[:, (e * K + k) * D:(e * K + k + 1) * D])
                        for e in range(E) for k in range(K)]).then_inc(S["fused"], 1)
            pe.wait_ge(S["weighted"], TILES)
            for m in range(TILES):
                last = pe.transpose(PS[0:E * R, m // 4, (m % 4) * P:(m % 4 + 1) * P], lw[:, m, :], b.ident[0:P, 0:P])
            last.then_inc(S["low_turned"], 1)
            pe.wait_ge(S["fused_out"], 1)
            pe.wait_ge(S["low_columns"], 2)
            for m in range(TILES):
                if m >= 4:
                    pe.wait_ge(S["added"], m - 3)
                pe.matmul(PS[0:P, 2 + m % 4, :], lT[:, m * P:(m + 1) * P], up_fc2[:, :], start=True, stop=True
                          ).then_inc(S["product"], 1)



class Buffers:

    def __init__(self, nc):
        self.nc, self.part = nc, "all"
        sb = self.sb

        self.ident = sb("ident", [128, 128])
        self.ones = sb("ones", [128, 128])
        self.X = sb("X", [P, TILES, D])
        self.XN = sb("XN", [P, TILES, D])
        self.XT = sb("XT", [128, K, PADDED])
        self.CT = sb("CT", [P, TILES, PADDED])
        self.W = [sb(f"W{n}", [128, 4 * K * D]) for n in range(2)]
        self.V = [sb(f"V{n}", [128, 8 * D]) for n in range(2)]
        self.U = [sb(f"U{n}", [128, 48]) for n in range(2)]
        self.stats = sb("stats", [P, TILES, 2, 6])
        self.mv = sb("mv", [P, TILES, 2])
        self.var = sb("var", [P, TILES])
        self.root = sb("root", [P, TILES])
        self.rstd = sb("rstd", [P, TILES])
        self.nmr = sb("nmr", [P, TILES])
        self.psum = nc.alloc_psum_tensor("PS", [128, 8, BANK], F32)
        self.mixed_dram = nc.dram_tensor("mixed_dram", [2, 128, STEPS * D], F32).ap()
        self.counts_dram = nc.dram_tensor("counts_dram", [2, P, TILES * PADDED], F32).ap()

    def sb(self, name, shape):
        return self.nc.alloc_sbuf_tensor(f"{self.part}_{name}", shape, F32)


def build(nc, t, out):
    b = Buffers(nc)
    loaders = ([lambda sp, s, d, n=n: load_conv(sp, b, t, s, d, n) for n in range(3)] +
               [lambda sp, s, d: load_experts(sp, b, t, s, d, "L0_ffn_W_exp", "L0_ffn_gate", "L0_ffn_gate_bias",
                                              "L0_ffn_b_exp")] +
               [lambda sp, s, d, n=n: load_attention(sp, b, t, s, d, n) for n in range(2)] +
               [lambda sp, s, d: load_experts(sp, b, t, s, d, "L1_ffn_experts", "L1_ffn_gate", None)] +
               [lambda sp, s, d, n=n: load_relations(sp, b, t, s, d, n) for n in range(2)] +
               [lambda sp, s, d: load_top2(sp, b, t, s, d),
                lambda sp, s, d: load_isomorphism(sp, b, t, s, d),
                lambda sp, s, d: load_lora(sp, b, t, s, d)])
    LOADS = [6, 7, 7, 7, 9, 9, 5, 4, 4, 5, 4, 7]
    numbers = iter(range(1 + len(loaders)))
    loaded = [nc.alloc_semaphore(f"loaded_{n}") for n in range(len(loaders))]
    b.counts_loaded = nc.alloc_semaphore("counts_loaded")
    b.relations_loaded = nc.alloc_semaphore("relations_loaded")

    def load_part(n, sp):
        if n < len(loaders):
            assert loaders[n](sp, n % 2, loaded[n]) == LOADS[n]

    def own(n):
        return n % 2, loaded[n], 16 * LOADS[n], lambda sp: load_part(n + 1, sp)

    def run(part, *args):
        with nc.cleanup_on_exit():
            b.part = f"part{next(numbers)}"
            part(nc, b, t, *args)

    run(count_edges, lambda sp: load_part(0, sp))
    for n in range(3):
        run(conv, n, *own(n))
    with nc.sbuf_tensor("log_counts", [P, TILES, PADDED], F32) as C, nc.sbuf_tensor("edged", [P, TILES], F32) as edged:
        slot, done, loads, load_next = own(3)

        def load_counts(sp, load_next=load_next):
            sp.dma_start(C[:, :, :].rearrange("p m n -> p (m n)"), b.counts_dram[0]).then_inc(b.counts_loaded, 16)
            load_next(sp)
        run(ffn_threshold, slot, done, loads, load_counts)
        for n in range(2):
            run(attention, n, *own(4 + n), C, edged)
    with nc.sbuf_tensor("relation_counts", [P, 2, TILES, PADDED], F32) as C2:
        slot, done, loads, load_next = own(6)

        def load_relation_counts(sp, load_next=load_next):
            for r in range(2):
                sp.dma_start(C2[:, r, :, :].rearrange("p m n -> p (m n)"), b.counts_dram[r]
                             ).then_inc(b.relations_loaded, 16)
            load_next(sp)
        run(ffn_sinkhorn, slot, done, loads, load_relation_counts)
        for n in range(2):
            run(relations, n, *own(7 + n), C2)
    run(ffn_top2, *own(9))
    run(isomorphism, *own(10))
    slot, done, loads, _ = own(11)
    run(ffn_lora, slot, done, loads, out)


def columns(v):
    import numpy as np
    v = np.asarray(v)
    v = v.reshape(len(v), -1)
    return np.ascontiguousarray(v.reshape(-1, 128, v.shape[1]).transpose(1, 0, 2).reshape(128, -1))


def laid_out(x):
    import numpy as np
    x = {n: np.ascontiguousarray(a) for n, a in x.items()}
    t = {n: x[n] for n in (
        "x", "src", "dst", "edge_type_2", "L0_gnn_cw", "L0_gnn_cb", "L0_ffn_W_exp", "L0_ffn_b_exp",
        "L1_gnn_ln_g", "L1_gnn_ln_b", "L1_ffn_experts", "L2_gnn_basis1", "L2_gnn_root1", "L2_gnn_bias1",
        "L2_gnn_basis2", "L2_gnn_root2", "L2_gnn_bias2", "L2_ffn_w2", "L2_ffn_b2", "L2_ffn_gamma", "L2_ffn_beta",
        "L3_gnn_W1", "L3_gnn_W2", "L3_gnn_b2")}
    for i in range(3):
        for n in ("mw1", "mb1", "mw2", "mb2") + (("lng", "lnb") if i else ()):
            t[f"L0_gnn_{n}_{i}"] = x[f"L0_gnn_{n}_{i}"]
        t[f"conv_columns{i}"] = np.concatenate(
            [columns(x[f"L0_gnn_mlg_{i}"]), columns(x[f"L0_gnn_mlb_{i}"]), np.tile(x[f"L0_gnn_t{i}"], (128, 1))], axis=1)
    t["L0_ffn_gate"] = columns(np.concatenate([x["L0_ffn_W_gate"], x["L0_ffn_W_thr"]], axis=1))
    t["L0_ffn_gate_bias"] = np.concatenate([x["L0_ffn_b_gate"], x["L0_ffn_b_thr"]])
    for n in "qkvo":
        t[f"att_W{n}"] = np.ascontiguousarray(x[f"L1_gnn_W{n}"].transpose(0, 2, 1))
    t["att_W1"] = np.ascontiguousarray(x["L1_gnn_W1"].transpose(0, 2, 1))
    t["att_W2"] = np.ascontiguousarray(x["L1_gnn_W2"].transpose(0, 2, 1))
    t["att_columns"] = np.stack([np.concatenate(
        [columns(x[f"L1_gnn_{n}"][i]) for n in ("bq", "bo", "b2", "g1", "beta1", "g2", "beta2")] +
        [np.tile(x["L1_gnn_b1"][i], 2)[:, None]], axis=1) for i in range(2)])
    t["L1_ffn_gate"] = columns(x["L1_ffn_gate_w"][0])
    for i in range(2):
        t[f"rel_columns{i}"] = columns(x[f"L2_gnn_gate_w{i + 1}"][:, :, 0].T)
    t["top2_w1"] = np.ascontiguousarray(x["L2_ffn_w1"].transpose(1, 0, 2).reshape(512, 512))
    t["top2_columns"] = np.concatenate([columns(x["L2_ffn_router_w"]), columns(x["L2_ffn_b1"].reshape(-1))], axis=1)
    t["gin_columns"] = columns(x["L3_gnn_b1"])
    t["lora_gate"] = columns(np.concatenate([x["L3_ffn_gate_w"], x["L3_ffn_thr_w"]]).T)
    t["lora_fc1"] = np.ascontiguousarray(x["L3_ffn_fc1_w"].transpose(0, 2, 1))
    t["lora_fc2"] = np.ascontiguousarray(x["L3_ffn_fc2_w"].transpose(0, 2, 1))
    t["lora_down"] = np.concatenate([columns(a) for a in x["L3_ffn_lora_A"]], axis=1)
    t["lora_up"] = np.concatenate([columns(a.T) for a in x["L3_ffn_lora_B"]], axis=1)
    t["ident"] = np.eye(128, dtype=np.float32)
    t["iota"] = np.tile(np.arange(NODES, dtype=np.float16), (P, 1))
    t["quarter"] = np.tile(np.eye(ROWS4, dtype=np.float32), (BASES, 1))
    t["atts"] = np.stack([np.repeat(x[f"L2_gnn_att{i + 1}"].T, ROWS4, axis=0) for i in range(2)], axis=1)
    return t


def kernel(**inputs):
    import numpy as np
    from concourse import bacc
    from concourse.bass_utils import run_bass_kernel_spmd

    nc = bacc.Bacc("TRN2", target_bir_lowering=False, num_devices=1)
    arrays = {f"in_{n}": np.ascontiguousarray(a) for n, a in laid_out(inputs).items()}
    t = {n[3:]: nc.dram_tensor(n, a.shape, mybir.dt.from_np(a.dtype), kind="ExternalInput").ap()
         for n, a in arrays.items()}
    out = nc.dram_tensor("out", [NODES, D], F32, kind="ExternalOutput").ap()
    build(nc, t, out)
    return run_bass_kernel_spmd(nc, [arrays], core_ids=[0]).results[0]["out"]
```

```python
from contextlib import ExitStack

import concourse.bass as bass
from concourse import mybir
from concourse.alu_op_type import AluOpType as ALU

ACT = mybir.ActivationFunctionType
AX = mybir.AxisListType
F32 = mybir.dt.float32
BF16 = mybir.dt.bfloat16
FP16 = mybir.dt.float16
I32 = mybir.dt.int32

NODES = 625
P = 125
TILES = NODES // P
PADDED = 626
HALF = PADDED // 2
EDGES = 20000
CHUNKS = EDGES // P
D = 512
K = D // 128
D2 = 2 * D
BASES = 30
ROWS4 = 4
MIX = BASES * ROWS4
GROUP = 16
STEPS = D // (ROWS4 * GROUP)
BANK = 512
BIG = 1e30


class Semaphores:

    def __init__(self, nc, part):
        self.nc, self.part, self.known = nc, part, {}

    def __getitem__(self, name):
        if name not in self.known:
            self.known[name] = self.nc.alloc_semaphore(f"{self.part}_{name}")
        return self.known[name]


def accumulate(pe, out, pairs):
    for n, (lhsT, rhs) in enumerate(pairs):
        last = pe.matmul(out, lhsT, rhs, start=(n == 0), stop=(n == len(pairs) - 1))
    return last


def tile_of(columns, k, m):
    return columns[:, k, m * P:(m + 1) * P]


def halves(row):
    return row.rearrange("p (h n) -> p h n", h=2)


def spread(ap, n):
    return ap.unsqueeze(2).to_broadcast([ap.shape[0], ap.shape[1], n])



def count_edges(nc, b, t, load_next):
    S = Semaphores(nc, b.part)
    PS = b.psum
    flat = PS.rearrange("p b n -> p (b n)")
    LAYERS = 2
    RADIX_BITS = 12
    RADIX = 1 << RADIX_BITS
    SLOTS = 4
    ROUNDS = STEPS
    ROUND = CHUNKS // ROUNDS
    assert ROUND * P < RADIX and ROUND * P * RADIX < 1 << 24

    def sb(name, shape, dt=F32):
        return nc.alloc_sbuf_tensor(name, shape, dt)

    ids_i = sb("ids_i", [P, 3, CHUNKS], I32)
    ids = sb("ids", [P, 3, CHUNKS])
    iota = sb("iota", [P, NODES], FP16)
    hot_dst = sb("hot_dst", [P, SLOTS, NODES], BF16)
    hot_src = sb("hot_src", [P, SLOTS, NODES], BF16)
    att = sb("att", [MIX, LAYERS, 2])
    quarter = sb("quarter", [MIX, ROWS4])
    ones = sb("ones16", [MIX, 4, 4])
    mixer = sb("mixer", [MIX, LAYERS, GROUP * 32])
    mixed = sb("mixed", [128, STEPS, D])
    count = sb("count", [P, TILES, PADDED])
    packed = count[:, :, :].rearrange("p m n -> p (m n)")[:, 0:TILES * NODES].bitcast(I32)
    upper = sb("upper", [P, TILES * NODES], I32)
    counts_0, counts_1 = (b.V[n][0:P, 0:TILES * PADDED].rearrange("p (m n) -> p m n", m=TILES) for n in range(2))

    pieces = []
    for m in range(TILES):
        at = m * NODES
        while at < (m + 1) * NODES:
            end = min((m + 1) * NODES, (at // BANK + 1) * BANK)
            pieces.append((m, at, end))
            at = end
    count_banks = -(-TILES * NODES // BANK)
    opens = {min(n for n, p in enumerate(pieces) if p[1] // BANK == k) for k in range(count_banks)}
    closes = {max(n for n, p in enumerate(pieces) if p[1] // BANK == k) for k in range(count_banks)}
    SPLIT = 3 * BANK

    with nc.Block() as block:
        @block.sync
        def _(sp):
            for n, name in enumerate(("src", "dst", "edge_type_2")):
                sp.dma_start(ids_i[:, n, :], t[name].rearrange("(p c) -> p c", p=P)).then_inc(S["ids_in"], 16)
            sp.dma_start(iota[:, :], t["iota"]).then_inc(S["ids_in"], 16)
            sp.dma_start(quarter[:, :], t["quarter"]).then_inc(S["att_in"], 16)
            sp.dma_start(att[:, :, :], t["atts"]).then_inc(S["att_in"], 16)
            for layer in range(LAYERS):
                rows = t[f"L2_gnn_basis{layer + 1}"].rearrange("b (t q j) o -> t b q (j o)", t=STEPS, q=ROWS4)
                with sp.Fori(0, STEPS // 2) as i:
                    for h in range(2):
                        sp.wait_ge(S["mixed_full"], STEPS * layer + 2 * i + h + 1)
                        sp.dma_start(b.W[h][0:MIX, :], rows[bass.ds(2 * i + h, 1)].rearrange("a b q n -> (a b) q n")
                                     ).then_inc(S[f"basis_in{h}"], 16)
            sp.dma_start(b.ident[:, :], t["ident"]).then_inc(S["ident_in"], 16)
            sp.dma_start(b.X[:, :, :], t["x"].rearrange("(m p) f -> p m f", p=P)).then_inc(S["ident_in"], 16)
            sp.wait_ge(S["mixed_full"], 2 + LAYERS * STEPS)
            sp.wait_ge(S["stored"], 16 * 5)
            load_next(sp)
            sp.wait_ge(S["ident_in"], 32)

        @block.gpsimd
        def _(pool):
            pool.memset(counts_0[:, :, :], 0.0).then_inc(S["no_counts"], 1)
            pool.memset(counts_1[:, :, :], 0.0).then_inc(S["no_counts"], 1)
            pool.wait_ge(S["no_counts"], 2)

            def add(total, part, done):
                total = total[:, :, 0:NODES]
                pool.tensor_tensor(total, total, part.bitcast(F32).rearrange("p (m n) -> p m n", m=TILES), ALU.add
                                   ).then_inc(done, 1)

            for layer in range(LAYERS):
                with pool.Fori(0, ROUNDS // 2) as i:
                    n = ROUNDS // 2 * layer + i
                    pool.wait_ge(S["upper_cast"], n + 1)
                    add(counts_1, upper[:, :], S["added"])
                    pool.wait_ge(S["lower_cast"], n + 1)
                    add(counts_0, packed, S["added"])
                pool.wait_ge(S["mixed_out"], 1 + STEPS * (layer + 1))
                pool.dma_start(b.mixed_dram[layer].rearrange("(rq cj) n -> cj rq n", rq=2 * ROWS4),
                               mixed[:, :, :].rearrange("p a n -> p (a n)")).then_inc(S["stored"], 16)
                if layer == 0:
                    pool.wait_ge(S["stored"], 16)
                    pool.sem_inc(S["mixed_free"], 1)
            pool.wait_ge(S["added"], 1 + 2 * ROUNDS)
            for n, c in enumerate((counts_0, counts_1)):
                pool.dma_start(b.counts_dram[1 + n], c.rearrange("p m n -> p (m n)")).then_inc(S["stored"], 16)
            pool.wait_ge(S["counted"], 1)
            pool.wait_ge(S["blank"], 6)
            pool.dma_start(b.counts_dram[0], count[:, :, :].rearrange("p m n -> p (m n)")).then_inc(S["stored"], 16)
            pool.wait_ge(S["stored"], 16 * 5)

        @block.vector
        def _(dve):
            dve.memset(mixer[:, :, :], 0.0).then_inc(S["blank"], 1)
            dve.memset(ones[:, :, :], 1.0).then_inc(S["blank"], 1)
            dve.wait_ge(S["ids_in"], 64)
            dve.tensor_copy(ids[:, 0:2, :], ids_i[:, 0:2, :]).then_inc(S["ids_cast"], 1)
            dve.tensor_scalar(ids[:, 2, :], ids_i[:, 2, :], 0.0, float(RADIX - 1), ALU.not_equal, ALU.mult
                              ).then_inc(S["ids_cast"], 1)
            dve.wait_ge(S["ids_cast"], 2)
            dve.tensor_scalar(ids[:, 2, :], ids[:, 2, :], 1.0, None, ALU.add).then_inc(S["ids_cast"], 1)
            dve.wait_ge(S["att_in"], 32)
            dve.wait_ge(S["blank"], 2)
            for layer in range(LAYERS):
                for r in range(2):
                    for q in range(ROWS4):
                        first = ROWS4 * r + q
                        by_tile = mixer[:, layer, :].rearrange("p (c n) -> p c n", c=4)
                        dve.tensor_scalar(by_tile[:, :, first:first + 3 * 40 + 1:40], ones[:, :, :],
                                          quarter[:, q:q + 1], att[:, layer, r:r + 1], ALU.mult, ALU.mult
                                          ).then_inc(S["mixer_made"], 1)
            dve.wait_ge(S["ids_cast"], 3)
            for layer in range(LAYERS):
                with dve.Fori(0, ROUNDS // 2) as i:
                    n = ROUNDS // 2 * layer + i
                    for j in range(ROUND):
                        c = ROUND * n + j
                        slot = j % SLOTS
                        dve.wait_ge(S["hot_free"], c + 1)
                        dve.tensor_scalar(hot_dst[:, slot, :], iota[:, :], ids[:, 1, bass.ds(c, 1)], None,
                                          ALU.is_equal).then_inc(S["hot_ready"], 1)
                        dve.tensor_scalar(hot_src[:, slot, :], iota[:, :], ids[:, 0, bass.ds(c, 1)],
                                          ids[:, 2, bass.ds(c, 1)], ALU.is_equal, ALU.mult).then_inc(S["hot_ready"], 1)
                    dve.wait_ge(S["hot_free"], SLOTS + ROUND * (n + 1))
                    dve.wait_ge(S["added"], 1 + 2 * n)
                    dve.tensor_copy(packed[:, 0:SPLIT], flat[0:P, 0:SPLIT]).then_inc(S["unpacked"], 1)
                    dve.wait_ge(S["unpacked"], 2 + 2 * (n + 1))
                    dve.tensor_scalar(upper[:, :], packed, RADIX_BITS, None, ALU.logical_shift_right
                                      ).then_inc(S["upper"], 1)
                    dve.wait_ge(S["upper"], n + 1)
                    dve.tensor_scalar(packed, packed, RADIX - 1, None, ALU.bitwise_and
                                      ).then_inc(S["lower"], 1)
            dve.memset(b.CT[:, :, NODES:], 0.0).then_inc(S["blank"], 1)
            dve.memset(b.XT[:, :, NODES:], 0.0).then_inc(S["blank"], 1)
            dve.memset(b.ones[:, :], 1.0).then_inc(S["blank"], 1)
            dve.wait_ge(S["added"], 1 + 2 * ROUNDS)
            dve.memset(count[:, :, NODES:], 0.0).then_inc(S["blank"], 1)
            dve.tensor_tensor(count[:, :, 0:NODES], counts_0[:, :, 0:NODES], counts_1[:, :, 0:NODES], ALU.add
                              ).then_inc(S["counted"], 1)
            for s in range(TILES):
                dve.wait_ge(S["turned"], s + 1)
                dve.tensor_copy(b.CT[:, s, 0:4 * P], PS[0:P, s, 0:4 * P]).then_inc(S["ct_out"], 1)
            dve.wait_ge(S["turned"], 2 * TILES)
            dve.tensor_copy(b.CT[:, 0:4, 4 * P:5 * P], PS[0:P, TILES, 0:4 * P].rearrange("p (s n) -> p s n", s=4)
                            ).then_inc(S["ct_out"], 1)
            dve.tensor_copy(b.CT[:, 4, 4 * P:5 * P], PS[0:P, TILES + 1, 0:P]).then_inc(S["ct_out"], 1)

        @block.scalar
        def _(act):
            for layer in range(LAYERS):
                if layer == 1:
                    act.wait_ge(S["mixed_free"], 1)
                with act.Fori(0, ROUNDS // 2) as i:
                    n = ROUNDS // 2 * layer + i
                    act.wait_ge(S["hot_free"], SLOTS + ROUND * (n + 1))
                    act.wait_ge(S["added"], 1 + 2 * n)
                    act.activation(packed[:, SPLIT:], flat[0:P, SPLIT:TILES * NODES], ACT.Copy).then_inc(S["unpacked"], 1)
                    for h in range(2):
                        step = 2 * i + h
                        act.wait_ge(S["mixed_full"], 2 + STEPS * layer + step + 1)
                        act.activation(mixed[:, bass.ds(step, 1), :], PS[:, count_banks:count_banks + 1, :], ACT.Copy
                                       ).then_inc(S["mixed_out"], 1)
                    act.wait_ge(S["upper"], n + 1)
                    act.wait_ge(S["lower"], n + 1)
                    act.activation(upper[:, :].bitcast(F32), upper[:, :], ACT.Copy).then_inc(S["upper_cast"], 1)
                    act.activation(packed.bitcast(F32), packed, ACT.Copy).then_inc(S["lower_cast"], 1)

        @block.tensor
        def _(pe):
            pe.sem_inc(S["hot_free"], SLOTS)
            pe.sem_inc(S["mixed_full"], 2)
            pe.sem_inc(S["mixed_out"], 1)
            pe.sem_inc(S["added"], 1)
            pe.sem_inc(S["unpacked"], 2)
            pe.wait_ge(S["mixer_made"], LAYERS * 2 * ROWS4)
            for layer in range(LAYERS):
                with pe.Fori(0, ROUNDS // 2) as i:
                    n = ROUNDS // 2 * layer + i
                    pe.wait_ge(S["unpacked"], 2 + 2 * n)
                    for j in range(ROUND):
                        slot = j % SLOTS
                        pe.wait_ge(S["hot_ready"], 2 * (ROUND * n + j + 1))
                        for at_piece, (m, at, end) in enumerate(pieces):
                            last = pe.matmul(flat[0:P, at:end], hot_dst[:, slot, m * P:(m + 1) * P],
                                             hot_src[:, slot, at - m * NODES:end - m * NODES],
                                             start=(j == 0 and at_piece in opens),
                                             stop=(j == ROUND - 1 and at_piece in closes), skip_group_check=True)
                        last.then_inc(S["hot_free"], 1)
                    for h in range(2):
                        step = 2 * i + h
                        pe.wait_ge(S[f"basis_in{h}"], 16 * (STEPS // 2 * layer + i + 1))
                        pe.wait_ge(S["mixed_out"], 1 + STEPS * layer + step)
                        for jj in range(4):
                            for c in range(4):
                                g = 4 * c + jj
                                last = pe.matmul(PS[32 * c:32 * c + 32, count_banks, :], mixer[:, layer, g * 32:(g + 1) * 32],
                                                 b.W[h][0:MIX, g * D:(g + 1) * D], start=(jj == 0), stop=(jj == 3))
                        last.then_inc(S["mixed_full"], 1)
            pe.wait_ge(S["ident_in"], 32)
            pe.wait_ge(S["counted"], 1)
            for s in range(TILES):
                for d in range(4):
                    last = pe.transpose(PS[0:P, s, d * P:(d + 1) * P], count[:, d, s * P:(s + 1) * P], b.ident[0:P, 0:P])
                last.then_inc(S["turned"], 1)
            for s in range(TILES):
                pe.transpose(PS[0:P, TILES + s // 4, (s % 4) * P:(s % 4 + 1) * P], count[:, 4, s * P:(s + 1) * P],
                             b.ident[0:P, 0:P]).then_inc(S["turned"], 1)



def prenorm_vector(dve, b, S):
    row_stats(dve, b, S, "pre", [[b.X[:, m, :]] for m in range(TILES)])
    for m in range(TILES):
        dve.tensor_scalar(b.XN[:, m, :], b.X[:, m, :], b.mv[:, m, 0:1], b.rstd[:, m:m + 1], ALU.subtract, ALU.mult
                          ).then_inc(S["pre_rows"], 1)


def prenorm_tensor(pe, b, S):
    for m in range(TILES):
        pe.wait_ge(S["pre_rows"], m + 1)
        for k in range(K):
            last = pe.transpose(b.psum[:, m, k * P:(k + 1) * P], b.XN[:, m, k * 128:(k + 1) * 128], b.ident[0:P, 0:P])
        last.then_inc(S["pre_turned"], 1)


def prenorm_scalar(act, b, S):
    row_root(act, b, S, "pre")
    for m in range(TILES):
        act.wait_ge(S["pre_turned"], m + 1)
        act.activation(b.XT[:, :, m * P:(m + 1) * P], b.psum[:, m, 0:K * P].rearrange("p (k n) -> p k n", k=K), ACT.Copy
                       ).then_inc(S["pre_columns"], 1)


def row_stats(dve, b, S, tag, views):
    n = len(views[0])
    for m in range(TILES):
        for h in range(n):
            dve.bn_stats(b.stats[:, m, h, :], views[m][h]).then_inc(S[tag + "_stats"], 1)
    dve.wait_ge(S[tag + "_stats"], n * TILES)
    for m in range(TILES):
        dve.bn_aggr(b.mv[:, m, :], b.stats[:, m, 0:n, :].rearrange("p h s -> p (h s)")).then_inc(S[tag + "_aggr"], 1)
    dve.wait_ge(S[tag + "_aggr"], TILES)
    dve.tensor_scalar(b.var[:, :], b.mv[:, :, 1], 1e-5, None, ALU.add).then_inc(S[tag + "_var"], 1)
    dve.wait_ge(S[tag + "_root"], 1)
    dve.reciprocal(b.rstd[:, :], b.root[:, :]).then_inc(S[tag + "_rstd"], 1)
    dve.wait_ge(S[tag + "_rstd"], 1)


def row_root(act, b, S, tag):
    act.wait_ge(S[tag + "_var"], 1)
    act.activation(b.root[:, :], b.var[:, :], ACT.Sqrt).then_inc(S[tag + "_root"], 1)


def column_vectors(b, slot, names):
    out, at = {}, 0
    for name, n in names:
        out[name] = b.U[slot][:, at:at + n]
        at += n
    return out



def load_conv(sp, b, t, slot, done, layer):
    W, V = b.W[slot], b.V[slot]
    sp.dma_start(W[:, 0:K * D2].rearrange("p (k n) -> p k n", k=K),
                 t[f"L0_gnn_mw1_{layer}"].rearrange("(k p) n -> p k n", p=128)).then_inc(done, 16)
    sp.dma_start(W[:, K * D2:].rearrange("p (k n) -> p k n", k=2 * K),
                 t[f"L0_gnn_mw2_{layer}"].rearrange("(k p) n -> p k n", p=128)).then_inc(done, 16)
    sp.dma_start(b.U[slot][:, 0:17], t[f"conv_columns{layer}"]).then_inc(done, 16)
    rows = [(f"L0_gnn_mb1_{layer}", 0), (f"L0_gnn_mb2_{layer}", D2)]
    rows += [("L0_gnn_cb", D2 + D)] if layer == 0 else [(f"L0_gnn_lng_{layer}", D2 + D), (f"L0_gnn_lnb_{layer}", D2 + 2 * D)]
    for name, at in rows:
        sp.dma_start(V[:, at:at + t[name].shape[0]], t[name].partition_broadcast(128)).then_inc(done, 16)
    return 3 + len(rows)


def load_experts(sp, b, t, slot, done, weights, columns, rows, bias=None):
    for e in range(4):
        sp.dma_start(b.W[slot][:, e * K * D:(e + 1) * K * D].rearrange("p (k n) -> p k n", k=K),
                     t[weights][e].rearrange("(k p) n -> p k n", p=128)).then_inc(done, 16)
    sp.dma_start(b.U[slot][:, 0:t[columns].shape[1]], t[columns]).then_inc(done, 16)
    n = 5
    if rows:
        sp.dma_start(b.V[slot][:, 0:t[rows].shape[0]], t[rows].partition_broadcast(128)).then_inc(done, 16)
        n += 1
    if bias:
        sp.dma_start(b.V[slot][0:8, D:2 * D], t[bias]).then_inc(done, 16)
        n += 1
    return n


def load_attention(sp, b, t, slot, done, layer):
    W, V = b.W[slot], b.V[slot]
    for n, name in enumerate(("q", "k", "v", "o")):
        sp.dma_start(W[:, n * K * D:(n + 1) * K * D].rearrange("p (k n) -> p k n", k=K),
                     t[f"att_W{name}"][layer].rearrange("(k p) n -> p k n", p=128)).then_inc(done, 16)
    sp.dma_start(V[:, 0:256].rearrange("p (k n) -> p k n", k=K),
                 t["att_W1"][layer].rearrange("(k p) n -> p k n", p=128)).then_inc(done, 16)
    sp.dma_start(V[0:64, 256:768], t["att_W2"][layer]).then_inc(done, 16)
    sp.dma_start(b.U[slot][:, 0:29], t["att_columns"][layer]).then_inc(done, 16)
    for name, at in (("L1_gnn_ln_g", 1024), ("L1_gnn_ln_b", 1536)):
        sp.dma_start(V[:, at:at + D], t[name].partition_broadcast(128)).then_inc(done, 16)
    return 9


def load_relations(sp, b, t, slot, done, layer):
    W = b.W[slot]
    sp.dma_start(W[:, 0:STEPS * D], b.mixed_dram[layer]).then_inc(done, 16)
    sp.dma_start(W[:, STEPS * D:STEPS * D + K * D].rearrange("p (k n) -> p k n", k=K),
                 t[f"L2_gnn_root{layer + 1}"].rearrange("(k p) n -> p k n", p=128)).then_inc(done, 16)
    sp.dma_start(b.U[slot][:, 0:2 * K], t[f"rel_columns{layer}"]).then_inc(done, 16)
    sp.dma_start(b.V[slot][:, 0:D], t[f"L2_gnn_bias{layer + 1}"].partition_broadcast(128)).then_inc(done, 16)
    return 4


def load_top2(sp, b, t, slot, done):
    W = b.W[slot]
    sp.dma_start(W[:, 0:K * D].rearrange("p (k n) -> p k n", k=K),
                 t["top2_w1"].rearrange("(k p) n -> p k n", p=128)).then_inc(done, 16)
    sp.dma_start(W[:, K * D:2 * K * D].rearrange("p (k n) -> p k n", k=K),
                 t["L2_ffn_w2"].rearrange("(a c) f o -> (c f) a o", c=2)).then_inc(done, 16)
    sp.dma_start(W[:, 2 * K * D:4 * K * D], t["L2_ffn_b2"].rearrange("e n -> (e n)").partition_broadcast(128)
                 ).then_inc(done, 16)
    sp.dma_start(b.V[slot][:, :], t["L2_ffn_gamma"].rearrange("e n -> (e n)").partition_broadcast(128)
                 ).then_inc(done, 16)
    sp.dma_start(b.U[slot][:, 0:9 * K], t["top2_columns"]).then_inc(done, 16)
    return 5


def load_isomorphism(sp, b, t, slot, done):
    for n in range(2):
        sp.dma_start(b.W[slot][:, n * K * D:(n + 1) * K * D].rearrange("p (k n) -> p k n", k=K),
                     t[f"L3_gnn_W{n + 1}"].rearrange("(k p) n -> p k n", p=128)).then_inc(done, 16)
    sp.dma_start(b.U[slot][:, 0:K], t["gin_columns"]).then_inc(done, 16)
    sp.dma_start(b.V[slot][:, 0:D], t["L3_gnn_b2"].partition_broadcast(128)).then_inc(done, 16)
    return 4


def load_lora(sp, b, t, slot, done):
    for e in range(4):
        sp.dma_start(b.W[slot][:, e * K * D:(e + 1) * K * D].rearrange("p (k n) -> p k n", k=K),
                     t["lora_fc1"][e].rearrange("(k p) n -> p k n", p=128)).then_inc(done, 16)
    sp.dma_start(b.U[slot][:, 0:5 * K], t["lora_gate"]).then_inc(done, 16)
    sp.dma_start(b.V[slot][:, 0:256], t["lora_down"]).then_inc(done, 16)
    sp.dma_start(b.V[slot][:, 256:512], t["lora_up"]).then_inc(done, 16)
    return 7



def conv(nc, b, t, layer, slot, loaded, loads, load_next):
    S = Semaphores(nc, b.part)
    PS = b.psum
    W, V = b.W[slot], b.V[slot]
    w1 = W[:, 0:K * D2].rearrange("p (k n) -> p k n", k=K)
    w2 = W[:, K * D2:].rearrange("p (k n) -> p k n", k=2 * K)
    b1, b2 = V[0:P, 0:D2], V[0:P, D2:D2 + D]
    cb = lng = V[0:P, D2 + D:D2 + 2 * D]
    lnb = V[0:P, D2 + 2 * D:D2 + 3 * D]
    cols = column_vectors(b, slot, [("g", 2 * K), ("b", 2 * K), ("t", 1)])
    temperature = cols["t"][0:P, :]

    M = b.sb("messages", [P, TILES, D])
    EE = b.sb("weights_and_weighted", [P, TILES, D2])
    hT = b.sb("h_columns", [128, K, PADDED])
    H2T = b.sb("hidden_columns", [128, 2 * K, NODES])
    den = V[:, 6 * D:6 * D + PADDED]
    cw = b.sb("cw", [128, K, D])
    ext = b.sb("extremes", [P, 8])
    H1 = EE

    with nc.Block() as block:
        @block.sync
        def _(sp):
            sp.dma_start(cw[:, :, :], t["L0_gnn_cw"][layer * D:(layer + 1) * D, :].rearrange("(k p) n -> p k n", p=128)
                         ).then_inc(S["cw_in"], 16)
            load_next(sp)

        @block.vector
        def _(dve):
            if layer == 0:
                prenorm_vector(dve, b, S)
                dve.wait_ge(S["pre_rows"], TILES)
            dve.tensor_scalar(M[:, :, :], b.XN[:, :, :], 0.0, 1e-7, ALU.max, ALU.add).then_inc(S["messages"], 1)
            dve.wait_ge(S["messages"], 1)
            dve.tensor_reduce(ext[:, 0:1], M[:, :, :], AX.XY, ALU.max).then_inc(S["ext"], 1)
            dve.tensor_reduce(ext[:, 1:2], M[:, :, :], AX.XY, ALU.min).then_inc(S["ext"], 1)
            dve.wait_ge(loaded, loads)
            dve.wait_ge(S["ext"], 2)
            dve.tensor_scalar(ext[:, 2:4], ext[:, 0:2], temperature, None, ALU.mult).then_inc(S["ext"], 1)
            dve.wait_ge(S["ext"], 3)
            dve.tensor_tensor(ext[:, 4:5], ext[:, 2:3], ext[:, 3:4], ALU.max).then_inc(S["ext_tile"], 1)
            dve.wait_ge(S["ext_turned"], 1)
            dve.tensor_reduce(ext[0:1, 5:6], PS[0:1, 7, 0:P], AX.X, ALU.max).then_inc(S["ext_all"], 1)
            dve.wait_ge(S["ext_everywhere"], 1)
            dve.tensor_scalar(ext[:, 6:7], PS[0:P, 7, 256:257], -1.0, None, ALU.mult).then_inc(S["shift"], 1)
            for m in range(TILES):
                dve.wait_ge(S["weights"], m + 1)
                dve.tensor_tensor(EE[:, m, D:], EE[:, m, 0:D], M[:, m, :], ALU.mult).then_inc(S["weighted"], 1)
            if layer == 0:
                dve.wait_ge(S["pre_columns"], TILES)
            for c in range(K):
                bank = 4 * (c % 2)
                dve.wait_ge(S["aggregated"], c + 1)
                dve.tensor_scalar(halves(den), PS[:, bank:bank + 2, 0:HALF], 1e-37, None, ALU.max
                                  ).then_inc(S["den"], 1)
                dve.wait_ge(S["den"], 2 * c + 1)
                dve.reciprocal(den, den).then_inc(S["den"], 1)
                dve.wait_ge(S["den"], 2 * c + 2)
                dve.tensor_tensor(halves(hT[:, c, :]), PS[:, bank + 2:bank + 4, 0:HALF], halves(den), ALU.mult
                                  ).then_inc(S["agg"], 1)
                dve.wait_ge(S["agg"], c + 1)
                dve.tensor_tensor(hT[:, c, :], hT[:, c, :], b.XT[:, c, :], ALU.add).then_inc(S["h"], 1)
            for m in range(TILES):
                dve.wait_ge(S["up"], m + 1)
                bank = 2 * (m % 4)
                dve.tensor_tensor(H1[:, m, :].rearrange("p (a n) -> p a n", a=2), PS[0:P, bank:bank + 2, :],
                                  b1.rearrange("p (a n) -> p a n", a=2), ALU.add).then_inc(S["up_out"], 1)
            dve.wait_ge(S["up_out"], TILES)
            row_stats(dve, b, S, "mid", [[H1[:, m, 0:D], H1[:, m, D:]] for m in range(TILES)])
            dve.scalar_tensor_tensor(b.nmr[:, :], b.mv[:, :, 0], -1.0, b.rstd[:, :], ALU.mult, ALU.mult
                                     ).then_inc(S["mid_nmr"], 1)
            if layer == 0:
                for m in range(TILES):
                    dve.wait_ge(S["down"], m + 1)
                    dve.tensor_tensor(b.XN[:, m, :], PS[0:P, m, :], b2, ALU.add).then_inc(S["x_rows"], 1)
            else:
                G = [H1[:, m, 0:D] for m in range(TILES)]
                for m in range(TILES):
                    dve.wait_ge(S["down"], m + 1)
                    dve.tensor_tensor(G[m], PS[0:P, m, :], b2, ALU.add).then_inc(S["down_out"], 1)
                dve.wait_ge(S["down_out"], TILES)
                row_stats(dve, b, S, "out", [[g] for g in G])
                for m in range(TILES):
                    dve.tensor_scalar(G[m], G[m], b.mv[:, m, 0:1], b.rstd[:, m:m + 1], ALU.subtract, ALU.mult
                                      ).then_inc(S["out_norm"], 1)
                for m in range(TILES):
                    dve.wait_ge(S["out_norm"], m + 1)
                    dve.tensor_tensor(G[m], G[m], lng, ALU.mult).then_inc(S["out_gain"], 1)
                for m in range(TILES):
                    dve.wait_ge(S["out_gain"], m + 1)
                    dve.tensor_tensor(G[m], G[m], lnb, ALU.add).then_inc(S["out_shift"], 1)
                for m in range(TILES):
                    dve.wait_ge(S["out_shift"], m + 1)
                    dve.scalar_tensor_tensor(b.XN[:, m, :], G[m], 0.0, b.XN[:, m, :], ALU.max, ALU.add
                                             ).then_inc(S["x_rows"], 1)
            if layer == 0:
                for m in range(TILES):
                    dve.tensor_tensor(b.X[:, m, :], b.X[:, m, :], cb, ALU.add).then_inc(S["cb"], 1)
                dve.wait_ge(S["cb"], TILES)
            for m in range(TILES):
                dve.wait_ge(S["share"], m + 1)
                dve.tensor_tensor(b.X[:, m, :], PS[0:P, 5 + m % 3, :], b.X[:, m, :], ALU.add).then_inc(S["share_out"], 1)

        @block.scalar
        def _(act):
            if layer == 0:
                prenorm_scalar(act, b, S)
            act.wait_ge(S["shift"], 1)
            act.wait_ge(loaded, loads)
            for m in range(TILES):
                act.activation(EE[:, m, 0:D], M[:, m, :], ACT.Exp, bias=ext[:, 6:7], scale=temperature
                               ).then_inc(S["weights"], 1)
            row_root(act, b, S, "mid")
            act.wait_ge(S["mid_nmr"], 1)
            for m in range(TILES):
                act.activation(H1[:, m, :], H1[:, m, :], ACT.Identity, bias=b.nmr[:, m:m + 1], scale=b.rstd[:, m:m + 1]
                               ).then_inc(S["mid_norm"], 1)
            for k in range(2 * K):
                bank = 2 * (k % 4)
                act.wait_ge(S["mid_turned"], k + 1)
                act.activation(H2T[:, k, 0:4 * P], PS[:, bank, 0:4 * P], ACT.Relu, bias=cols["b"][:, k:k + 1],
                               scale=cols["g"][:, k:k + 1]).then_inc(S["hidden"], 1)
                act.activation(H2T[:, k, 4 * P:], PS[:, bank + 1, 0:P], ACT.Relu, bias=cols["b"][:, k:k + 1],
                               scale=cols["g"][:, k:k + 1]).then_inc(S["hidden"], 1)
            if layer > 0:
                row_root(act, b, S, "out")
            for m in range(TILES):
                act.wait_ge(S["x_turned"], m + 1)
                act.activation(b.XT[:, :, m * P:(m + 1) * P], PS[:, m, 0:K * P].rearrange("p (k n) -> p k n", k=K),
                               ACT.Copy).then_inc(S["x_columns"], 1)

        @block.tensor
        def _(pe):
            if layer == 0:
                prenorm_tensor(pe, b, S)
            pe.wait_ge(S["ext_tile"], 1)
            pe.transpose(PS[0:1, 7, 0:P], ext[:, 4:5], b.ident[0:P, 0:P]).then_inc(S["ext_turned"], 1)
            pe.wait_ge(S["ext_all"], 1)
            pe.matmul(PS[0:P, 7, 256:257], b.ones[0:1, 0:P], ext[0:1, 5:6], start=True, stop=True
                      ).then_inc(S["ext_everywhere"], 1)
            if layer == 0:
                pe.wait_ge(S["pre_columns"], TILES)
            pe.wait_ge(S["weighted"], TILES)
            for c in range(K):
                if c >= 2:
                    pe.wait_ge(S["h"], c - 1)
                for part in range(2):
                    at = part * D + c * 128
                    for h in range(2):
                        last = accumulate(pe, PS[:, 4 * (c % 2) + 2 * part + h, 0:HALF],
                                          [(EE[:, s, at:at + 128], b.CT[:, s, h * HALF:(h + 1) * HALF])
                                           for s in range(TILES)])
                last.then_inc(S["aggregated"], 1)
            pe.wait_ge(S["h"], K)
            pe.wait_ge(loaded, loads)
            for m in range(TILES):
                if m >= 4:
                    pe.wait_ge(S["up_out"], m - 3)
                for h in range(2):
                    last = accumulate(pe, PS[0:P, 2 * (m % 4) + h, :],
                                      [(tile_of(hT, k, m), w1[:, k, h * D:(h + 1) * D]) for k in range(K)])
                last.then_inc(S["up"], 1)
            pe.wait_ge(S["mid_norm"], TILES)
            for k in range(2 * K):
                if k >= 4:
                    pe.wait_ge(S["hidden"], 2 * (k - 3))
                for m in range(TILES):
                    last = pe.transpose(PS[:, 2 * (k % 4) + m // 4, (m % 4) * P:(m % 4 + 1) * P],
                                        H1[:, m, k * 128:(k + 1) * 128], b.ident[0:P, 0:P])
                last.then_inc(S["mid_turned"], 1)
            pe.wait_ge(S["hidden"], 4 * K)
            for m in range(TILES):
                accumulate(pe, PS[0:P, m, :], [(tile_of(H2T, k, m), w2[:, k, :]) for k in range(2 * K)]
                           ).then_inc(S["down"], 1)
            for m in range(TILES):
                pe.wait_ge(S["x_rows"], m + 1)
                for k in range(K):
                    last = pe.transpose(PS[:, m, k * P:(k + 1) * P], b.XN[:, m, k * 128:(k + 1) * 128], b.ident[0:P, 0:P])
                last.then_inc(S["x_turned"], 1)
            pe.wait_ge(S["cw_in"], 16)
            for m in range(TILES):
                pe.wait_ge(S["x_columns"], m + 1)
                if m >= 3:
                    pe.wait_ge(S["share_out"], m - 2)
                accumulate(pe, PS[0:P, 5 + m % 3, :], [(tile_of(b.XT, k, m), cw[:, k, :]) for k in range(K)]
                           ).then_inc(S["share"], 1)



def threshold_gates_vector(dve, b, S, G, E, bias, cap):
    lg = G["lg"]
    dve.wait_ge(S["logits"], 1)
    logits = b.psum[0:P, 7, 0:TILES * (E + 1)].rearrange("p (m e) -> p m e", m=TILES)
    if bias is not None:
        dve.tensor_tensor(lg[:, :, :], logits, bias.unsqueeze(1).to_broadcast([P, TILES, E + 1]), ALU.add
                          ).then_inc(S["gate"], 1)
    else:
        dve.tensor_copy(lg[:, :, :], logits).then_inc(S["gate"], 1)
    dve.wait_ge(S["gate"], 1)
    dve.tensor_reduce(G["s"][:, :], lg[:, :, 0:E], AX.X, ALU.max).then_inc(S["gate"], 1)
    dve.wait_ge(S["gate"], 2)
    dve.tensor_tensor(lg[:, :, 0:E], lg[:, :, 0:E], spread(G["s"][:, :], E), ALU.subtract).then_inc(S["gate_shifted"], 1)
    dve.wait_ge(S["gate_exp"], 2)
    dve.tensor_reduce(G["s"][:, :], G["w"][:, :, :], AX.X, ALU.add).then_inc(S["gate"], 1)
    dve.tensor_scalar(G["t"][:, :], G["t"][:, :], 1.0, None, ALU.add).then_inc(S["gate"], 1)
    dve.wait_ge(S["gate"], 4)
    dve.reciprocal(G["s"][:, :], G["s"][:, :]).then_inc(S["gate"], 1)
    dve.reciprocal(G["t"][:, :], G["t"][:, :]).then_inc(S["gate"], 1)
    dve.wait_ge(S["gate"], 6)
    dve.tensor_tensor(G["w"][:, :, :], G["w"][:, :, :], spread(G["s"][:, :], E), ALU.mult).then_inc(S["gate"], 1)
    dve.tensor_scalar(G["t"][:, :], G["t"][:, :], cap, None, ALU.mult).then_inc(S["gate"], 1)
    dve.wait_ge(S["gate"], 8)
    dve.tensor_tensor(G["w"][:, :, :], G["w"][:, :, :], spread(G["t"][:, :], E), ALU.subtract).then_inc(S["gate"], 1)
    dve.wait_ge(S["gate"], 9)
    dve.tensor_scalar(G["w"][:, :, :], G["w"][:, :, :], 0.0, None, ALU.max).then_inc(S["gate"], 1)
    dve.wait_ge(S["gate"], 10)
    dve.tensor_reduce(G["s"][:, :], G["w"][:, :, :], AX.X, ALU.add).then_inc(S["gate"], 1)
    dve.wait_ge(S["gate"], 11)
    dve.scalar_tensor_tensor(G["t"][:, :], G["s"][:, :], 0.0, G["s"][:, :], ALU.is_equal, ALU.add).then_inc(S["gate"], 1)
    dve.wait_ge(S["gate"], 12)
    dve.reciprocal(G["t"][:, :], G["t"][:, :]).then_inc(S["gate"], 1)
    dve.wait_ge(S["gate"], 13)
    dve.tensor_tensor(G["w"][:, :, :], G["w"][:, :, :], spread(G["t"][:, :], E), ALU.mult).then_inc(S["gates"], 1)


def threshold_gates_scalar(act, b, S, G, E):
    act.wait_ge(S["gate_shifted"], 1)
    act.activation(G["w"][:, :, :], G["lg"][:, :, 0:E], ACT.Exp).then_inc(S["gate_exp"], 1)
    act.activation(G["t"][:, :], G["lg"][:, :, E], ACT.Exp, scale=-1.0).then_inc(S["gate_exp"], 1)


def logits_tensor(pe, b, S, weights, n):
    for m in range(TILES):
        last = accumulate(pe, b.psum[0:P, 7, m * n:(m + 1) * n],
                          [(tile_of(b.XT, k, m), weights[:, k, :]) for k in range(K)])
    last.then_inc(S["logits"], 1)


def gate_buffers(b, E):
    return {"lg": b.sb("gate_logits", [P, TILES, E + 1]),
            "w": b.sb("gate_weights", [P, TILES, E]),
            "s": b.sb("gate_sums", [P, TILES]),
            "t": b.sb("gate_thresholds", [P, TILES])}


def experts_vector(dve, b, S, w, first, E):
    for n in range(E * TILES):
        e, m = divmod(n, TILES)
        dve.wait_ge(S["expert"], n + 1)
        if n >= TILES:
            dve.wait_ge(S["expert_out"], n - TILES + 1)
        dve.scalar_tensor_tensor(b.X[:, m, :], b.psum[0:P, (first + n) % 7, :], w[:, m, e:e + 1], b.X[:, m, :],
                                 ALU.mult, ALU.add).then_inc(S["expert_out"], 1)


def experts_tensor(pe, b, S, W, first, E):
    for n in range(E * TILES):
        e, m = divmod(n, TILES)
        if e >= 4 and m == 0:
            pe.wait_ge(S[f"ring_in{e % 4}"], 16)
        if n >= 7:
            pe.wait_ge(S["expert_out"], n - 6)
        accumulate(pe, b.psum[0:P, (first + n) % 7, :],
                   [(tile_of(b.XT, k, m), W[:, ((e % 4) * K + k) * D:((e % 4) * K + k + 1) * D]) for k in range(K)]
                   ).then_inc(S["expert"], 1)


def experts_sync(sp, b, S, t, weights, W, E):
    for e in range(4, E):
        sp.wait_ge(S["expert"], TILES * (e - 3))
        sp.dma_start(W[:, (e - 4) * K * D:(e - 3) * K * D].rearrange("p (k n) -> p k n", k=K),
                     t[weights][e].rearrange("(k p) n -> p k n", p=128)).then_inc(S[f"ring_in{e % 4}"], 16)


def ffn_threshold(nc, b, t, slot, loaded, loads, load_next):
    S = Semaphores(nc, b.part)
    E = 8
    W, V = b.W[slot], b.V[slot]
    gate = b.U[slot][:, 0:K * (E + 1)].rearrange("p (k e) -> p k e", k=K)
    G = gate_buffers(b, E)
    wT = b.sb("gates_columns", [E, NODES])
    bias = V[0:E, D:2 * D]

    with nc.Block() as block:
        @block.sync
        def _(sp):
            experts_sync(sp, b, S, t, "L0_ffn_W_exp", W, E)
            load_next(sp)

        @block.vector
        def _(dve):
            prenorm_vector(dve, b, S)
            dve.wait_ge(loaded, loads)
            threshold_gates_vector(dve, b, S, G, E, V[0:P, 0:E + 1], 0.25)
            dve.wait_ge(S["gates_turned"], 1)
            dve.tensor_copy(wT[:, 0:4 * P], b.psum[0:E, 0, 0:4 * P]).then_inc(S["gates_out"], 1)
            dve.tensor_copy(wT[:, 4 * P:], b.psum[0:E, 1, 0:P]).then_inc(S["gates_out"], 1)
            for m in range(TILES):
                dve.wait_ge(S["bias"], m + 1)
                dve.tensor_tensor(b.X[:, m, :], b.psum[0:P, 2 + m, :], b.X[:, m, :], ALU.add).then_inc(S["bias_out"], 1)
            dve.wait_ge(S["bias_out"], TILES)
            experts_vector(dve, b, S, G["w"], 0, E)

        @block.scalar
        def _(act):
            prenorm_scalar(act, b, S)
            threshold_gates_scalar(act, b, S, G, E)

        @block.tensor
        def _(pe):
            prenorm_tensor(pe, b, S)
            pe.wait_ge(S["pre_columns"], TILES)
            pe.wait_ge(loaded, loads)
            logits_tensor(pe, b, S, gate, E + 1)
            pe.wait_ge(S["gates"], 1)
            for m in range(TILES):
                last = pe.transpose(b.psum[0:E, m // 4, (m % 4) * P:(m % 4 + 1) * P], G["w"][:, m, :], b.ident[0:P, 0:P])
            last.then_inc(S["gates_turned"], 1)
            pe.wait_ge(S["gates_out"], 2)
            for m in range(TILES):
                pe.matmul(b.psum[0:P, 2 + m, :], wT[:, m * P:(m + 1) * P], bias, start=True, stop=True
                          ).then_inc(S["bias"], 1)
            pe.wait_ge(S["bias_out"], TILES)
            experts_tensor(pe, b, S, W, 0, E)


def ffn_sinkhorn(nc, b, t, slot, loaded, loads, load_next):
    S = Semaphores(nc, b.part)
    E, ROUNDS = 8, 8
    TOP = NODES // E
    PICKS = -(-TOP // 8)
    SENTINELS = 8 * PICKS - TOP
    W = b.W[slot]
    PS = b.psum
    gate = b.U[slot][:, 0:K * E].rearrange("p (k e) -> p k e", k=K)
    T = b.sb("balanced", [P, TILES, E])
    T2 = b.sb("column_scaled", [P, TILES, E])
    rc = b.sb("column_factor", [P, E])
    rr = b.sb("row_factor", [P, TILES])
    rank = [b.sb(f"ranked{n}", [E, NODES + SENTINELS]) for n in range(2)]
    top8 = b.sb("top8", [E, 8])
    picked = b.sb("picked_columns", [E, NODES])
    sel = b.sb("picked", [P, TILES, E])
    w = b.sb("combine", [P, TILES, E])

    with nc.Block() as block:
        @block.sync
        def _(sp):
            experts_sync(sp, b, S, t, "L1_ffn_experts", W, E)
            load_next(sp)

        @block.vector
        def _(dve):
            prenorm_vector(dve, b, S)
            dve.wait_ge(S["logits"], 1)
            dve.tensor_scalar(T[:, :, :], PS[0:P, 7, 0:TILES * E].rearrange("p (m e) -> p m e", m=TILES), 1e-10, None,
                              ALU.max).then_inc(S["balanced"], 1)
            for i in range(ROUNDS):
                dve.wait_ge(S["column_sums"], i + 1)
                dve.reciprocal(rc[:, :], PS[0:P, 6, 0:E]).then_inc(S["bal"], 1)
                dve.wait_ge(S["bal"], 4 * i + 1)
                dve.tensor_tensor(T2[:, :, :], T[:, :, :], rc[:, :].unsqueeze(1).to_broadcast([P, TILES, E]), ALU.mult
                                  ).then_inc(S["bal"], 1)
                dve.wait_ge(S["bal"], 4 * i + 2)
                dve.tensor_reduce(rr[:, :], T2[:, :, :], AX.X, ALU.add).then_inc(S["bal"], 1)
                dve.wait_ge(S["bal"], 4 * i + 3)
                dve.reciprocal(rr[:, :], rr[:, :]).then_inc(S["bal"], 1)
                dve.wait_ge(S["bal"], 4 * i + 4)
                dve.tensor_tensor(T[:, :, :], T2[:, :, :], spread(rr[:, :], E), ALU.mult).then_inc(S["balanced"], 1)
            for n in range(SENTINELS):
                dve.memset(rank[0][:, NODES + n:NODES + n + 1], 4.0 + n).then_inc(S["ranked"], 1)
            dve.wait_ge(S["ranks_turned"], 1)
            dve.tensor_copy(rank[0][:, 0:4 * P], PS[0:E, 0, 0:4 * P]).then_inc(S["ranked"], 1)
            dve.tensor_copy(rank[0][:, 4 * P:NODES], PS[0:E, 1, 0:P]).then_inc(S["ranked"], 1)
            dve.wait_ge(S["ranked"], SENTINELS + 2)
            for n in range(PICKS):
                dve.max(top8[:, :], rank[n % 2][:, :]).then_inc(S["top8"], 1)
                dve.wait_ge(S["top8"], n + 1)
                dve.match_replace(rank[1 - n % 2][:, :], top8[:, :], rank[n % 2][:, :], -1.0).then_inc(S["taken"], 1)
                dve.wait_ge(S["taken"], n + 1)
            dve.tensor_scalar(picked[:, :], rank[PICKS % 2][:, 0:NODES], -1.0, None, ALU.is_equal).then_inc(S["picked"], 1)
            dve.wait_ge(S["picked_turned"], 1)
            dve.tensor_copy(sel[:, :, :], PS[0:P, 5, 0:TILES * E].rearrange("p (m e) -> p m e", m=TILES)
                            ).then_inc(S["comb"], 1)
            dve.wait_ge(S["comb"], 1)
            dve.tensor_reduce(rr[:, :], sel[:, :, :], AX.X, ALU.add).then_inc(S["comb"], 1)
            dve.scalar_tensor_tensor(w[:, :, :], T[:, :, :], 0.5, sel[:, :, :], ALU.is_gt, ALU.mult).then_inc(S["comb"], 1)
            dve.wait_ge(S["comb"], 3)
            dve.tensor_scalar(rr[:, :], rr[:, :], 1.0, None, ALU.add).then_inc(S["comb"], 1)
            dve.wait_ge(S["comb"], 4)
            dve.reciprocal(rr[:, :], rr[:, :]).then_inc(S["comb"], 1)
            dve.wait_ge(S["comb"], 5)
            dve.tensor_tensor(w[:, :, :], w[:, :, :], spread(rr[:, :], E), ALU.mult).then_inc(S["comb"], 1)
            dve.wait_ge(S["comb"], 6)
            experts_vector(dve, b, S, w, 0, E)

        @block.scalar
        def _(act):
            prenorm_scalar(act, b, S)

        @block.tensor
        def _(pe):
            prenorm_tensor(pe, b, S)
            pe.wait_ge(S["pre_columns"], TILES)
            pe.wait_ge(loaded, loads)
            logits_tensor(pe, b, S, gate, E)
            for i in range(ROUNDS):
                pe.wait_ge(S["balanced"], i + 1)
                accumulate(pe, PS[0:P, 6, 0:E], [(b.ones[0:P, 0:P], T[:, m, :]) for m in range(TILES)]
                           ).then_inc(S["column_sums"], 1)
            pe.wait_ge(S["balanced"], ROUNDS + 1)
            for m in range(TILES):
                last = pe.transpose(PS[0:E, m // 4, (m % 4) * P:(m % 4 + 1) * P], T[:, m, :], b.ident[0:P, 0:P])
            last.then_inc(S["ranks_turned"], 1)
            pe.wait_ge(S["picked"], 1)
            for m in range(TILES):
                last = pe.transpose(PS[0:P, 5, m * E:(m + 1) * E], picked[:, m * P:(m + 1) * P], b.ident[0:E, 0:E])
            last.then_inc(S["picked_turned"], 1)
            pe.wait_ge(S["comb"], 1)
            experts_tensor(pe, b, S, W, 0, E)


def attention(nc, b, t, layer, slot, loaded, loads, load_next, C, edged):
    S = Semaphores(nc, b.part)
    PS = b.psum
    HEADS, DH = 8, 64
    W, V = b.W[slot], b.V[slot]
    wq, wk, wv, wo = (W[:, n * K * D:(n + 1) * K * D].rearrange("p (k n) -> p k n", k=K) for n in range(4))
    w1 = V[:, 0:256].rearrange("p (k n) -> p k n", k=K)
    w2 = V[0:64, 256:768]
    ln_g, ln_b = V[0:P, 1024:1536], V[0:P, 1536:2048]
    cols = column_vectors(b, slot, [(n, K) for n in ("bq", "bo", "b2", "g1", "beta1", "g2", "beta2")] + [("b1", 1)])
    PAIRS = HEADS // 2
    ITEMS = TILES * PAIRS
    RING = 3

    qT = b.sb("q_columns", [128, K, PADDED])
    kT = b.sb("k_columns", [128, K, PADDED])
    v = b.XN
    bqs = b.sb("bq_scaled", [128, K])
    ring = [b.sb(f"scores{n}", [P, 2, PADDED]) for n in range(RING - 1)]
    ring.append(V[0:P, 4 * D:4 * D + 2 * PADDED].rearrange("p (a n) -> p a n", a=2))
    pT = b.sb("probabilities_turned", [P, 2, 2, TILES, P])
    top = b.sb("score_max", [P, ITEMS, 2])
    ntop = b.sb("minus_max", [P, ITEMS, 2])
    total = b.sb("prob_sum", [P, ITEMS, 2])
    inv = b.sb("inverse_sum", [P, ITEMS, 2])
    aT = b.sb("attended_columns", [128, K, PADDED])
    fT = kT[0:64, 0, :]
    bs = b.sb("batch_stats", [128, K, 2, 6])
    bm = b.sb("batch_mean", [128, K, 2])
    bv = b.sb("batch_scale", [128, 4, K])
    z = qT

    def batch_norm_vector(dve, tag, product, bias, gain, shift):
        for c in range(K + 1):
            if c < K:
                bank = 2 * (c % 4)
                dve.wait_ge(S[product], c + 1)
                dve.scalar_tensor_tensor(halves(z[:, c, :]), PS[:, bank:bank + 2, 0:HALF], bias[:, c:c + 1],
                                         halves(b.XT[:, c, :]), ALU.add, ALU.add).then_inc(S[tag + "_sums"], 1)
            if c >= 1:
                dve.wait_ge(S[tag + "_sums"], c)
                dve.bn_stats(bs[:, c - 1, 0, :], z[:, c - 1, 0:HALF]).then_inc(S[tag + "_stats"], 1)
                dve.bn_stats(bs[:, c - 1, 1, :], z[:, c - 1, HALF:NODES]).then_inc(S[tag + "_stats"], 1)
        dve.wait_ge(S[tag + "_stats"], 2 * K)
        for c in range(K):
            dve.bn_aggr(bm[:, c, :], bs[:, c, :, :].rearrange("p h s -> p (h s)")).then_inc(S[tag + "_aggr"], 1)
        dve.wait_ge(S[tag + "_aggr"], K)
        dve.tensor_scalar(bv[:, 0, :], bm[:, :, 1], 1e-5, None, ALU.add).then_inc(S[tag + "_var"], 1)
        dve.wait_ge(S[tag + "_root"], 1)
        dve.reciprocal(bv[:, 1, :], bv[:, 1, :]).then_inc(S[tag], 1)
        dve.wait_ge(S[tag], 1)
        dve.tensor_tensor(bv[:, 2, :], bv[:, 1, :], gain, ALU.mult).then_inc(S[tag], 1)
        dve.wait_ge(S[tag], 2)
        dve.tensor_tensor(bv[:, 3, :], bm[:, :, 0], bv[:, 2, :], ALU.mult).then_inc(S[tag], 1)
        dve.wait_ge(S[tag], 3)
        dve.tensor_tensor(bv[:, 3, :], shift, bv[:, 3, :], ALU.subtract).then_inc(S[tag], 1)
        dve.wait_ge(S[tag], 4)
        for c in range(0, K, 2):
            dve.tensor_scalar(b.XT[:, c, 0:NODES], z[:, c, 0:NODES], bv[:, 2, c:c + 1], bv[:, 3, c:c + 1], ALU.mult, ALU.add
                              ).then_inc(S[tag + "_even"], 1)

    def batch_norm_scalar(act, tag):
        act.wait_ge(S[tag + "_var"], 1)
        act.activation(bv[:, 1, :], bv[:, 0, :], ACT.Sqrt).then_inc(S[tag + "_root"], 1)
        act.wait_ge(S[tag], 4)
        for c in range(1, K, 2):
            act.activation(b.XT[:, c, 0:NODES], z[:, c, 0:NODES], ACT.Identity, bias=bv[:, 3, c:c + 1],
                           scale=bv[:, 2, c:c + 1]).then_inc(S[tag + "_odd"], 1)

    with nc.Block() as block:
        @block.sync
        def _(sp):
            load_next(sp)

        @block.gpsimd
        def _(pool):
            for n in range(ITEMS):
                pool.wait_ge(S["inv"], n + 1)
                for e in range(2):
                    pool.tensor_scalar(ring[n % RING][:, e, :], ring[n % RING][:, e, :], inv[:, n, e:e + 1],
                                       edged[:, n // PAIRS:n // PAIRS + 1], ALU.mult, ALU.mult).then_inc(S["scaled"], 1)

        @block.vector
        def _(dve):
            def last_source_tile(n):
                dve.wait_ge(S["turned"], n + 1)
                if n >= 2:
                    dve.wait_ge(S["pv"], n - 1)
                dve.tensor_copy(pT[:, n % 2, :, 4, :], PS[0:P, 6, 0:2 * P].rearrange("p (e d) -> p e d", e=2)).then_inc(S["turned_last"], 1)

            if layer == 0:
                prenorm_vector(dve, b, S)
                dve.wait_ge(b.counts_loaded, 16)
                dve.wait_ge(S["pre_turned"], TILES)
                dve.tensor_reduce(edged[:, :], C[:, :, :], AX.X, ALU.max).then_inc(S["edged"], 1)
                dve.wait_ge(S["edged"], 1)
                dve.tensor_scalar(edged[:, :], edged[:, :], 0.0, None, ALU.is_gt).then_inc(S["edged"], 1)
                dve.tensor_scalar(v[:, :, :], C[:, :, 0:D], 0.0, None, ALU.is_equal).then_inc(S["none"], 1)
                dve.tensor_scalar(aT[0:P, 0:1, 0:TILES * (PADDED - D)].rearrange("p a (m n) -> p (a m) n", m=TILES),
                                  C[:, :, D:], 0.0, None, ALU.is_equal).then_inc(S["none"], 1)
                dve.wait_ge(S["none"], 2)
                dve.tensor_tensor(C[:, :, 0:D], C[:, :, 0:D], v[:, :, :], ALU.add).then_inc(S["none"], 1)
                dve.tensor_tensor(C[:, :, D:], C[:, :, D:],
                                  aT[0:P, 0:1, 0:TILES * (PADDED - D)].rearrange("p a (m n) -> p (a m) n", m=TILES),
                                  ALU.add).then_inc(S["counts_safe"], 1)
                dve.wait_ge(S["counts_log"], 1)
                dve.scalar_tensor_tensor(C[:, :, 0:D], v[:, :, :], -BIG, C[:, :, 0:D], ALU.mult, ALU.add
                                         ).then_inc(S["log_counts"], 1)
                dve.scalar_tensor_tensor(C[:, :, D:],
                                         aT[0:P, 0:1, 0:TILES * (PADDED - D)].rearrange("p a (m n) -> p (a m) n", m=TILES),
                                         -BIG, C[:, :, D:], ALU.mult, ALU.add).then_inc(S["log_counts"], 1)
                dve.wait_ge(S["log_counts"], 2)
            dve.memset(aT[:, :, NODES:], 0.0).then_inc(S["padding"], 1)
            dve.wait_ge(loaded, loads)
            dve.tensor_scalar(bqs[:, :], cols["bq"], float(DH) ** -0.5, None, ALU.mult).then_inc(S["bq"], 1)
            for c in range(K):
                dve.wait_ge(S["qk"], 2 * c + 2)
                bank = 4 * (c % 2) + 2
                dve.tensor_copy(halves(kT[:, c, :]), PS[:, bank:bank + 2, 0:HALF]).then_inc(S["k_out"], 1)
            for m in range(TILES):
                dve.wait_ge(S["v"], m + 1)
                dve.tensor_copy(v[:, m, :], PS[0:P, m, :]).then_inc(S["v_out"], 1)
            for n in range(ITEMS + 2):
                if n < ITEMS:
                    m, pair = divmod(n, PAIRS)
                    dve.wait_ge(S["scores"], n + 1)
                    if n >= RING:
                        dve.wait_ge(S["turned"], n - RING + 1)
                    for e in range(2):
                        dve.tensor_tensor_reduce(halves(ring[n % RING][:, e, :]), PS[0:P, 2 * e:2 * e + 2, 0:HALF],
                                                 halves(C[:, m, :]), 1.0, -3e38, ALU.add, ALU.max, top[:, n, e:e + 1]
                                                 ).then_inc(S["scored"], 1)
                    dve.wait_ge(S["scored"], 2 * n + 2)
                    dve.tensor_scalar(ntop[:, n, :], top[:, n, :], -1.0, None, ALU.mult).then_inc(S["ntop"], 1)
                if 1 <= n <= ITEMS:
                    dve.wait_ge(S["probs"], 2 * n)
                    dve.reciprocal(inv[:, n - 1, :], total[:, n - 1, :]).then_inc(S["inv"], 1)
                if n >= 2:
                    last_source_tile(n - 2)
            batch_norm_vector(dve, "bn1", "wo", cols["bo"], cols["g1"], cols["beta1"])
            batch_norm_vector(dve, "bn2", "ff2", cols["b2"], cols["g2"], cols["beta2"])
            if layer == 1:
                for m in range(TILES):
                    dve.wait_ge(S["rows"], m + 1)
                    dve.tensor_copy(b.XN[:, m, :], PS[0:P, m, :]).then_inc(S["rows_out"], 1)
                dve.wait_ge(S["rows_out"], TILES)
                row_stats(dve, b, S, "last", [[b.XN[:, m, :]] for m in range(TILES)])
                for m in range(TILES):
                    dve.tensor_scalar(b.XN[:, m, :], b.XN[:, m, :], b.mv[:, m, 0:1], b.rstd[:, m:m + 1],
                                      ALU.subtract, ALU.mult).then_inc(S["last_norm"], 1)
                    dve.tensor_tensor(b.X[:, m, :], b.X[:, m, :], ln_b, ALU.add).then_inc(S["last_shift"], 1)
                for m in range(TILES):
                    dve.wait_ge(S["last_norm"], m + 1)
                    dve.tensor_tensor(b.XN[:, m, :], b.XN[:, m, :], ln_g, ALU.mult).then_inc(S["last_gain"], 1)
                dve.wait_ge(S["last_shift"], TILES)
                for m in range(TILES):
                    dve.wait_ge(S["last_gain"], m + 1)
                    dve.tensor_tensor(b.X[:, m, :], b.X[:, m, :], b.XN[:, m, :], ALU.add).then_inc(S["last_sum"], 1)

        @block.scalar
        def _(act):
            def source_tiles(n):
                act.wait_ge(S["turned"], n + 1)
                if n >= 2:
                    act.wait_ge(S["pv"], n - 1)
                act.activation(pT[:, n % 2, :, 0:4, :].rearrange("p e s d -> p e (s d)"), PS[0:P, 4:6, 0:4 * P], ACT.Copy
                               ).then_inc(S["turned_first"], 1)

            def attended(m):
                act.wait_ge(S["pv"], PAIRS * (m + 1))
                act.activation(aT[:, :, m * P:(m + 1) * P], PS[:, 7, 0:K * P].rearrange("p (k n) -> p k n", k=K),
                               ACT.Copy).then_inc(S["att_columns"], 1)

            if layer == 0:
                prenorm_scalar(act, b, S)
                act.wait_ge(S["counts_safe"], 1)
                act.wait_ge(S["none"], 3)
                act.activation(C[:, :, :], C[:, :, :], ACT.Ln).then_inc(S["counts_log"], 1)
            act.wait_ge(S["bq"], 1)
            for c in range(K):
                act.wait_ge(S["qk"], 2 * c + 1)
                bank = 4 * (c % 2)
                act.activation(halves(qT[:, c, :]), PS[:, bank:bank + 2, 0:HALF], ACT.Identity, bias=bqs[:, c:c + 1],
                               scale=float(DH) ** -0.5).then_inc(S["q_out"], 1)
            for n in range(ITEMS + 2):
                if n >= 4 and (n - 4) % PAIRS == PAIRS - 1:
                    attended((n - 4) // PAIRS)
                if n < ITEMS:
                    act.wait_ge(S["ntop"], n + 1)
                    for e in range(2):
                        act.activation(ring[n % RING][:, e, :], ring[n % RING][:, e, :], ACT.Exp,
                                       bias=ntop[:, n, e:e + 1], scale=1.0, accum_out=total[:, n, e:e + 1]
                                       ).then_inc(S["probs"], 1)
                if n >= 2:
                    source_tiles(n - 2)
            attended(TILES - 1)
            batch_norm_scalar(act, "bn1")
            act.wait_ge(S["ff1"], 1)
            act.activation(halves(fT), PS[0:64, 0:2, 0:HALF], ACT.Relu, bias=cols["b1"][0:64, :]).then_inc(S["ff"], 1)
            batch_norm_scalar(act, "bn2")
            if layer == 1:
                row_root(act, b, S, "last")

        @block.tensor
        def _(pe):
            if layer == 0:
                prenorm_tensor(pe, b, S)
                pe.wait_ge(S["pre_columns"], TILES)
            pe.wait_ge(loaded, loads)
            for c in range(K):
                for part, w in enumerate((wq, wk)):
                    if c >= 2:
                        pe.wait_ge(S[("q_out", "k_out")[part]], c - 1)
                    for h in range(2):
                        last = accumulate(pe, PS[:, 4 * (c % 2) + 2 * part + h, 0:HALF],
                                          [(w[:, k, c * 128:(c + 1) * 128], b.XT[:, k, h * HALF:(h + 1) * HALF])
                                           for k in range(K)])
                    last.then_inc(S["qk"], 1)
            pe.wait_ge(S["q_out"], K)
            pe.wait_ge(S["k_out"], K)
            for m in range(TILES):
                accumulate(pe, PS[0:P, m, :], [(tile_of(b.XT, k, m), wv[:, k, :]) for k in range(K)]).then_inc(S["v"], 1)
            pe.wait_ge(S["v_out"], TILES)

            def scores(n):
                m, pair = divmod(n, PAIRS)
                if n >= 1:
                    pe.wait_ge(S["scored"], 2 * n)
                for half in range(2):
                    for e in range(2):
                        rows = slice(DH * e, DH * e + DH)
                        last = pe.matmul(PS[0:P, 2 * e + half, 0:HALF], qT[rows, pair, m * P:(m + 1) * P],
                                         kT[rows, pair, half * HALF:(half + 1) * HALF], start=True, stop=True)
                last.then_inc(S["scores"], 1)

            def turn(n):
                pe.wait_ge(S["scaled"], 2 * n + 2)
                if n >= 1:
                    pe.wait_ge(S["turned_first"], n)
                    pe.wait_ge(S["turned_last"], n)
                for e in range(2):
                    for s in range(TILES):
                        bank, at = (4 + e, s * P) if s < 4 else (6, e * P)
                        last = pe.transpose(PS[0:P, bank, at:at + P], ring[n % RING][:, e, s * P:(s + 1) * P],
                                            b.ident[0:P, 0:P])
                last.then_inc(S["turned"], 1)

            def weigh(n):
                m, pair = divmod(n, PAIRS)
                if pair == 0 and m >= 1:
                    pe.wait_ge(S["att_columns"], m)
                pe.wait_ge(S["turned_first"], n + 1)
                pe.wait_ge(S["turned_last"], n + 1)
                for s in range(TILES):
                    for e in range(2):
                        at = (2 * pair + e) * DH
                        last = pe.matmul(PS[DH * e:DH * e + DH, 7, pair * P:(pair + 1) * P], v[:, s, at:at + DH],
                                         pT[:, n % 2, e, s, :], start=(s == 0), stop=(s == TILES - 1),
                                         skip_group_check=True)
                last.then_inc(S["pv"], 1)

            for n in range(ITEMS + 3):
                if n < ITEMS:
                    scores(n)
                if 2 <= n < ITEMS + 2:
                    turn(n - 2)
                if n >= 3:
                    weigh(n - 3)
            pe.wait_ge(S["att_columns"], TILES)
            pe.wait_ge(S["padding"], 1)
            for c in range(K):
                for h in range(2):
                    last = accumulate(pe, PS[:, 2 * c + h, 0:HALF],
                                      [(wo[:, k, c * 128:(c + 1) * 128], aT[:, k, h * HALF:(h + 1) * HALF])
                                       for k in range(K)])
                last.then_inc(S["wo"], 1)
            for k in range(K):
                pe.wait_ge(S[("bn1_even", "bn1_odd")[k % 2]], k // 2 + 1)
                for h in range(2):
                    last = pe.matmul(PS[0:64, h, 0:HALF], w1[:, k, :], b.XT[:, k, h * HALF:(h + 1) * HALF],
                                     start=(k == 0), stop=(k == K - 1))
            last.then_inc(S["ff1"], 1)
            pe.wait_ge(S["ff"], 1)
            for c in range(K):
                for h in range(2):
                    last = pe.matmul(PS[:, 2 * c + h, 0:HALF], w2[:, c * 128:(c + 1) * 128],
                                     fT[:, h * HALF:(h + 1) * HALF], start=True, stop=True)
                last.then_inc(S["ff2"], 1)
            if layer == 1:
                pe.wait_ge(S["bn2_even"], K // 2)
                pe.wait_ge(S["bn2_odd"], K // 2)
                for m in range(TILES):
                    for k in range(K):
                        last = pe.transpose(PS[0:P, m, k * 128:(k + 1) * 128], tile_of(b.XT, k, m), b.ident[:, :])
                    last.then_inc(S["rows"], 1)



def relations(nc, b, t, layer, slot, loaded, loads, load_next, C2):
    S = Semaphores(nc, b.part)
    PS = b.psum
    W = b.W[slot]
    mixed = W[:, 0:STEPS * D].rearrange("p (a n) -> p a n", a=STEPS)
    root = W[:, STEPS * D:STEPS * D + K * D].rearrange("p (k n) -> p k n", k=K)
    bias = b.V[slot][0:P, 0:D]
    gate = b.U[slot][:, 0:2 * K].rearrange("p (k r) -> p k r", k=K)
    g = b.sb("gates", [P, TILES, 2])
    xg = b.sb("gated", [P, 2, TILES, D])
    yT = b.sb("gathered_columns", [128, STEPS, PADDED])

    with nc.Block() as block:
        @block.sync
        def _(sp):
            load_next(sp)

        @block.vector
        def _(dve):
            if layer == 0:
                prenorm_vector(dve, b, S)
            dve.wait_ge(S["gate_exp"], 1)
            dve.tensor_scalar(g[:, :, :], g[:, :, :], 1.0, None, ALU.add).then_inc(S["gate"], 1)
            dve.wait_ge(S["gate"], 1)
            dve.reciprocal(g[:, :, :], g[:, :, :]).then_inc(S["gate"], 1)
            dve.wait_ge(S["gate"], 2)
            for m in range(TILES):
                dve.tensor_scalar(xg[:, 1, m, :], b.XN[:, m, :], g[:, m, 1:2], None, ALU.mult).then_inc(S["gated_1"], 1)
            for n in range(2 * K):
                c, r = divmod(n, 2)
                bank = 2 * (n % 4)
                dve.wait_ge(S["gathered"], n + 1)
                dve.tensor_copy(halves(yT[64 * r:64 * r + 64, 2 * c, :]), PS[0:64, bank:bank + 2, 0:HALF]
                                ).then_inc(S["y_low"], 1)
            dve.wait_ge(loaded, loads)
            for m in range(TILES):
                dve.wait_ge(S["sum"], m + 1)
                if layer == 0:
                    dve.tensor_tensor(xg[:, 0, m, :], PS[0:P, m, :], bias, ALU.add).then_inc(S["biased"], 1)
                else:
                    dve.tensor_tensor(xg[:, 0, m, :], PS[0:P, m, :], bias, ALU.add).then_inc(S["biased"], 1)
                    dve.wait_ge(S["biased"], m + 1)
                    dve.tensor_tensor(b.X[:, m, :], xg[:, 0, m, :], b.X[:, m, :], ALU.add).then_inc(S["added"], 1)

        @block.scalar
        def _(act):
            if layer == 0:
                prenorm_scalar(act, b, S)
            act.wait_ge(S["logits"], 1)
            act.activation(g[:, :, :], PS[0:P, 7, 0:2 * TILES].rearrange("p (m r) -> p m r", m=TILES), ACT.Exp, scale=-1.0
                           ).then_inc(S["gate_exp"], 1)
            act.wait_ge(S["gate"], 2)
            for m in range(TILES):
                act.activation(xg[:, 0, m, :], b.XN[:, m, :], ACT.Copy, scale=g[:, m, 0:1]).then_inc(S["gated_0"], 1)
            for n in range(2 * K):
                c, r = divmod(n, 2)
                bank = 2 * (n % 4)
                act.wait_ge(S["gathered"], n + 1)
                act.activation(halves(yT[64 * r:64 * r + 64, 2 * c + 1, :]), PS[64:128, bank:bank + 2, 0:HALF], ACT.Copy
                               ).then_inc(S["y_high"], 1)
            if layer == 0:
                for m in range(TILES):
                    act.wait_ge(S["biased"], m + 1)
                    act.activation(b.XN[:, m, :], xg[:, 0, m, :], ACT.Relu).then_inc(S["x_rows"], 1)
                for m in range(TILES):
                    act.wait_ge(S["x_turned"], m + 1)
                    act.activation(b.XT[:, :, m * P:(m + 1) * P], PS[:, m, 0:K * P].rearrange("p (k n) -> p k n", k=K),
                                   ACT.Copy).then_inc(S["x_columns"], 1)

        @block.tensor
        def _(pe):
            if layer == 0:
                prenorm_tensor(pe, b, S)
                pe.wait_ge(S["pre_columns"], TILES)
            pe.wait_ge(loaded, loads)
            logits_tensor(pe, b, S, gate, 2)
            pe.wait_ge(b.relations_loaded, 32)
            pe.wait_ge(S["gated_0"], TILES)
            pe.wait_ge(S["gated_1"], TILES)
            for n in range(2 * K):
                c, r = divmod(n, 2)
                if n >= 4:
                    pe.wait_ge(S["y_low"], n - 3)
                    pe.wait_ge(S["y_high"], n - 3)
                for h in range(2):
                    last = accumulate(pe, PS[:, 2 * (n % 4) + h, 0:HALF],
                                      [(xg[:, r, m, c * 128:(c + 1) * 128], C2[:, r, m, h * HALF:(h + 1) * HALF])
                                       for m in range(TILES)])
                last.then_inc(S["gathered"], 1)
            pe.wait_ge(S["y_low"], 2 * K)
            pe.wait_ge(S["y_high"], 2 * K)
            for m in range(TILES):
                accumulate(pe, PS[0:P, m, :], [(tile_of(yT, a, m), mixed[:, a, :]) for a in range(STEPS)] +
                           [(tile_of(b.XT, k, m), root[:, k, :]) for k in range(K)]).then_inc(S["sum"], 1)
            if layer == 0:
                for m in range(TILES):
                    pe.wait_ge(S["x_rows"], m + 1)
                    for k in range(K):
                        last = pe.transpose(PS[:, m, k * P:(k + 1) * P], b.XN[:, m, k * 128:(k + 1) * 128],
                                            b.ident[0:P, 0:P])
                    last.then_inc(S["x_turned"], 1)



def ffn_top2(nc, b, t, slot, loaded, loads, load_next):
    S = Semaphores(nc, b.part)
    PS = b.psum
    E = 8
    FILL = 6
    W = b.W[slot]
    w1 = W[:, 0:K * D].rearrange("p (k n) -> p k n", k=K)
    w2 = W[:, K * D:2 * K * D].rearrange("p (k n) -> p k n", k=K)
    b2 = W[0:P, 2 * K * D:].rearrange("p (e n) -> p e n", e=E)
    gamma = b.V[slot][0:P, :].rearrange("p (e n) -> p e n", e=E)
    router = b.U[slot][:, 0:K * E].rearrange("p (k e) -> p k e", k=K)
    b1 = b.U[slot][:, K * E:K * E + K]
    lg = b.sb("router_logits", [P, TILES, E + FILL])
    lg2 = b.sb("router_taken", [P, TILES, E + FILL])
    top8 = b.sb("router_top8", [P, TILES, 8])
    sel = b.sb("router_sel", [P, TILES, E])
    w = b.sb("router_weights", [P, TILES, E])
    s = b.sb("router_sums", [P, TILES])
    wT = b.sb("router_columns", [E, NODES])
    beta = b.sb("beta", [E, D])
    fT = b.sb("hidden_columns", [128, K, PADDED])
    xb = b.sb("x_plus_b2", [P, 2, TILES, D])
    y = b.sb("y", [P, 2, TILES, D])
    st = b.sb("y_stats", [P, 2, TILES, 6])
    mv = b.sb("y_mean", [P, 2, TILES, 2])
    sd = b.sb("y_root", [P, 2, TILES])
    ws = b.sb("y_scale", [P, 2, TILES])
    nm = b.sb("y_shift", [P, 2, TILES])

    with nc.Block() as block:
        @block.sync
        def _(sp):
            sp.dma_start(beta[:, :], t["L2_ffn_beta"]).then_inc(S["beta_in"], 16)
            load_next(sp)

        @block.gpsimd
        def _(pool):
            pool.wait_ge(loaded, loads)
            pool.wait_ge(S["pre_rows"], TILES)
            for e in range(E):
                if e >= 2:
                    pool.wait_ge(S["y_sum"], TILES * (e - 1))
                for m in range(TILES):
                    pool.tensor_tensor(xb[:, e % 2, m, :], b.XN[:, m, :], b2[:, e, :], ALU.add).then_inc(S["xb"], 1)

        @block.vector
        def _(dve):
            prenorm_vector(dve, b, S)
            dve.memset(lg[:, :, E:], 3e38).then_inc(S["route"], 1)
            dve.wait_ge(S["logits"], 1)
            dve.tensor_copy(lg[:, :, 0:E], PS[0:P, 7, 0:TILES * E].rearrange("p (m e) -> p m e", m=TILES)
                            ).then_inc(S["route"], 1)
            dve.wait_ge(S["route"], 2)
            for m in range(TILES):
                dve.max(top8[:, m, :], lg[:, m, :]).then_inc(S["top8"], 1)
            for m in range(TILES):
                dve.wait_ge(S["top8"], m + 1)
                dve.match_replace(lg2[:, m, :], top8[:, m, :], lg[:, m, :], -3e38).then_inc(S["route"], 1)
            dve.wait_ge(S["route"], 2 + TILES)
            dve.tensor_tensor(sel[:, :, :], lg[:, :, 0:E], lg2[:, :, 0:E], ALU.not_equal).then_inc(S["route"], 1)
            dve.tensor_tensor(w[:, :, :], lg[:, :, 0:E], top8[:, :, FILL:FILL + 1].to_broadcast([P, TILES, E]),
                              ALU.subtract).then_inc(S["route_shifted"], 1)
            dve.wait_ge(S["route_exp"], 1)
            dve.wait_ge(S["route"], 3 + TILES)
            dve.tensor_tensor(w[:, :, :], w[:, :, :], sel[:, :, :], ALU.mult).then_inc(S["route"], 1)
            dve.wait_ge(S["route"], 4 + TILES)
            dve.tensor_reduce(s[:, :], w[:, :, :], AX.X, ALU.add).then_inc(S["route"], 1)
            dve.wait_ge(S["route"], 5 + TILES)
            dve.reciprocal(s[:, :], s[:, :]).then_inc(S["route"], 1)
            dve.wait_ge(S["route"], 6 + TILES)
            dve.tensor_tensor(w[:, :, :], w[:, :, :], spread(s[:, :], E), ALU.mult).then_inc(S["gates"], 1)
            dve.wait_ge(S["gates_turned"], 1)
            dve.tensor_copy(wT[:, 0:4 * P], PS[0:E, 0, 0:4 * P]).then_inc(S["gates_out"], 1)
            dve.tensor_copy(wT[:, 4 * P:], PS[0:E, 1, 0:P]).then_inc(S["gates_out"], 1)
            for m in range(TILES):
                dve.wait_ge(S["betas"], m + 1)
                dve.tensor_tensor(b.X[:, m, :], PS[0:P, 2 + m, :], b.X[:, m, :], ALU.add).then_inc(S["betas_out"], 1)
            for e in range(E + 1):
                if e < E:
                    for m in range(TILES):
                        n = e * TILES + m
                        dve.wait_ge(S["expert"], n + 1)
                        dve.wait_ge(S["xb"], n + 1)
                        if e >= 2:
                            dve.wait_ge(S["added"], (e - 2) * TILES + m + 1)
                        dve.tensor_tensor(y[:, e % 2, m, :], PS[0:P, n % 8, :], xb[:, e % 2, m, :], ALU.add
                                          ).then_inc(S["y_sum"], 1)
                    for m in range(TILES):
                        dve.wait_ge(S["y_sum"], e * TILES + m + 1)
                        dve.bn_stats(st[:, e % 2, m, :], y[:, e % 2, m, :]).then_inc(S["y_stats"], 1)
                    dve.wait_ge(S["y_stats"], TILES * (e + 1))
                    for m in range(TILES):
                        dve.bn_aggr(mv[:, e % 2, m, :], st[:, e % 2, m, :]).then_inc(S["y_aggr"], 1)
                    dve.wait_ge(S["y_aggr"], TILES * (e + 1))
                    dve.tensor_scalar(sd[:, e % 2, :], mv[:, e % 2, :, 1], 1e-6, None, ALU.add).then_inc(S["y_var"], 1)
                    dve.wait_ge(S["y_root"], e + 1)
                    dve.reciprocal(ws[:, e % 2, :], sd[:, e % 2, :]).then_inc(S["y_scale"], 1)
                    dve.wait_ge(S["y_scale"], 2 * e + 1)
                    dve.tensor_tensor(ws[:, e % 2, :], ws[:, e % 2, :], w[:, :, e], ALU.mult).then_inc(S["y_scale"], 1)
                    dve.wait_ge(S["y_scale"], 2 * e + 2)
                    dve.scalar_tensor_tensor(nm[:, e % 2, :], mv[:, e % 2, :, 0], -1.0, ws[:, e % 2, :], ALU.mult, ALU.mult
                                             ).then_inc(S["y_shift"], 1)
                if e >= 1:
                    f = e - 1
                    for m in range(TILES):
                        n = f * TILES + m
                        dve.wait_ge(S["y_norm"], n + 1)
                        dve.tensor_tensor(y[:, f % 2, m, :], y[:, f % 2, m, :], gamma[:, f, :], ALU.mult
                                          ).then_inc(S["y_gain"], 1)
                    for m in range(TILES):
                        dve.wait_ge(S["y_gain"], f * TILES + m + 1)
                        if f == 0:
                            dve.wait_ge(S["betas_out"], m + 1)
                        else:
                            dve.wait_ge(S["added"], (f - 1) * TILES + m + 1)
                        dve.tensor_tensor(b.X[:, m, :], b.X[:, m, :], y[:, f % 2, m, :], ALU.add).then_inc(S["added"], 1)

        @block.scalar
        def _(act):
            prenorm_scalar(act, b, S)
            for c in range(K):
                act.wait_ge(S["hidden"], c + 1)
                bank = 2 * (c % 3)
                act.activation(halves(fT[:, c, :]), PS[:, bank:bank + 2, 0:HALF], ACT.Relu, bias=b1[:, c:c + 1]
                               ).then_inc(S["hidden_out"], 1)
            act.wait_ge(S["route_shifted"], 1)
            act.activation(w[:, :, :], w[:, :, :], ACT.Exp).then_inc(S["route_exp"], 1)
            for e in range(E):
                act.wait_ge(S["y_var"], e + 1)
                act.activation(sd[:, e % 2, :], sd[:, e % 2, :], ACT.Sqrt).then_inc(S["y_root"], 1)
                act.wait_ge(S["y_shift"], e + 1)
                for m in range(TILES):
                    act.activation(y[:, e % 2, m, :], y[:, e % 2, m, :], ACT.Identity, bias=nm[:, e % 2, m:m + 1],
                                   scale=ws[:, e % 2, m:m + 1]).then_inc(S["y_norm"], 1)

        @block.tensor
        def _(pe):
            prenorm_tensor(pe, b, S)
            pe.wait_ge(S["pre_columns"], TILES)
            pe.wait_ge(loaded, loads)
            logits_tensor(pe, b, S, router, E)
            for c in range(K):
                if c >= 3:
                    pe.wait_ge(S["hidden_out"], c - 2)
                for h in range(2):
                    last = accumulate(pe, PS[:, 2 * (c % 3) + h, 0:HALF],
                                      [(w1[:, k, c * 128:(c + 1) * 128], b.XT[:, k, h * HALF:(h + 1) * HALF])
                                       for k in range(K)])
                last.then_inc(S["hidden"], 1)
            pe.wait_ge(S["hidden_out"], K)
            pe.wait_ge(S["gates"], 1)
            for m in range(TILES):
                last = pe.transpose(PS[0:E, m // 4, (m % 4) * P:(m % 4 + 1) * P], w[:, m, :], b.ident[0:P, 0:P])
            last.then_inc(S["gates_turned"], 1)
            pe.wait_ge(S["gates_out"], 2)
            pe.wait_ge(S["beta_in"], 16)
            for m in range(TILES):
                pe.matmul(PS[0:P, 2 + m, :], wT[:, m * P:(m + 1) * P], beta[:, :], start=True, stop=True
                          ).then_inc(S["betas"], 1)
            pe.wait_ge(S["betas_out"], TILES)
            for n in range(E * TILES):
                e, m = divmod(n, TILES)
                rows = slice(64 * (e % 2), 64 * (e % 2) + 64)
                if n >= 8:
                    pe.wait_ge(S["y_sum"], n - 7)
                pe.matmul(PS[0:P, n % 8, :], fT[rows, e // 2, m * P:(m + 1) * P], w2[rows, e // 2, :],
                          start=True, stop=True).then_inc(S["expert"], 1)



def isomorphism(nc, b, t, slot, loaded, loads, load_next):
    S = Semaphores(nc, b.part)
    PS = b.psum
    W = b.W[slot]
    w1 = W[:, 0:K * D].rearrange("p (k n) -> p k n", k=K)
    w2 = W[:, K * D:2 * K * D].rearrange("p (k n) -> p k n", k=K)
    b1 = b.U[slot][:, 0:K]
    b2 = b.V[slot][0:P, 0:D]
    hT = b.sb("h_columns", [128, K, PADDED])
    fT = b.sb("hidden_columns", [128, K, PADDED])

    with nc.Block() as block:
        @block.sync
        def _(sp):
            load_next(sp)

        @block.vector
        def _(dve):
            prenorm_vector(dve, b, S)
            dve.wait_ge(loaded, loads)
            for m in range(TILES):
                dve.tensor_tensor(b.X[:, m, :], b.X[:, m, :], b2, ALU.add).then_inc(S["b2"], 1)
            dve.wait_ge(S["pre_columns"], TILES)
            for c in range(K):
                dve.wait_ge(S["aggregated"], c + 1)
                dve.tensor_tensor(halves(hT[:, c, :]), PS[:, 2 * c:2 * c + 2, 0:HALF], halves(b.XT[:, c, :]), ALU.add
                                  ).then_inc(S["h"], 1)
            dve.wait_ge(S["b2"], TILES)
            for m in range(TILES):
                dve.wait_ge(S["down"], m + 1)
                dve.tensor_tensor(b.X[:, m, :], PS[0:P, m, :], b.X[:, m, :], ALU.add).then_inc(S["added"], 1)

        @block.scalar
        def _(act):
            prenorm_scalar(act, b, S)
            act.wait_ge(loaded, loads)
            for c in range(K):
                act.wait_ge(S["up"], c + 1)
                act.activation(halves(fT[:, c, :]), PS[:, 2 * c:2 * c + 2, 0:HALF], ACT.Relu, bias=b1[:, c:c + 1]
                               ).then_inc(S["up_out"], 1)

        @block.tensor
        def _(pe):
            prenorm_tensor(pe, b, S)
            pe.wait_ge(S["pre_columns"], TILES)
            for c in range(K):
                for h in range(2):
                    last = accumulate(pe, PS[:, 2 * c + h, 0:HALF],
                                      [(b.XN[:, m, c * 128:(c + 1) * 128], b.CT[:, m, h * HALF:(h + 1) * HALF])
                                       for m in range(TILES)])
                last.then_inc(S["aggregated"], 1)
            pe.wait_ge(S["h"], K)
            pe.wait_ge(loaded, loads)
            for c in range(K):
                for h in range(2):
                    last = accumulate(pe, PS[:, 2 * c + h, 0:HALF],
                                      [(w1[:, k, c * 128:(c + 1) * 128], hT[:, k, h * HALF:(h + 1) * HALF])
                                       for k in range(K)])
                last.then_inc(S["up"], 1)
            pe.wait_ge(S["up_out"], K)
            for m in range(TILES):
                accumulate(pe, PS[0:P, m, :], [(tile_of(fT, k, m), w2[:, k, :]) for k in range(K)]).then_inc(S["down"], 1)



def ffn_lora(nc, b, t, slot, loaded, loads, out):
    S = Semaphores(nc, b.part)
    PS = b.psum
    E, R = 4, 16
    W = b.W[slot]
    fc2 = b.W[1 - slot]
    gate = b.U[slot][:, 0:K * (E + 1)].rearrange("p (k e) -> p k e", k=K)
    down = b.V[slot][:, 0:E * K * R].rearrange("p (e k r) -> p e k r", e=E, k=K)
    up = b.V[slot][:, 256:256 + E * K * R].rearrange("p (e k r) -> p e k r", e=E, k=K)
    G = gate_buffers(b, E)
    up_wide = b.sb("up_wide", [128, E, K, E * R])
    up_fc2 = b.sb("up_times_fc2", [E * R, D])
    hT = b.sb("hidden_columns", [128, K, PADDED])
    lo = b.sb("low", [P, TILES, E, R])
    lw = b.sb("low_weighted", [P, TILES, E * R])
    lT = b.sb("low_columns", [E * R, NODES])

    with nc.Block() as block:
        @block.sync
        def _(sp):
            for e in range(E):
                sp.dma_start(fc2[:, e * K * D:(e + 1) * K * D].rearrange("p (k n) -> p k n", k=K),
                             t["lora_fc2"][e].rearrange("(k p) n -> p k n", p=128)).then_inc(S["fc2_in"], 16)
            for m in range(TILES):
                sp.wait_ge(S["added"], m + 1)
                sp.dma_start(out[m * P:(m + 1) * P, :], b.X[:, m, :]).then_inc(S["stored"], 16)
            sp.wait_ge(S["stored"], 16 * TILES)

        @block.vector
        def _(dve):
            prenorm_vector(dve, b, S)
            dve.memset(up_wide[:, :, :, :], 0.0).then_inc(S["wide"], 1)
            dve.wait_ge(loaded, loads)
            dve.wait_ge(S["wide"], 1)
            for e in range(E):
                dve.tensor_copy(up_wide[:, e, :, e * R:(e + 1) * R], up[:, e, :, :]).then_inc(S["wide"], 1)
            threshold_gates_vector(dve, b, S, G, E, None, 1.0 / E)
            for e in range(E):
                dve.wait_ge(S["low"], e + 1)
                dve.tensor_copy(lo[:, :, e, :], PS[0:P, 6, 0:TILES * R].rearrange("p (m r) -> p m r", m=TILES)
                                ).then_inc(S["low_out"], 1)
            dve.wait_ge(S["gates"], 1)
            dve.wait_ge(S["low_out"], E)
            for m in range(TILES):
                dve.tensor_tensor(lw[:, m, :].rearrange("p (e r) -> p e r", e=E), lo[:, m, :, :],
                                  spread(G["w"][:, m, :], R), ALU.mult).then_inc(S["weighted"], 1)
            dve.wait_ge(S["fused"], 1)
            dve.tensor_copy(up_fc2[:, :], PS[0:E * R, 7, :]).then_inc(S["fused_out"], 1)
            dve.wait_ge(S["low_turned"], 1)
            dve.tensor_copy(lT[:, 0:4 * P], PS[0:E * R, 0, 0:4 * P]).then_inc(S["low_columns"], 1)
            dve.tensor_copy(lT[:, 4 * P:], PS[0:E * R, 1, 0:P]).then_inc(S["low_columns"], 1)
            for m in range(TILES):
                dve.wait_ge(S["product"], m + 1)
                dve.tensor_tensor(b.X[:, m, :], PS[0:P, 2 + m % 4, :], b.X[:, m, :], ALU.add).then_inc(S["added"], 1)

        @block.scalar
        def _(act):
            prenorm_scalar(act, b, S)
            threshold_gates_scalar(act, b, S, G, E)
            for n in range(E * K):
                e, c = divmod(n, K)
                act.wait_ge(S["hidden"], n + 1)
                if e >= 1 and c == 0:
                    act.wait_ge(S["low"], e)
                act.activation(halves(hT[:, c, :]), PS[:, 2 * (n % 3):2 * (n % 3) + 2, 0:HALF], ACT.Relu
                               ).then_inc(S["hidden_out"], 1)

        @block.tensor
        def _(pe):
            prenorm_tensor(pe, b, S)
            pe.wait_ge(S["pre_columns"], TILES)
            pe.wait_ge(loaded, loads)
            logits_tensor(pe, b, S, gate, E + 1)

            def hidden(e):
                for c in range(K):
                    n = e * K + c
                    if n >= 3:
                        pe.wait_ge(S["hidden_out"], n - 2)
                    for h in range(2):
                        at = e * K * D + c * 128
                        last = accumulate(pe, PS[:, 2 * (n % 3) + h, 0:HALF],
                                          [(W[:, at + k * D:at + k * D + 128], b.XT[:, k, h * HALF:(h + 1) * HALF])
                                           for k in range(K)])
                    last.then_inc(S["hidden"], 1)

            def low(e):
                pe.wait_ge(S["hidden_out"], K * (e + 1))
                if e >= 1:
                    pe.wait_ge(S["low_out"], e)
                for m in range(TILES):
                    last = accumulate(pe, PS[0:P, 6, m * R:(m + 1) * R],
                                      [(tile_of(hT, k, m), down[:, e, k, :]) for k in range(K)])
                last.then_inc(S["low"], 1)

            for e in range(E):
                hidden(e)
                low(e)
            pe.wait_ge(S["fc2_in"], 16 * E)
            pe.wait_ge(S["wide"], E + 1)
            pe.wait_ge(S["gate_shifted"], 1)
            accumulate(pe, PS[0:E * R, 7, :],
                       [(up_wide[:, e, k, :], fc2[:, (e * K + k) * D:(e * K + k + 1) * D])
                        for e in range(E) for k in range(K)]).then_inc(S["fused"], 1)
            pe.wait_ge(S["weighted"], TILES)
            for m in range(TILES):
                last = pe.transpose(PS[0:E * R, m // 4, (m % 4) * P:(m % 4 + 1) * P], lw[:, m, :], b.ident[0:P, 0:P])
            last.then_inc(S["low_turned"], 1)
            pe.wait_ge(S["fused_out"], 1)
            pe.wait_ge(S["low_columns"], 2)
            for m in range(TILES):
                if m >= 4:
                    pe.wait_ge(S["added"], m - 3)
                pe.matmul(PS[0:P, 2 + m % 4, :], lT[:, m * P:(m + 1) * P], up_fc2[:, :], start=True, stop=True
                          ).then_inc(S["product"], 1)



class Buffers:

    def __init__(self, nc):
        self.nc, self.part = nc, "all"
        sb = self.sb

        self.ident = sb("ident", [128, 128])
        self.ones = sb("ones", [128, 128])
        self.X = sb("X", [P, TILES, D])
        self.XN = sb("XN", [P, TILES, D])
        self.XT = sb("XT", [128, K, PADDED])
        self.CT = sb("CT", [P, TILES, PADDED])
        self.W = [sb(f"W{n}", [128, 4 * K * D]) for n in range(2)]
        self.V = [sb(f"V{n}", [128, 8 * D]) for n in range(2)]
        self.U = [sb(f"U{n}", [128, 48]) for n in range(2)]
        self.stats = sb("stats", [P, TILES, 2, 6])
        self.mv = sb("mv", [P, TILES, 2])
        self.var = sb("var", [P, TILES])
        self.root = sb("root", [P, TILES])
        self.rstd = sb("rstd", [P, TILES])
        self.nmr = sb("nmr", [P, TILES])
        self.psum = nc.alloc_psum_tensor("PS", [128, 8, BANK], F32)
        self.mixed_dram = nc.dram_tensor("mixed_dram", [2, 128, STEPS * D], F32).ap()
        self.counts_dram = nc.dram_tensor("counts_dram", [3, P, TILES * PADDED], F32).ap()

    def sb(self, name, shape):
        return self.nc.alloc_sbuf_tensor(f"{self.part}_{name}", shape, F32)


def build(nc, t, out):
    b = Buffers(nc)
    loaders = ([lambda sp, s, d, n=n: load_conv(sp, b, t, s, d, n) for n in range(3)] +
               [lambda sp, s, d: load_experts(sp, b, t, s, d, "L0_ffn_W_exp", "L0_ffn_gate", "L0_ffn_gate_bias",
                                              "L0_ffn_b_exp")] +
               [lambda sp, s, d, n=n: load_attention(sp, b, t, s, d, n) for n in range(2)] +
               [lambda sp, s, d: load_experts(sp, b, t, s, d, "L1_ffn_experts", "L1_ffn_gate", None)] +
               [lambda sp, s, d, n=n: load_relations(sp, b, t, s, d, n) for n in range(2)] +
               [lambda sp, s, d: load_top2(sp, b, t, s, d),
                lambda sp, s, d: load_isomorphism(sp, b, t, s, d),
                lambda sp, s, d: load_lora(sp, b, t, s, d)])
    LOADS = [6, 7, 7, 7, 9, 9, 5, 4, 4, 5, 4, 7]
    numbers = iter(range(1 + len(loaders)))
    loaded = [nc.alloc_semaphore(f"loaded_{n}") for n in range(len(loaders))]
    b.counts_loaded = nc.alloc_semaphore("counts_loaded")
    b.relations_loaded = nc.alloc_semaphore("relations_loaded")

    def load_part(n, sp):
        if n < len(loaders):
            assert loaders[n](sp, n % 2, loaded[n]) == LOADS[n]

    def own(n):
        return n % 2, loaded[n], 16 * LOADS[n], lambda sp: load_part(n + 1, sp)

    def run(part, *args):
        with nc.cleanup_on_exit():
            b.part = f"part{next(numbers)}"
            part(nc, b, t, *args)

    run(count_edges, lambda sp: load_part(0, sp))
    for n in range(3):
        run(conv, n, *own(n))
    with nc.sbuf_tensor("log_counts", [P, TILES, PADDED], F32) as C, nc.sbuf_tensor("edged", [P, TILES], F32) as edged:
        slot, done, loads, load_next = own(3)

        def load_counts(sp, load_next=load_next):
            sp.dma_start(C[:, :, :].rearrange("p m n -> p (m n)"), b.counts_dram[0]).then_inc(b.counts_loaded, 16)
            load_next(sp)
        run(ffn_threshold, slot, done, loads, load_counts)
        for n in range(2):
            run(attention, n, *own(4 + n), C, edged)
    with nc.sbuf_tensor("relation_counts", [P, 2, TILES, PADDED], F32) as C2:
        slot, done, loads, load_next = own(6)

        def load_relation_counts(sp, load_next=load_next):
            for r in range(2):
                sp.dma_start(C2[:, r, :, :].rearrange("p m n -> p (m n)"), b.counts_dram[1 + r]
                             ).then_inc(b.relations_loaded, 16)
            load_next(sp)
        run(ffn_sinkhorn, slot, done, loads, load_relation_counts)
        for n in range(2):
            run(relations, n, *own(7 + n), C2)
    run(ffn_top2, *own(9))
    run(isomorphism, *own(10))
    slot, done, loads, _ = own(11)
    run(ffn_lora, slot, done, loads, out)


def columns(v):
    import numpy as np
    v = np.asarray(v)
    v = v.reshape(len(v), -1)
    return np.ascontiguousarray(v.reshape(-1, 128, v.shape[1]).transpose(1, 0, 2).reshape(128, -1))


def laid_out(x):
    import numpy as np
    x = {n: np.ascontiguousarray(a) for n, a in x.items()}
    t = {n: x[n] for n in (
        "x", "src", "dst", "edge_type_2", "L0_gnn_cw", "L0_gnn_cb", "L0_ffn_W_exp", "L0_ffn_b_exp",
        "L1_gnn_ln_g", "L1_gnn_ln_b", "L1_ffn_experts", "L2_gnn_basis1", "L2_gnn_root1", "L2_gnn_bias1",
        "L2_gnn_basis2", "L2_gnn_root2", "L2_gnn_bias2", "L2_ffn_w2", "L2_ffn_b2", "L2_ffn_gamma", "L2_ffn_beta",
        "L3_gnn_W1", "L3_gnn_W2", "L3_gnn_b2")}
    for i in range(3):
        for n in ("mw1", "mb1", "mw2", "mb2") + (("lng", "lnb") if i else ()):
            t[f"L0_gnn_{n}_{i}"] = x[f"L0_gnn_{n}_{i}"]
        t[f"conv_columns{i}"] = np.concatenate(
            [columns(x[f"L0_gnn_mlg_{i}"]), columns(x[f"L0_gnn_mlb_{i}"]), np.tile(x[f"L0_gnn_t{i}"], (128, 1))], axis=1)
    t["L0_ffn_gate"] = columns(np.concatenate([x["L0_ffn_W_gate"], x["L0_ffn_W_thr"]], axis=1))
    t["L0_ffn_gate_bias"] = np.concatenate([x["L0_ffn_b_gate"], x["L0_ffn_b_thr"]])
    for n in "qkvo":
        t[f"att_W{n}"] = np.ascontiguousarray(x[f"L1_gnn_W{n}"].transpose(0, 2, 1))
    t["att_W1"] = np.ascontiguousarray(x["L1_gnn_W1"].transpose(0, 2, 1))
    t["att_W2"] = np.ascontiguousarray(x["L1_gnn_W2"].transpose(0, 2, 1))
    t["att_columns"] = np.stack([np.concatenate(
        [columns(x[f"L1_gnn_{n}"][i]) for n in ("bq", "bo", "b2", "g1", "beta1", "g2", "beta2")] +
        [np.tile(x["L1_gnn_b1"][i], 2)[:, None]], axis=1) for i in range(2)])
    t["L1_ffn_gate"] = columns(x["L1_ffn_gate_w"][0])
    for i in range(2):
        t[f"rel_columns{i}"] = columns(x[f"L2_gnn_gate_w{i + 1}"][:, :, 0].T)
    t["top2_w1"] = np.ascontiguousarray(x["L2_ffn_w1"].transpose(1, 0, 2).reshape(512, 512))
    t["top2_columns"] = np.concatenate([columns(x["L2_ffn_router_w"]), columns(x["L2_ffn_b1"].reshape(-1))], axis=1)
    t["gin_columns"] = columns(x["L3_gnn_b1"])
    t["lora_gate"] = columns(np.concatenate([x["L3_ffn_gate_w"], x["L3_ffn_thr_w"]]).T)
    t["lora_fc1"] = np.ascontiguousarray(x["L3_ffn_fc1_w"].transpose(0, 2, 1))
    t["lora_fc2"] = np.ascontiguousarray(x["L3_ffn_fc2_w"].transpose(0, 2, 1))
    t["lora_down"] = np.concatenate([columns(a) for a in x["L3_ffn_lora_A"]], axis=1)
    t["lora_up"] = np.concatenate([columns(a.T) for a in x["L3_ffn_lora_B"]], axis=1)
    t["ident"] = np.eye(128, dtype=np.float32)
    t["iota"] = np.tile(np.arange(NODES, dtype=np.float16), (P, 1))
    t["quarter"] = np.tile(np.eye(ROWS4, dtype=np.float32), (BASES, 1))
    t["atts"] = np.stack([np.repeat(x[f"L2_gnn_att{i + 1}"].T, ROWS4, axis=0) for i in range(2)], axis=1)
    return t


def kernel(**inputs):
    import numpy as np
    from concourse import bacc
    from concourse.bass_utils import run_bass_kernel_spmd

    nc = bacc.Bacc("TRN2", target_bir_lowering=False, num_devices=1)
    arrays = {f"in_{n}": np.ascontiguousarray(a) for n, a in laid_out(inputs).items()}
    t = {n[3:]: nc.dram_tensor(n, a.shape, mybir.dt.from_np(a.dtype), kind="ExternalInput").ap()
         for n, a in arrays.items()}
    out = nc.dram_tensor("out", [NODES, D], F32, kind="ExternalOutput").ap()
    build(nc, t, out)
    return run_bass_kernel_spmd(nc, [arrays], core_ids=[0]).results[0]["out"]
```

```python
from contextlib import ExitStack

import concourse.bass as bass
from concourse import mybir
from concourse.alu_op_type import AluOpType as ALU

ACT = mybir.ActivationFunctionType
AX = mybir.AxisListType
F32 = mybir.dt.float32
BF16 = mybir.dt.bfloat16
F32R = mybir.dt.float32r
FP16 = mybir.dt.float16
I32 = mybir.dt.int32

NODES = 625
P = 125
TILES = NODES // P
PADDED = 626
HALF = PADDED // 2
EDGES = 20000
CHUNKS = EDGES // P
D = 512
K = D // 128
D2 = 2 * D
BASES = 30
ROWS4 = 4
MIX = BASES * ROWS4
GROUP = 16
STEPS = D // (ROWS4 * GROUP)
BANK = 512
BIG = 1e30


class Semaphores:

    def __init__(self, nc, part):
        self.nc, self.part, self.known = nc, part, {}

    def __getitem__(self, name):
        if name not in self.known:
            self.known[name] = self.nc.alloc_semaphore(f"{self.part}_{name}")
        return self.known[name]


def accumulate(pe, out, pairs):
    for n, (lhsT, rhs) in enumerate(pairs):
        last = pe.matmul(out, lhsT, rhs, start=(n == 0), stop=(n == len(pairs) - 1))
    return last


def tile_of(columns, k, m):
    return columns[:, k, m * P:(m + 1) * P]


def halves(row):
    return row.rearrange("p (h n) -> p h n", h=2)


def spread(ap, n):
    return ap.unsqueeze(2).to_broadcast([ap.shape[0], ap.shape[1], n])



def count_edges(nc, b, t, load_next):
    S = Semaphores(nc, b.part)
    PS = b.psum
    flat = PS.rearrange("p b n -> p (b n)")
    LAYERS = 2
    RADIX_BITS = 12
    RADIX = 1 << RADIX_BITS
    SLOTS = 4
    ROUNDS = STEPS
    ROUND = CHUNKS // ROUNDS
    assert ROUND * P < RADIX and ROUND * P * RADIX < 1 << 24

    def sb(name, shape, dt=F32):
        return nc.alloc_sbuf_tensor(name, shape, dt)

    ids_i = sb("ids_i", [P, 3, CHUNKS], I32)
    ids = sb("ids", [P, 3, CHUNKS])
    iota = sb("iota", [P, NODES], FP16)
    hot_dst = sb("hot_dst", [P, SLOTS, NODES], BF16)
    hot_src = sb("hot_src", [P, SLOTS, NODES], BF16)
    att = sb("att", [MIX, LAYERS, 2])
    quarter = sb("quarter", [MIX, ROWS4])
    ones = sb("ones16", [MIX, 4, 4])
    mixer = sb("mixer", [MIX, LAYERS, GROUP * 32])
    mixed = sb("mixed", [128, STEPS, D])
    count = sb("count", [P, TILES, PADDED])
    packed = count[:, :, :].rearrange("p m n -> p (m n)")[:, 0:TILES * NODES].bitcast(I32)
    upper = sb("upper", [P, TILES * NODES], I32)
    counts_0, counts_1 = (b.V[n][0:P, 0:TILES * PADDED].rearrange("p (m n) -> p m n", m=TILES) for n in range(2))

    pieces = []
    for m in range(TILES):
        at = m * NODES
        while at < (m + 1) * NODES:
            end = min((m + 1) * NODES, (at // BANK + 1) * BANK)
            pieces.append((m, at, end))
            at = end
    count_banks = -(-TILES * NODES // BANK)
    opens = {min(n for n, p in enumerate(pieces) if p[1] // BANK == k) for k in range(count_banks)}
    closes = {max(n for n, p in enumerate(pieces) if p[1] // BANK == k) for k in range(count_banks)}
    PIECES_AT = (8, 13)
    PIECES = len(PIECES_AT)
    SPLIT = 3 * BANK

    with nc.Block() as block:
        @block.sync
        def _(sp):
            for n, name in enumerate(("src", "dst", "edge_type_2")):
                sp.dma_start(ids_i[:, n, :], t[name].rearrange("(p c) -> p c", p=P)).then_inc(S["ids_in"], 16)
            sp.dma_start(iota[:, :], t["iota"]).then_inc(S["ids_in"], 16)
            sp.dma_start(quarter[:, :], t["quarter"]).then_inc(S["att_in"], 16)
            sp.dma_start(att[:, :, :], t["atts"]).then_inc(S["att_in"], 16)
            for layer in range(LAYERS):
                rows = t[f"L2_gnn_basis{layer + 1}"].rearrange("b (t q j) o -> t b q (j o)", t=STEPS, q=ROWS4)
                with sp.Fori(0, STEPS // 2) as i:
                    for h in range(2):
                        sp.wait_ge(S["mixed_full"], STEPS * layer + 2 * i + h + 1)
                        sp.dma_start(b.W[h][0:MIX, :], rows[bass.ds(2 * i + h, 1)].rearrange("a b q n -> (a b) q n")
                                     ).then_inc(S[f"basis_in{h}"], 16)
            sp.dma_start(b.ident[:, :], t["ident"]).then_inc(S["ident_in"], 16)
            sp.dma_start(b.temperatures[:, :], t["temperatures"]).then_inc(S["temperatures_in"], 16)
            sp.dma_start(b.X[:, :, :], t["x"].rearrange("(m p) f -> p m f", p=P)).then_inc(S["ident_in"], 16)
            sp.wait_ge(S["mixed_full"], 2 + LAYERS * STEPS)

            def counts_read():
                sp.wait_ge(S["relations_stored"], 32)
                sp.wait_ge(S["counted"], 1)

            load_next(sp, counts_read)
            sp.wait_ge(S["ident_in"], 32)
            sp.wait_ge(S["temperatures_in"], 16)

        @block.gpsimd
        def _(pool):
            pool.memset(counts_0[:, :, :], 0.0).then_inc(S["no_counts"], 1)
            pool.memset(packed.bitcast(F32), 0.0).then_inc(S["no_counts"], 1)
            pool.memset(counts_1[:, :, :], 0.0).then_inc(S["no_counts"], 1)
            pool.wait_ge(S["no_counts"], 3)

            total = counts_1[:, :, 0:NODES]
            for layer in range(LAYERS):
                with pool.Fori(0, ROUNDS // 2) as i:
                    n = ROUNDS // 2 * layer + i
                    pool.wait_ge(S["upper_cast"], n + 1)
                    pool.tensor_tensor(total, total, upper[:, :].bitcast(F32).rearrange("p (m n) -> p m n", m=TILES),
                                       ALU.add).then_inc(S["upper_added"], 1)
                pool.wait_ge(S["mixed_out"], 1 + STEPS * (layer + 1))
                pool.dma_start(b.mixed_dram[layer].rearrange("(rq cj) n -> cj rq n", rq=2 * ROWS4),
                               mixed[:, :, :].rearrange("p a n -> p (a n)")).then_inc(S["stored"], 16)
                if layer == 0:
                    pool.wait_ge(S["stored"], 16)
                    pool.sem_inc(S["mixed_free"], 1)
            pool.wait_ge(S["upper_added"], 1 + ROUNDS)
            pool.wait_ge(S["lower_added"], PIECES * (ROUNDS + 1))
            for n, c in enumerate((counts_0, counts_1)):
                pool.dma_start(b.counts_dram[1 + n], c.rearrange("p m n -> p (m n)")).then_inc(S["relations_stored"], 16)
            pool.wait_ge(S["stored"], 16 * LAYERS)
            pool.wait_ge(S["relations_stored"], 32)
            pool.wait_ge(S["total_stored"], 16)

        @block.vector
        def _(dve):
            dve.memset(mixer[:, :, :], 0.0).then_inc(S["blank"], 1)
            dve.memset(ones[:, :, :], 1.0).then_inc(S["blank"], 1)
            dve.wait_ge(S["ids_in"], 64)
            dve.tensor_copy(ids[:, 0:2, :], ids_i[:, 0:2, :]).then_inc(S["ids_cast"], 1)
            dve.tensor_scalar(ids[:, 2, :], ids_i[:, 2, :], 0.0, float(RADIX - 1), ALU.not_equal, ALU.mult
                              ).then_inc(S["ids_cast"], 1)
            dve.wait_ge(S["ids_cast"], 2)
            dve.tensor_scalar(ids[:, 2, :], ids[:, 2, :], 1.0, None, ALU.add).then_inc(S["ids_cast"], 1)
            dve.wait_ge(S["att_in"], 32)
            dve.wait_ge(S["blank"], 2)
            for layer in range(LAYERS):
                for r in range(2):
                    for q in range(ROWS4):
                        first = ROWS4 * r + q
                        by_tile = mixer[:, layer, :].rearrange("p (c n) -> p c n", c=4)
                        dve.tensor_scalar(by_tile[:, :, first:first + 3 * 40 + 1:40], ones[:, :, :],
                                          quarter[:, q:q + 1], att[:, layer, r:r + 1], ALU.mult, ALU.mult
                                          ).then_inc(S["mixer_made"], 1)
            def add_lower(piece):
                tiles = (slice(0, 3), slice(3, TILES))[piece]
                part = packed.bitcast(F32).rearrange("p (m n) -> p m n", m=TILES)
                dve.tensor_tensor(counts_0[:, tiles, 0:NODES], counts_0[:, tiles, 0:NODES], part[:, tiles, :], ALU.add
                                  ).then_inc(S["lower_added"], 1)

            dve.wait_ge(S["no_counts"], 3)
            dve.wait_ge(S["ids_cast"], 3)
            for layer in range(LAYERS):
                with dve.Fori(0, ROUNDS // 2) as i:
                    n = ROUNDS // 2 * layer + i
                    for j in range(ROUND):
                        c = ROUND * n + j
                        slot = j % SLOTS
                        dve.wait_ge(S["hot_free"], c + 1)
                        dve.tensor_scalar(hot_dst[:, slot, :], iota[:, :], ids[:, 1, bass.ds(c, 1)], None,
                                          ALU.is_equal).then_inc(S["hot_ready"], 1)
                        dve.tensor_scalar(hot_src[:, slot, :], iota[:, :], ids[:, 0, bass.ds(c, 1)],
                                          ids[:, 2, bass.ds(c, 1)], ALU.is_equal, ALU.mult).then_inc(S["hot_ready"], 1)
                        if j in PIECES_AT:
                            dve.wait_ge(S["lower_cast"], n + 1)
                            add_lower(PIECES_AT.index(j))
                    dve.wait_ge(S["hot_free"], SLOTS + ROUND * (n + 1))
                    dve.wait_ge(S["lower_added"], PIECES * (n + 1))
                    dve.tensor_copy(packed[:, 0:SPLIT], flat[0:P, 0:SPLIT]).then_inc(S["unpacked"], 1)
                    dve.wait_ge(S["unpacked"], 2 + 2 * (n + 1))
                    dve.wait_ge(S["upper_added"], n + 1)
                    dve.tensor_scalar(upper[:, :], packed, RADIX_BITS, None, ALU.logical_shift_right
                                      ).then_inc(S["upper"], 1)
                    dve.wait_ge(S["upper"], n + 1)
                    dve.tensor_scalar(packed, packed, RADIX - 1, None, ALU.bitwise_and
                                      ).then_inc(S["lower"], 1)
            dve.memset(b.CT[:, :, NODES:], 0.0).then_inc(S["blank"], 1)
            dve.memset(b.XT[:, :, NODES:], 0.0).then_inc(S["blank"], 1)
            dve.memset(b.ones[:, :], 1.0).then_inc(S["blank"], 1)
            dve.wait_ge(S["ident_in"], 32)
            for m in range(TILES):
                begin_stats(dve, b, S, "pre", m, [b.X[:, m, :]])
                if m >= 1:
                    input_scale(dve, b, S, m - 1)
            input_scale(dve, b, S, TILES - 1)
            dve.wait_ge(S["lower_cast"], ROUNDS + 1)
            for piece in range(PIECES):
                add_lower(piece)
            dve.wait_ge(S["lower_added"], PIECES * (ROUNDS + 1))
            dve.wait_ge(S["upper_added"], 1 + ROUNDS)
            dve.memset(count[:, :, NODES:], 0.0).then_inc(S["blank"], 1)
            dve.tensor_tensor(count[:, :, 0:NODES], counts_0[:, :, 0:NODES], counts_1[:, :, 0:NODES], ALU.add
                              ).then_inc(S["counted"], 1)
            for m in range(TILES):
                dve.wait_ge(S["pre_rows"], m + 1)
                row_extremes(dve, b, S, m)

        @block.scalar
        def _(act):
            for layer in range(LAYERS):
                if layer == 1:
                    act.wait_ge(S["mixed_free"], 1)
                with act.Fori(0, ROUNDS // 2) as i:
                    n = ROUNDS // 2 * layer + i
                    act.wait_ge(S["hot_free"], SLOTS + ROUND * (n + 1))
                    act.wait_ge(S["lower_added"], PIECES * (n + 1))
                    act.activation(packed[:, SPLIT:], flat[0:P, SPLIT:TILES * NODES], ACT.Copy).then_inc(S["unpacked"], 1)
                    for h in range(2):
                        step = 2 * i + h
                        act.wait_ge(S["mixed_full"], 2 + STEPS * layer + step + 1)
                        act.activation(mixed[:, bass.ds(step, 1), :], PS[:, count_banks:count_banks + 1, :], ACT.Copy
                                       ).then_inc(S["mixed_out"], 1)
                    act.wait_ge(S["upper"], n + 1)
                    act.wait_ge(S["lower"], n + 1)
                    act.activation(upper[:, :].bitcast(F32), upper[:, :], ACT.Copy).then_inc(S["upper_cast"], 1)
                    act.activation(packed.bitcast(F32), packed, ACT.Copy).then_inc(S["lower_cast"], 1)
            input_columns(act, b, S, lambda m: m, 1)
            act.wait_ge(S["counted"], 1)
            act.wait_ge(S["blank"], 6)
            act.dma_start(b.counts_dram[0], count[:, :, :].rearrange("p m n -> p (m n)")).then_inc(S["total_stored"], 16)
            for s in range(TILES):
                act.wait_ge(S["turned"], s + 1)
                act.activation(b.CT[:, s, 0:4 * P], PS[0:P, s, 0:4 * P], ACT.Copy).then_inc(S["ct_out"], 1)
            act.wait_ge(S["turned"], 2 * TILES)
            act.activation(b.CT[:, 0:4, 4 * P:5 * P], PS[0:P, TILES, 0:4 * P].rearrange("p (s n) -> p s n", s=4),
                           ACT.Copy).then_inc(S["ct_out"], 1)
            act.activation(b.CT[:, 4, 4 * P:5 * P], PS[0:P, TILES + 1, 0:P], ACT.Copy).then_inc(S["ct_out"], 1)

        @block.tensor
        def _(pe):
            pe.sem_inc(S["hot_free"], SLOTS)
            pe.sem_inc(S["mixed_full"], 2)
            pe.sem_inc(S["mixed_out"], 1)
            pe.sem_inc(S["upper_added"], 1)
            pe.sem_inc(S["lower_cast"], 1)
            pe.sem_inc(S["unpacked"], 2)
            pe.wait_ge(S["mixer_made"], LAYERS * 2 * ROWS4)
            for layer in range(LAYERS):
                with pe.Fori(0, ROUNDS // 2) as i:
                    n = ROUNDS // 2 * layer + i
                    pe.wait_ge(S["unpacked"], 2 + 2 * n)
                    for j in range(ROUND):
                        slot = j % SLOTS
                        pe.wait_ge(S["hot_ready"], 2 * (ROUND * n + j + 1))
                        for at_piece, (m, at, end) in enumerate(pieces):
                            last = pe.matmul(flat[0:P, at:end], hot_dst[:, slot, m * P:(m + 1) * P],
                                             hot_src[:, slot, at - m * NODES:end - m * NODES],
                                             start=(j == 0 and at_piece in opens),
                                             stop=(j == ROUND - 1 and at_piece in closes), skip_group_check=True)
                        last.then_inc(S["hot_free"], 1)
                    for h in range(2):
                        step = 2 * i + h
                        pe.wait_ge(S[f"basis_in{h}"], 16 * (STEPS // 2 * layer + i + 1))
                        pe.wait_ge(S["mixed_out"], 1 + STEPS * layer + step)
                        for jj in range(4):
                            for c in range(4):
                                g = 4 * c + jj
                                last = pe.matmul(PS[32 * c:32 * c + 32, count_banks, :], mixer[:, layer, g * 32:(g + 1) * 32],
                                                 b.W[h][0:MIX, g * D:(g + 1) * D], start=(jj == 0), stop=(jj == 3))
                        last.then_inc(S["mixed_full"], 1)
            pe.wait_ge(S["ident_in"], 32)
            pe.wait_ge(S["unpacked"], 2 + 2 * ROUNDS)
            for m in range(TILES):
                input_turn(pe, b, S, m, m)
            pe.wait_ge(S["pre_columns"], TILES)
            pe.wait_ge(S["counted"], 1)
            for s in range(TILES):
                for d in range(4):
                    last = pe.transpose(PS[0:P, s, d * P:(d + 1) * P], count[:, d, s * P:(s + 1) * P], b.ident[0:P, 0:P])
                last.then_inc(S["turned"], 1)
            for s in range(TILES):
                pe.transpose(PS[0:P, TILES + s // 4, (s % 4) * P:(s % 4 + 1) * P], count[:, 4, s * P:(s + 1) * P],
                             b.ident[0:P, 0:P]).then_inc(S["turned"], 1)




def input_rows(dve, b, S, m):
    begin_stats(dve, b, S, "pre", m, [b.X[:, m, :]])
    input_scale(dve, b, S, m)


def input_scale(dve, b, S, m):
    end_stats(dve, b, S, "pre", m)
    dve.tensor_scalar(b.XN[:, m, :], b.X[:, m, :], b.mv[:, m, 0:1], b.rstd[:, m:m + 1], ALU.subtract, ALU.mult
                      ).then_inc(S["pre_rows"], 1)


def row_extremes(dve, b, S, m):
    dve.tensor_reduce(b.extremes[:, m, 0:1], b.XN[:, m, :], AX.X, ALU.max).then_inc(S["x_extremes"], 1)
    dve.tensor_reduce(b.extremes[:, m, 1:2], b.XN[:, m, :], AX.X, ALU.min).then_inc(S["x_extremes"], 1)


def input_turn(pe, b, S, m, bank):
    pe.wait_ge(S["pre_rows"], m + 1)
    for k in range(K):
        last = pe.transpose(b.psum[:, bank, k * P:(k + 1) * P], b.XN[:, m, k * 128:(k + 1) * 128], b.ident[0:P, 0:P])
    last.then_inc(S["pre_turned"], 1)


def input_columns(act, b, S, bank_of, lag):
    for m in range(TILES + lag):
        if m < TILES:
            tile_root(act, b, S, "pre", m)
        if m >= lag:
            input_column(act, b, S, m - lag, bank_of(m - lag))


def input_column(act, b, S, m, bank):
    act.wait_ge(S["pre_turned"], m + 1)
    act.activation(b.XT[:, :, m * P:(m + 1) * P], b.psum[:, bank, 0:K * P].rearrange("p (k n) -> p k n", k=K), ACT.Copy
                   ).then_inc(S["pre_columns"], 1)


def row_stats(dve, b, S, tag, views):
    n = len(views[0])
    for m in range(TILES):
        for h in range(n):
            dve.bn_stats(b.stats[:, m, h, :], views[m][h]).then_inc(S[tag + "_stats"], 1)
    dve.wait_ge(S[tag + "_stats"], n * TILES)
    for m in range(TILES):
        dve.bn_aggr(b.mv[:, m, :], b.stats[:, m, 0:n, :].rearrange("p h s -> p (h s)")).then_inc(S[tag + "_aggr"], 1)
    dve.wait_ge(S[tag + "_aggr"], TILES)
    dve.tensor_scalar(b.var[:, :], b.mv[:, :, 1], 1e-5, None, ALU.add).then_inc(S[tag + "_var"], 1)
    dve.wait_ge(S[tag + "_root"], 1)
    dve.reciprocal(b.rstd[:, :], b.root[:, :]).then_inc(S[tag + "_rstd"], 1)
    dve.wait_ge(S[tag + "_rstd"], 1)


def tile_stats(dve, b, S, tag, m, views):
    begin_stats(dve, b, S, tag, m, views)
    end_stats(dve, b, S, tag, m)


def begin_stats(dve, b, S, tag, m, views):
    for h, view in enumerate(views):
        dve.bn_stats(b.stats[:, m, h, :], view).then_inc(S[tag + "_stats"], 1)
    dve.wait_ge(S[tag + "_stats"], len(views) * (m + 1))
    dve.bn_aggr(b.mv[:, m, :], b.stats[:, m, 0:len(views), :].rearrange("p h s -> p (h s)")).then_inc(S[tag + "_aggr"], 1)
    dve.wait_ge(S[tag + "_aggr"], m + 1)
    dve.tensor_scalar(b.var[:, m:m + 1], b.mv[:, m, 1:2], 1e-5, None, ALU.add).then_inc(S[tag + "_var"], 1)


def end_stats(dve, b, S, tag, m):
    dve.wait_ge(S[tag + "_root"], m + 1)
    dve.reciprocal(b.rstd[:, m:m + 1], b.root[:, m:m + 1]).then_inc(S[tag + "_rstd"], 1)
    dve.wait_ge(S[tag + "_rstd"], m + 1)


def tile_root(act, b, S, tag, m):
    act.wait_ge(S[tag + "_var"], m + 1)
    act.activation(b.root[:, m:m + 1], b.var[:, m:m + 1], ACT.Sqrt).then_inc(S[tag + "_root"], 1)


def row_root(act, b, S, tag):
    act.wait_ge(S[tag + "_var"], 1)
    act.activation(b.root[:, :], b.var[:, :], ACT.Sqrt).then_inc(S[tag + "_root"], 1)


def column_vectors(b, slot, names):
    out, at = {}, 0
    for name, n in names:
        out[name] = b.U[slot][:, at:at + n]
        at += n
    return out



def load_conv(sp, b, t, slot, done, layer, rows_free=None):
    W, V = b.W[slot], b.V[slot]
    sp.dma_start(W[:, 0:K * D2].rearrange("p (k n) -> p k n", k=K),
                 t[f"L0_gnn_mw1_{layer}"].rearrange("(k p) n -> p k n", p=128)).then_inc(done, 16)
    sp.dma_start(W[:, K * D2:].rearrange("p (k n) -> p k n", k=2 * K),
                 t[f"L0_gnn_mw2_{layer}"].rearrange("(k p) n -> p k n", p=128)).then_inc(done, 16)
    sp.dma_start(b.U[slot][:, 0:4 * K], t[f"conv_columns{layer}"]).then_inc(done, 16)
    if rows_free:
        rows_free()
    rows = [(f"L0_gnn_mb1_{layer}", 0), (f"L0_gnn_mb2_{layer}", D2)]
    rows += [("L0_gnn_cb", D2 + D)] if layer == 0 else [(f"L0_gnn_lng_{layer}", D2 + D), (f"L0_gnn_lnb_{layer}", D2 + 2 * D)]
    for name, at in rows:
        sp.dma_start(V[:, at:at + t[name].shape[0]], t[name].partition_broadcast(128)).then_inc(done, 16)
    return 3 + len(rows)


def load_experts(sp, b, t, slot, done, weights, columns, rows, bias=None):
    for e in range(4):
        sp.dma_start(b.W[slot][:, e * K * D:(e + 1) * K * D].rearrange("p (k n) -> p k n", k=K),
                     t[weights][e].rearrange("(k p) n -> p k n", p=128)).then_inc(done, 16)
    sp.dma_start(b.U[slot][:, 0:t[columns].shape[1]], t[columns]).then_inc(done, 16)
    n = 5
    if rows:
        sp.dma_start(b.V[slot][:, 0:t[rows].shape[0]], t[rows].partition_broadcast(128)).then_inc(done, 16)
        n += 1
    if bias:
        sp.dma_start(b.V[slot][0:8, D:2 * D], t[bias]).then_inc(done, 16)
        n += 1
    return n


def load_attention(sp, b, t, slot, done, layer):
    W, V = b.W[slot], b.V[slot]
    for n, name in enumerate(("q", "k", "v", "o")):
        sp.dma_start(W[:, n * K * D:(n + 1) * K * D].rearrange("p (k n) -> p k n", k=K),
                     t[f"att_W{name}"][layer].rearrange("(k p) n -> p k n", p=128)).then_inc(done, 16)
    sp.dma_start(V[:, 0:256].rearrange("p (k n) -> p k n", k=K),
                 t["att_W1"][layer].rearrange("(k p) n -> p k n", p=128)).then_inc(done, 16)
    sp.dma_start(V[0:64, 256:768], t["att_W2"][layer]).then_inc(done, 16)
    sp.dma_start(b.U[slot][:, 0:29], t["att_columns"][layer]).then_inc(done, 16)
    for name, at in (("L1_gnn_ln_g", 1024), ("L1_gnn_ln_b", 1536)):
        sp.dma_start(V[:, at:at + D], t[name].partition_broadcast(128)).then_inc(done, 16)
    return 9


def load_relations(sp, b, t, slot, done, layer):
    W = b.W[slot]
    sp.dma_start(W[:, 0:STEPS * D], b.mixed_dram[layer]).then_inc(done, 16)
    sp.dma_start(W[:, STEPS * D:STEPS * D + K * D].rearrange("p (k n) -> p k n", k=K),
                 t[f"L2_gnn_root{layer + 1}"].rearrange("(k p) n -> p k n", p=128)).then_inc(done, 16)
    sp.dma_start(b.U[slot][:, 0:2 * K], t[f"rel_columns{layer}"]).then_inc(done, 16)
    sp.dma_start(b.V[slot][:, 0:D], t[f"L2_gnn_bias{layer + 1}"].partition_broadcast(128)).then_inc(done, 16)
    return 4


def load_top2(sp, b, t, slot, done):
    W = b.W[slot]
    sp.dma_start(W[:, 0:K * D].rearrange("p (k n) -> p k n", k=K),
                 t["top2_w1"].rearrange("(k p) n -> p k n", p=128)).then_inc(done, 16)
    sp.dma_start(W[:, K * D:2 * K * D].rearrange("p (k n) -> p k n", k=K),
                 t["L2_ffn_w2"].rearrange("(a c) f o -> (c f) a o", c=2)).then_inc(done, 16)
    sp.dma_start(W[:, 2 * K * D:2 * K * D + D], t["top2_b2"]).then_inc(done, 16)
    sp.dma_start(b.V[slot][:, :], t["L2_ffn_gamma"].rearrange("e n -> (e n)").partition_broadcast(128)
                 ).then_inc(done, 16)
    sp.dma_start(b.U[slot][:, 0:9 * K], t["top2_columns"]).then_inc(done, 16)
    return 5


def load_isomorphism(sp, b, t, slot, done):
    for n in range(2):
        sp.dma_start(b.W[slot][:, n * K * D:(n + 1) * K * D].rearrange("p (k n) -> p k n", k=K),
                     t[f"L3_gnn_W{n + 1}"].rearrange("(k p) n -> p k n", p=128)).then_inc(done, 16)
    sp.dma_start(b.U[slot][:, 0:K], t["gin_columns"]).then_inc(done, 16)
    sp.dma_start(b.V[slot][:, 0:D], t["L3_gnn_b2"].partition_broadcast(128)).then_inc(done, 16)
    return 4


def load_lora(sp, b, t, slot, done):
    for e in range(4):
        sp.dma_start(b.W[slot][:, e * K * D:(e + 1) * K * D].rearrange("p (k n) -> p k n", k=K),
                     t["lora_fc1"][e].rearrange("(k p) n -> p k n", p=128)).then_inc(done, 16)
    sp.dma_start(b.U[slot][:, 0:5 * K], t["lora_gate"]).then_inc(done, 16)
    sp.dma_start(b.V[slot][:, 0:256], t["lora_down"]).then_inc(done, 16)
    sp.dma_start(b.V[slot][:, 256:512], t["lora_up"]).then_inc(done, 16)
    return 7



def conv(nc, b, t, layer, slot, loaded, loads, load_next):
    S = Semaphores(nc, b.part)
    PS = b.psum
    W, V = b.W[slot], b.V[slot]
    w1 = W[:, 0:K * D2].rearrange("p (k n) -> p k n", k=K)
    w2 = W[:, K * D2:].rearrange("p (k n) -> p k n", k=2 * K)
    b1, b2 = V[0:P, 0:D2], V[0:P, D2:D2 + D]
    cb = lng = V[0:P, D2 + D:D2 + 2 * D]
    lnb = V[0:P, D2 + 2 * D:D2 + 3 * D]
    cols = column_vectors(b, slot, [("g", 2 * K), ("b", 2 * K)])
    temperature = b.temperatures[0:P, layer:layer + 1]

    M = b.sb("messages", [P, TILES, D])
    EE128 = b.sb("weights_and_weighted", [128, TILES, D2])
    EE = EE128[0:P, :, :]
    hT = b.sb("h_columns", [128, K, PADDED])
    H2T = b.sb("hidden_columns", [128, 2 * K, NODES])
    den = V[:, 6 * D:6 * D + PADDED]
    cw = b.sb("cw", [128, K, D])
    ext = b.sb("extremes", [P, 8])
    corner = b.sb("extremes_on_diagonal", [2, 2])
    wide = b.nc.alloc_sbuf_tensor(f"{b.part}_wide", [P, 1], I32)
    H1 = EE

    WIDE = 60.0
    by_feature = EE128[:, :, :].rearrange("p a n -> p (a n)")
    zT = by_feature[:, 0:K * NODES].rearrange("p (k n) -> p k n", k=K)
    mT = by_feature[:, K * NODES:2 * K * NODES].rearrange("p (k n) -> p k n", k=K)
    row, no_edge = H2T[:, 0, :], H2T[:, 1, :]
    own_e = H2T[:, 2:2 + K, :]
    own = [H2T[:, 2 + K, n * K:(n + 1) * K] for n in range(4)]
    row_counts = b.counts_dram[0].rearrange("p (m n) -> m p n", m=TILES)

    def own_max_sync(sp):
        sp.wait_ge(S["wide"], 1)
        flag = sp.value_load(wide[0:1, 0:1], min_val=0, max_val=1)
        with sp.If(flag):
            with sp.Fori(0, TILES) as m:
                with sp.Fori(0, P) as p:
                    sp.wait_ge(S["own_wanted"], P * m + p + 1)
                    sp.dma_start(row, row_counts[bass.ds(m, 1), bass.ds(p, 1), 0:NODES].rearrange("m p n -> (m p n)")
                                 .partition_broadcast(128)).then_inc(S["own_row"], 16)

    def own_max_scalar(act):
        act.wait_ge(S["wide"], 1)
        flag = act.value_load(wide[0:1, 0:1], min_val=0, max_val=1)
        with act.If(flag):
            with act.Fori(0, NODES) as d:
                act.wait_ge(S["own_top"], d + 1)
                for c in range(K):
                    act.activation(own_e[:, c, :], own_e[:, c, :], ACT.Exp, bias=own[0][:, c:c + 1]
                                   ).then_inc(S["own_exp"], 1)

    def own_max_vector(dve):
        flag = dve.value_load(wide[0:1, 0:1], min_val=0, max_val=1)
        with dve.If(flag):
            dve.tensor_scalar(mT, b.XT[:, :, 0:NODES], 0.0, 1e-7, ALU.max, ALU.add).then_inc(S["own_messages"], 1)
            dve.wait_ge(S["own_messages"], 1)
            dve.tensor_scalar(zT, mT, b.temperatures[:, layer:layer + 1], None, ALU.mult).then_inc(S["own_messages"], 1)
            dve.wait_ge(S["own_messages"], 2)
            dve.sem_inc(S["own_wanted"], 1)
            with dve.Fori(0, TILES) as m:
                with dve.Fori(0, P) as p:
                    d = P * m + p
                    dve.wait_ge(S["own_row"], 16 * (d + 1))
                    dve.tensor_scalar(no_edge, row, 0.0, -BIG, ALU.is_equal, ALU.mult).then_inc(S["own_mask"], 1)
                    dve.wait_ge(S["own_mask"], d + 1)
                    dve.tensor_tensor(own_e, zT, no_edge.unsqueeze(1).to_broadcast([128, K, NODES]), ALU.add
                                      ).then_inc(S["own_scores"], 1)
                    dve.wait_ge(S["own_scores"], d + 1)
                    dve.tensor_reduce(own[0], own_e, AX.X, ALU.max).then_inc(S["own_max"], 1)
                    dve.wait_ge(S["own_max"], d + 1)
                    dve.tensor_scalar(own[0], own[0], -1.0, None, ALU.mult).then_inc(S["own_top"], 1)
                    dve.wait_ge(S["own_exp"], K * (d + 1))
                    dve.tensor_tensor(own_e, own_e, row.unsqueeze(1).to_broadcast([128, K, NODES]), ALU.mult
                                      ).then_inc(S["own_counted"], 1)
                    dve.wait_ge(S["own_counted"], d + 1)
                    dve.tensor_reduce(own[1], own_e, AX.X, ALU.add).then_inc(S["own_den"], 1)
                    dve.wait_ge(S["own_den"], d + 1)
                    dve.tensor_tensor(own_e, own_e, mT, ALU.mult).then_inc(S["own_weighted"], 1)
                    dve.wait_ge(S["own_weighted"], d + 1)
                    dve.tensor_reduce(own[2], own_e, AX.X, ALU.add).then_inc(S["own_num"], 1)
                    dve.tensor_scalar(own[1], own[1], 1e-37, None, ALU.max).then_inc(S["own_step"], 1)
                    dve.wait_ge(S["own_step"], 4 * d + 1)
                    dve.reciprocal(own[1], own[1]).then_inc(S["own_step"], 1)
                    dve.wait_ge(S["own_step"], 4 * d + 2)
                    dve.wait_ge(S["own_num"], d + 1)
                    dve.tensor_tensor(own[3], own[2], own[1], ALU.mult).then_inc(S["own_step"], 1)
                    dve.wait_ge(S["own_step"], 4 * d + 3)
                    dve.tensor_tensor(hT[:, :, bass.ds(d, 1)], own[3].unsqueeze(2), b.XT[:, :, bass.ds(d, 1)], ALU.add
                                      ).then_inc(S["own_step"], 1)
                    dve.wait_ge(S["own_step"], 4 * d + 4)
                    dve.sem_inc(S["own_wanted"], 1)
        dve.sem_inc(S["h_final"], 1)

    with nc.Block() as block:
        @block.sync
        def _(sp):
            sp.dma_start(cw[:, :, :], t["L0_gnn_cw"][layer * D:(layer + 1) * D, :].rearrange("(k p) n -> p k n", p=128)
                         ).then_inc(S["cw_in"], 16)
            load_next(sp)
            own_max_sync(sp)

        @block.gpsimd
        def _(pool):
            for m in range(TILES):
                pool.tensor_scalar(M[:, m, :], b.XN[:, m, :], 0.0, 1e-7, ALU.max, ALU.add).then_inc(S["messages"], 1)

        @block.vector
        def _(dve):
            dve.tensor_reduce(ext[:, 0:1], b.extremes[:, :, 0], AX.X, ALU.max).then_inc(S["ext"], 1)
            dve.tensor_reduce(ext[:, 1:2], b.extremes[:, :, 1], AX.X, ALU.min).then_inc(S["ext"], 1)
            dve.wait_ge(S["ext"], 2)
            dve.tensor_scalar(ext[:, 0:2], ext[:, 0:2], 0.0, 1e-7, ALU.max, ALU.add).then_inc(S["ext"], 1)
            dve.wait_ge(S["ext"], 3)
            dve.tensor_scalar(ext[:, 2:4], ext[:, 0:2], temperature, None, ALU.mult).then_inc(S["ext"], 1)
            dve.wait_ge(S["ext"], 4)
            dve.tensor_tensor(ext[:, 4:5], ext[:, 2:3], ext[:, 3:4], ALU.max).then_inc(S["ext_tile"], 1)
            dve.scalar_tensor_tensor(ext[:, 5:6], ext[:, 2:3], -1.0, ext[:, 3:4], ALU.mult, ALU.subtract
                                     ).then_inc(S["ext_tile"], 1)
            dve.wait_ge(S["ext_tile"], 2)
            dve.tensor_tensor(ext[:, 5:6], ext[:, 5:6], ext[:, 4:5], ALU.add).then_inc(S["ext_tile"], 1)
            dve.wait_ge(S["ext_turned"], 1)
            dve.tensor_reduce(ext[0:2, 6:7], PS[0:2, 7, 0:P], AX.X, ALU.max).then_inc(S["ext_all"], 1)
            dve.wait_ge(S["ext_all"], 1)
            dve.tensor_scalar(corner[:, :], b.ident[0:2, 0:2], ext[0:2, 6:7], None, ALU.mult).then_inc(S["ext_all"], 1)
            dve.wait_ge(S["ext_everywhere"], 1)
            dve.tensor_scalar(ext[:, 7:8], PS[0:P, 7, 256:257], -1.0, None, ALU.mult).then_inc(S["shift"], 1)
            dve.tensor_scalar(ext[:, 4:5], PS[0:P, 7, 257:258], -WIDE, None, ALU.add).then_inc(S["shift"], 1)
            dve.wait_ge(S["shift"], 2)
            dve.tensor_tensor(wide[:, :], ext[:, 4:5], ext[:, 7:8], ALU.is_gt).then_inc(S["wide"], 1)
            for m in range(TILES):
                dve.wait_ge(S["messages"], m + 1)
                dve.wait_ge(S["weights"], m + 1)
                dve.tensor_tensor(EE[:, m, D:], EE[:, m, 0:D], M[:, m, :], ALU.mult).then_inc(S["weighted"], 1)
            for c in range(K):
                bank = 4 * (c % 2)
                dve.wait_ge(S["denominators"], c + 1)
                dve.tensor_scalar(halves(den), PS[:, bank:bank + 2, 0:HALF], 1e-37, None, ALU.max
                                  ).then_inc(S["den"], 1)
                dve.wait_ge(S["den"], 2 * c + 1)
                dve.reciprocal(den, den).then_inc(S["den"], 1)
                dve.wait_ge(S["numerators"], c + 1)
                dve.wait_ge(S["den"], 2 * c + 2)
                dve.tensor_tensor(halves(hT[:, c, :]), PS[:, bank + 2:bank + 4, 0:HALF], halves(den), ALU.mult
                                  ).then_inc(S["agg"], 1)
                dve.wait_ge(S["agg"], c + 1)
                dve.tensor_tensor(hT[:, c, :], hT[:, c, :], b.XT[:, c, :], ALU.add).then_inc(S["h"], 1)
            own_max_vector(dve)
            dve.wait_ge(loaded, loads)
            for m in range(TILES):
                dve.wait_ge(S["up"], m + 1)
                bank = 2 * (m % 2)
                dve.tensor_tensor(H1[:, m, :].rearrange("p (a n) -> p a n", a=2), PS[0:P, bank:bank + 2, :],
                                  b1.rearrange("p (a n) -> p a n", a=2), ALU.add).then_inc(S["up_out"], 1)
                dve.wait_ge(S["up_out"], m + 1)
                tile_stats(dve, b, S, "mid", m, [H1[:, m, 0:D], H1[:, m, D:]])
                dve.scalar_tensor_tensor(b.nmr[:, m:m + 1], b.mv[:, m, 0:1], -1.0, b.rstd[:, m:m + 1], ALU.mult, ALU.mult
                                         ).then_inc(S["mid_nmr"], 1)
                if layer == 0:
                    dve.tensor_tensor(b.X[:, m, :], b.X[:, m, :], cb, ALU.add).then_inc(S["cb"], 1)
            for m in range(TILES):
                dve.wait_ge(S["down"], m + 1)
                if layer == 0:
                    dve.tensor_tensor(b.XN[:, m, :], PS[0:P, 6 + m % 2, :], b2, ALU.add).then_inc(S["x_rows"], 1)
                else:
                    G = H1[:, m, 0:D]
                    dve.tensor_tensor(G, PS[0:P, 6 + m % 2, :], b2, ALU.add).then_inc(S["down_out"], 1)
                    dve.wait_ge(S["down_out"], m + 1)
                    tile_stats(dve, b, S, "out", m, [G])
                    dve.tensor_scalar(G, G, b.mv[:, m, 0:1], b.rstd[:, m:m + 1], ALU.subtract, ALU.mult
                                      ).then_inc(S["out_norm"], 1)
                    dve.wait_ge(S["out_norm"], m + 1)
                    dve.tensor_tensor(G, G, lng, ALU.mult).then_inc(S["out_gain"], 1)
                    dve.wait_ge(S["out_gain"], m + 1)
                    dve.tensor_tensor(G, G, lnb, ALU.add).then_inc(S["out_shift"], 1)
                    dve.wait_ge(S["out_shift"], m + 1)
                    dve.scalar_tensor_tensor(b.XN[:, m, :], G, 0.0, b.XN[:, m, :], ALU.max, ALU.add
                                             ).then_inc(S["x_rows"], 1)
                if layer < 2:
                    dve.wait_ge(S["x_rows"], m + 1)
                    row_extremes(dve, b, S, m)
            for m in range(TILES):
                dve.wait_ge(S["share"], m + 1)
                dve.tensor_tensor(b.X[:, m, :], PS[0:P, 2 + m % 4, :], b.X[:, m, :], ALU.add).then_inc(S["share_out"], 1)
                if layer == 2:
                    dve.wait_ge(S["share_out"], m + 1)
                    input_rows(dve, b, S, m)

        @block.scalar
        def _(act):
            act.wait_ge(S["shift"], 1)
            for m in range(TILES):
                act.wait_ge(S["messages"], m + 1)
                act.activation(EE[:, m, 0:D], M[:, m, :], ACT.Exp, bias=ext[:, 7:8], scale=temperature
                               ).then_inc(S["weights"], 1)
            own_max_scalar(act)
            act.wait_ge(loaded, loads)

            def hidden_columns(m):
                act.wait_ge(S["mid_turned"], m + 1)
                for k in range(2 * K):
                    act.activation(H2T[:, k, m * P:(m + 1) * P], PS[:, 4 + k // 4, (k % 4) * P:(k % 4 + 1) * P], ACT.Relu,
                                   bias=cols["b"][:, k:k + 1], scale=cols["g"][:, k:k + 1]).then_inc(S["hidden"], 1)

            for m in range(TILES):
                tile_root(act, b, S, "mid", m)
                act.wait_ge(S["mid_nmr"], m + 1)
                act.activation(H1[:, m, :], H1[:, m, :], ACT.Identity, bias=b.nmr[:, m:m + 1], scale=b.rstd[:, m:m + 1]
                               ).then_inc(S["mid_norm"], 1)
                if m >= 1:
                    hidden_columns(m - 1)
            hidden_columns(TILES - 1)
            for m in range(TILES + 1):
                if layer > 0 and m < TILES:
                    tile_root(act, b, S, "out", m)
                if m >= 1:
                    act.wait_ge(S["x_turned"], m)
                    act.activation(b.XT[:, :, (m - 1) * P:m * P],
                                   PS[:, (m - 1) % 2, 0:K * P].rearrange("p (k n) -> p k n", k=K), ACT.Copy
                                   ).then_inc(S["x_columns"], 1)
            if layer == 2:
                input_columns(act, b, S, lambda m: 6 + m % 2, 1)

        @block.tensor
        def _(pe):
            pe.wait_ge(S["ext_tile"], 3)
            pe.transpose(PS[0:2, 7, 0:P], ext[:, 4:6], b.ident[0:P, 0:P]).then_inc(S["ext_turned"], 1)
            pe.wait_ge(S["ext_all"], 2)
            pe.matmul(PS[0:P, 7, 256:258], b.ones[0:2, 0:P], corner[:, :], start=True, stop=True
                      ).then_inc(S["ext_everywhere"], 1)
            def sums(c, part, s):
                at = part * D + c * 128
                for h in range(2):
                    last = pe.matmul(PS[:, 4 * (c % 2) + 2 * part + h, 0:HALF], EE[:, s, at:at + 128],
                                     b.CT[:, s, h * HALF:(h + 1) * HALF], start=(s == 0), stop=(s == TILES - 1))
                if s == TILES - 1:
                    last.then_inc(S[("denominators", "numerators")[part]], 1)

            for s in range(TILES - 1):
                pe.wait_ge(S["weights"], s + 1)
                for c in range(2):
                    sums(c, 0, s)
                pe.wait_ge(S["weighted"], s + 1)
                for c in range(2):
                    sums(c, 1, s)
            pe.wait_ge(S["weighted"], TILES)
            for c in range(2):
                for part in range(2):
                    sums(c, part, TILES - 1)
            for c in range(2, K):
                pe.wait_ge(S["h"], c - 1)
                for part in range(2):
                    for s in range(TILES):
                        sums(c, part, s)
            pe.wait_ge(S["h"], K)
            pe.wait_ge(S["h_final"], 1)
            pe.wait_ge(loaded, loads)

            def up(m):
                if m >= 2:
                    pe.wait_ge(S["up_out"], m - 1)
                for h in range(2):
                    last = accumulate(pe, PS[0:P, 2 * (m % 2) + h, :],
                                      [(tile_of(hT, k, m), w1[:, k, h * D:(h + 1) * D]) for k in range(K)])
                last.then_inc(S["up"], 1)

            def turn_hidden(m):
                pe.wait_ge(S["mid_norm"], m + 1)
                if m >= 1:
                    pe.wait_ge(S["hidden"], 2 * K * m)
                for k in range(2 * K):
                    last = pe.transpose(PS[:, 4 + k // 4, (k % 4) * P:(k % 4 + 1) * P], H1[:, m, k * 128:(k + 1) * 128],
                                        b.ident[0:P, 0:P])
                last.then_inc(S["mid_turned"], 1)

            def down(m):
                pe.wait_ge(S["hidden"], 2 * K * (m + 1))
                if m >= 2:
                    pe.wait_ge(S[("x_rows" if layer == 0 else "down_out")], m - 1)
                accumulate(pe, PS[0:P, 6 + m % 2, :], [(tile_of(H2T, k, m), w2[:, k, :]) for k in range(2 * K)]
                           ).then_inc(S["down"], 1)

            def turn_x(m):
                pe.wait_ge(S["x_rows"], m + 1)
                if m >= 2:
                    pe.wait_ge(S["x_columns"], m - 1)
                for k in range(K):
                    last = pe.transpose(PS[:, m % 2, k * P:(k + 1) * P], b.XN[:, m, k * 128:(k + 1) * 128],
                                        b.ident[0:P, 0:P])
                last.then_inc(S["x_turned"], 1)

            def share(m):
                pe.wait_ge(S["x_columns"], m + 1)
                if m >= 4:
                    pe.wait_ge(S["share_out"], m - 3)
                accumulate(pe, PS[0:P, 2 + m % 4, :], [(tile_of(b.XT, k, m), cw[:, k, :]) for k in range(K)]
                           ).then_inc(S["share"], 1)

            for m in range(TILES):
                up(m)
                if m >= 1:
                    turn_hidden(m - 1)
            down(0)
            turn_hidden(TILES - 1)
            down(1)
            pe.wait_ge(S["cw_in"], 16)
            for m in range(2, TILES):
                down(m)
                turn_x(m - 2)
            share(0)
            turn_x(TILES - 2)
            share(1)
            share(2)
            turn_x(TILES - 1)
            share(3)
            if layer == 2:
                input_turn(pe, b, S, 0, 6)
            share(4)
            if layer == 2:
                input_turn(pe, b, S, 1, 7)
                for m in range(2, TILES):
                    pe.wait_ge(S["pre_columns"], m - 1)
                    input_turn(pe, b, S, m, 6 + m % 2)



def threshold_gates_vector(dve, b, S, G, E, bias, cap):
    lg = G["lg"]
    dve.wait_ge(S["logits"], 1)
    logits = b.psum[0:P, 7, 0:TILES * (E + 1)].rearrange("p (m e) -> p m e", m=TILES)
    if bias is not None:
        dve.tensor_tensor(lg[:, :, :], logits, bias.unsqueeze(1).to_broadcast([P, TILES, E + 1]), ALU.add
                          ).then_inc(S["gate"], 1)
    else:
        dve.tensor_copy(lg[:, :, :], logits).then_inc(S["gate"], 1)
    dve.wait_ge(S["gate"], 1)
    dve.tensor_reduce(G["s"][:, :], lg[:, :, 0:E], AX.X, ALU.max).then_inc(S["gate"], 1)
    dve.wait_ge(S["gate"], 2)
    dve.tensor_tensor(lg[:, :, 0:E], lg[:, :, 0:E], spread(G["s"][:, :], E), ALU.subtract).then_inc(S["gate_shifted"], 1)
    dve.wait_ge(S["gate_exp"], 2)
    dve.tensor_reduce(G["s"][:, :], G["w"][:, :, :], AX.X, ALU.add).then_inc(S["gate"], 1)
    dve.tensor_scalar(G["t"][:, :], G["t"][:, :], 1.0, None, ALU.add).then_inc(S["gate"], 1)
    dve.wait_ge(S["gate"], 4)
    dve.reciprocal(G["s"][:, :], G["s"][:, :]).then_inc(S["gate"], 1)
    dve.reciprocal(G["t"][:, :], G["t"][:, :]).then_inc(S["gate"], 1)
    dve.wait_ge(S["gate"], 6)
    dve.tensor_tensor(G["w"][:, :, :], G["w"][:, :, :], spread(G["s"][:, :], E), ALU.mult).then_inc(S["gate"], 1)
    dve.tensor_scalar(G["t"][:, :], G["t"][:, :], cap, None, ALU.mult).then_inc(S["gate"], 1)
    dve.wait_ge(S["gate"], 8)
    dve.tensor_tensor(G["w"][:, :, :], G["w"][:, :, :], spread(G["t"][:, :], E), ALU.subtract).then_inc(S["gate"], 1)
    dve.wait_ge(S["gate"], 9)
    dve.tensor_scalar(G["w"][:, :, :], G["w"][:, :, :], 0.0, None, ALU.max).then_inc(S["gate"], 1)
    dve.wait_ge(S["gate"], 10)
    dve.tensor_reduce(G["s"][:, :], G["w"][:, :, :], AX.X, ALU.add).then_inc(S["gate"], 1)
    dve.wait_ge(S["gate"], 11)
    dve.scalar_tensor_tensor(G["t"][:, :], G["s"][:, :], 0.0, G["s"][:, :], ALU.is_equal, ALU.add).then_inc(S["gate"], 1)
    dve.wait_ge(S["gate"], 12)
    dve.reciprocal(G["t"][:, :], G["t"][:, :]).then_inc(S["gate"], 1)
    dve.wait_ge(S["gate"], 13)
    dve.tensor_tensor(G["w"][:, :, :], G["w"][:, :, :], spread(G["t"][:, :], E), ALU.mult).then_inc(S["gates"], 1)


def threshold_gates_scalar(act, b, S, G, E):
    act.wait_ge(S["gate_shifted"], 1)
    act.activation(G["w"][:, :, :], G["lg"][:, :, 0:E], ACT.Exp).then_inc(S["gate_exp"], 1)
    act.activation(G["t"][:, :], G["lg"][:, :, E], ACT.Exp, scale=-1.0).then_inc(S["gate_exp"], 1)


def logits_tensor(pe, b, S, weights, n):
    for m in range(TILES):
        last = accumulate(pe, b.psum[0:P, 7, m * n:(m + 1) * n],
                          [(tile_of(b.XT, k, m), weights[:, k, :]) for k in range(K)])
    last.then_inc(S["logits"], 1)


def gate_buffers(b, E):
    return {"lg": b.sb("gate_logits", [P, TILES, E + 1]),
            "w": b.sb("gate_weights", [P, TILES, E]),
            "s": b.sb("gate_sums", [P, TILES]),
            "t": b.sb("gate_thresholds", [P, TILES])}


EXPERT_BANKS = 5


def expert_turn_bank(m):
    return EXPERT_BANKS + (m + 2) % 3


def experts_vector(dve, b, S, w, first, end, E, parked=None):
    for n in range(first, end):
        e, m = divmod(n, TILES)
        if parked is not None and n < len(parked):
            dve.wait_ge(S["parked"], n + 1)
            product = parked[n]
        else:
            dve.wait_ge(S["expert"], n + 1)
            product = b.psum[0:P, n % EXPERT_BANKS, :]
        if n >= TILES:
            dve.wait_ge(S["expert_out"], n - TILES + 1)
        dve.scalar_tensor_tensor(b.X[:, m, :], product, w[:, m, e:e + 1], b.X[:, m, :],
                                 ALU.mult, ALU.add).then_inc(S["expert_out"], 1)
        if e == E - 1:
            dve.wait_ge(S["expert_out"], n + 1)
            input_rows(dve, b, S, m)


class Halves:
    TILE = 128

    WIDTH = (TILES - 1) * P + TILE

    def __init__(self, b, x=None, w=None):
        def sb(name, shape):
            return b.nc.alloc_sbuf_tensor(f"{b.part}_{name}", shape, F32R)
        self.x = x or [sb(f"x_{n}", [128, K, self.WIDTH]) for n in ("high", "low")]
        self.w = w or [sb(f"w_{n}", [128, 2, K * D]) for n in ("high", "low")]

    def x_tile(self, part, k, m):
        return self.x[part][:, k, m * P:m * P + self.TILE]

    def split_x_high(self, act, b, S):
        for k in range(K):
            act.activation(self.x[0][:, k, 0:NODES], b.XT[:, k, 0:NODES], ACT.Copy).then_inc(S["x_high"], 1)

    def split_x_low(self, dve, b, S):
        for x in self.x:
            dve.tensor_scalar(x[:, :, NODES:], b.XT[:, :, 0:x.shape[2] - NODES], 0.0, None, ALU.mult
                              ).then_inc(S["x_padding"], 1)
        for k in range(K):
            dve.wait_ge(S["x_high"], k + 1)
            dve.tensor_tensor(self.x[1][:, k, 0:NODES], b.XT[:, k, 0:NODES], self.x[0][:, k, 0:NODES].bitcast(F32),
                              ALU.subtract).then_inc(S["x_low"], 1)

    def split_w_high(self, act, S, W, e, used="expert", steps=TILES):
        if e >= 4:
            act.wait_ge(S[f"ring_in{e % 4}"], 16)
        if e >= 2:
            act.wait_ge(S[used], steps * (e - 1))
        act.activation(self.w[0][:, e % 2, :], W[:, (e % 4) * K * D:(e % 4 + 1) * K * D], ACT.Copy).then_inc(S["w_high"], 1)

    def split_w_low(self, pool, S, W, e):
        pool.wait_ge(S["w_high"], e + 1)
        pool.tensor_tensor(self.w[1][:, e % 2, :], W[:, (e % 4) * K * D:(e % 4 + 1) * K * D],
                           self.w[0][:, e % 2, :].bitcast(F32), ALU.subtract).then_inc(S["w_low"], 1)

    def product(self, pe, b, S, out, e, m):
        pe.wait_ge(S["x_low"], K)
        pe.wait_ge(S["x_padding"], 2)
        pe.wait_ge(S["w_low"], e + 1)
        return accumulate(pe, out, [(self.x_tile(px, k, m), self.w[pw][:, e % 2, k * D:(k + 1) * D])
                                    for k in range(K) for px, pw in ((0, 0), (0, 1), (1, 0))])


def experts_tensor(pe, b, S, W, first, end, E, parked=0, parts=None):
    for n in range(first, end):
        e, m = divmod(n, TILES)
        if parts is None and e >= 4 and m == 0:
            pe.wait_ge(S[f"ring_in{e % 4}"], 16)
        before = n - EXPERT_BANKS
        if 0 <= before < parked:
            pe.wait_ge(S["parked"], before + 1)
        elif before >= 0:
            pe.wait_ge(S["expert_out"], before + 1)
        if parts is not None:
            parts.product(pe, b, S, b.psum[:, n % EXPERT_BANKS, :], e, m).then_inc(S["expert"], 1)
        else:
            accumulate(pe, b.psum[0:P, n % EXPERT_BANKS, :],
                       [(tile_of(b.XT, k, m), W[:, ((e % 4) * K + k) * D:((e % 4) * K + k + 1) * D]) for k in range(K)]
                       ).then_inc(S["expert"], 1)
        if e == E - 1 and m >= 2:
            input_turn(pe, b, S, m - 2, expert_turn_bank(m - 2))
    if end == E * TILES:
        for m in (TILES - 2, TILES - 1):
            pe.wait_ge(S["pre_columns"], m - 2)
            input_turn(pe, b, S, m, expert_turn_bank(m))


def experts_sync(sp, b, S, t, weights, W, E, split=False):
    for e in range(4, E):
        if split:
            sp.wait_ge(S["w_low"], e - 3)
        else:
            sp.wait_ge(S["expert"], TILES * (e - 3))
        sp.dma_start(W[:, (e - 4) * K * D:(e - 3) * K * D].rearrange("p (k n) -> p k n", k=K),
                     t[weights][e].rearrange("(k p) n -> p k n", p=128)).then_inc(S[f"ring_in{e % 4}"], 16)


def ffn_threshold(nc, b, t, slot, loaded, loads, load_next, C, edged):
    S = Semaphores(nc, b.part)
    E = 8
    W, V = b.W[slot], b.V[slot]
    gate = b.U[slot][:, 0:K * (E + 1)].rearrange("p (k e) -> p k e", k=K)
    G = gate_buffers(b, E)
    wT = b.sb("gates_columns", [E, NODES])
    bias = V[0:E, D:2 * D]
    parts = Halves(b)

    pieces = [(C[:, :, 0:D], b.XN[:, :, :]),
              (C[:, :, D:], V[0:P, 4 * D:4 * D + TILES * (PADDED - D)].rearrange("p (m n) -> p m n", m=TILES))]

    def edges_vector(dve):
        dve.wait_ge(b.counts_loaded, 16)
        dve.tensor_reduce(edged[:, :], C[:, :, :], AX.X, ALU.max).then_inc(S["edged"], 1)
        for counts, none in pieces:
            dve.tensor_scalar(none, counts, 0.0, None, ALU.is_equal).then_inc(S["none"], 1)
        dve.wait_ge(S["edged"], 1)
        dve.tensor_scalar(edged[:, :], edged[:, :], 0.0, None, ALU.is_gt).then_inc(S["edged"], 1)
        dve.wait_ge(S["none"], 2)
        for counts, none in pieces:
            dve.tensor_tensor(counts, counts, none, ALU.add).then_inc(S["counts_safe"], 1)

    def logarithms_vector(dve):
        dve.wait_ge(S["counts_log"], 1)
        for counts, none in pieces:
            dve.scalar_tensor_tensor(counts, none, -BIG, counts, ALU.mult, ALU.add).then_inc(S["log_counts"], 1)
        dve.wait_ge(S["log_counts"], 2)

    with nc.Block() as block:
        @block.sync
        def _(sp):
            sp.dma_start(C[:, :, :].rearrange("p m n -> p (m n)"), b.counts_dram[0]).then_inc(b.counts_loaded, 16)
            experts_sync(sp, b, S, t, "L0_ffn_W_exp", W, E, split=True)
            load_next(sp)

        @block.gpsimd
        def _(pool):
            for e in range(E):
                parts.split_w_low(pool, S, W, e)

        @block.vector
        def _(dve):
            parts.split_x_low(dve, b, S)
            dve.wait_ge(loaded, loads)
            threshold_gates_vector(dve, b, S, G, E, V[0:P, 0:E + 1], 0.25)
            dve.wait_ge(S["gates"], 1)
            experts_vector(dve, b, S, G["w"], 0, TILES, E)
            dve.wait_ge(S["gates_turned"], 1)
            dve.tensor_copy(wT[:, 0:4 * P], b.psum[0:E, 5, 0:4 * P]).then_inc(S["gates_out"], 1)
            dve.tensor_copy(wT[:, 4 * P:], b.psum[0:E, 6, 0:P]).then_inc(S["gates_out"], 1)
            experts_vector(dve, b, S, G["w"], TILES, 2 * TILES, E)
            dve.wait_ge(S["expert_out"], 2 * TILES)
            for m in range(TILES):
                dve.wait_ge(S["bias"], m + 1)
                dve.tensor_tensor(b.X[:, m, :], b.psum[0:P, 5 + m % 2, :], b.X[:, m, :], ALU.add).then_inc(S["bias_out"], 1)
            dve.wait_ge(S["bias_out"], TILES)
            experts_vector(dve, b, S, G["w"], 2 * TILES, 3 * TILES, E)
            edges_vector(dve)
            experts_vector(dve, b, S, G["w"], 3 * TILES, 4 * TILES, E)
            logarithms_vector(dve)
            experts_vector(dve, b, S, G["w"], 4 * TILES, E * TILES, E)

        @block.scalar
        def _(act):
            parts.split_x_high(act, b, S)
            act.wait_ge(loaded, loads)
            parts.split_w_high(act, S, W, 0)
            threshold_gates_scalar(act, b, S, G, E)
            for e in range(1, E):
                parts.split_w_high(act, S, W, e)
                if e == 4:
                    act.wait_ge(S["counts_safe"], 2)
                    act.activation(C[:, :, :], C[:, :, :], ACT.Ln).then_inc(S["counts_log"], 1)
            input_columns(act, b, S, expert_turn_bank, 2)

        @block.tensor
        def _(pe):
            pe.wait_ge(loaded, loads)
            logits_tensor(pe, b, S, gate, E + 1)
            experts_tensor(pe, b, S, W, 0, TILES, E, parts=parts)
            pe.wait_ge(S["gates"], 1)
            for m in range(TILES):
                last = pe.transpose(b.psum[0:E, 5 + m // 4, (m % 4) * P:(m % 4 + 1) * P], G["w"][:, m, :],
                                    b.ident[0:P, 0:P])
            last.then_inc(S["gates_turned"], 1)
            experts_tensor(pe, b, S, W, TILES, 2 * TILES, E, parts=parts)
            pe.wait_ge(S["gates_out"], 2)
            for m in range(TILES):
                if m >= 2:
                    pe.wait_ge(S["bias_out"], m - 1)
                pe.matmul(b.psum[0:P, 5 + m % 2, :], wT[:, m * P:(m + 1) * P], bias, start=True, stop=True
                          ).then_inc(S["bias"], 1)
            experts_tensor(pe, b, S, W, 2 * TILES, E * TILES, E, parts=parts)


def ffn_sinkhorn(nc, b, t, slot, loaded, loads, load_next):
    S = Semaphores(nc, b.part)
    E, ROUNDS = 8, 8
    TOP = NODES // E
    PICKS = -(-TOP // 8)
    SENTINELS = 8 * PICKS - TOP
    W = b.W[slot]
    PS = b.psum
    gate = b.U[slot][:, 0:K * E].rearrange("p (k e) -> p k e", k=K)
    T = b.sb("balanced", [P, TILES, E])
    T2 = b.sb("column_scaled", [P, TILES, E])
    rc = b.sb("column_factor", [P, E])
    rr = b.sb("row_factor", [P, TILES])
    space = b.XN[0:E, :, :].rearrange("p m n -> p (m n)")
    WIDTH = NODES + SENTINELS
    rank = [space[:, n * WIDTH:(n + 1) * WIDTH] for n in range(2)]
    top8 = b.sb("top8", [E, 8])
    picked = space[:, 2 * WIDTH:2 * WIDTH + NODES]
    sel = b.sb("picked", [P, TILES, E])
    w = b.sb("combine", [P, TILES, E])
    RANKED_MEANWHILE = 7
    PARKED = ROUNDS + RANKED_MEANWHILE
    more = b.sb("parked_products", [P, RANKED_MEANWHILE, D])
    parked = [b.V[slot][0:P, n * D:(n + 1) * D] for n in range(ROUNDS)] + [more[:, n, :] for n in range(RANKED_MEANWHILE)]
    parts = Halves(b)

    with nc.Block() as block:
        @block.sync
        def _(sp):
            experts_sync(sp, b, S, t, "L1_ffn_experts", W, E, split=True)
            load_next(sp)

        @block.gpsimd
        def _(pool):
            for e in range(E):
                parts.split_w_low(pool, S, W, e)

        @block.vector
        def _(dve):
            parts.split_x_low(dve, b, S)
            dve.wait_ge(S["logits"], 1)
            dve.tensor_scalar(T[:, :, :], PS[0:P, 7, 0:TILES * E].rearrange("p (m e) -> p m e", m=TILES), 1e-10, None,
                              ALU.max).then_inc(S["balanced"], 1)
            for i in range(ROUNDS):
                dve.wait_ge(S["column_sums"], i + 1)
                dve.reciprocal(rc[:, :], PS[0:P, 6, 0:E]).then_inc(S["bal"], 1)
                dve.wait_ge(S["bal"], 4 * i + 1)
                dve.tensor_tensor(T2[:, :, :], T[:, :, :], rc[:, :].unsqueeze(1).to_broadcast([P, TILES, E]), ALU.mult
                                  ).then_inc(S["bal"], 1)
                dve.wait_ge(S["bal"], 4 * i + 2)
                dve.tensor_reduce(rr[:, :], T2[:, :, :], AX.X, ALU.add).then_inc(S["bal"], 1)
                dve.wait_ge(S["bal"], 4 * i + 3)
                dve.reciprocal(rr[:, :], rr[:, :]).then_inc(S["bal"], 1)
                dve.wait_ge(S["bal"], 4 * i + 4)
                dve.tensor_tensor(T[:, :, :], T2[:, :, :], spread(rr[:, :], E), ALU.mult).then_inc(S["balanced"], 1)
            for n in range(SENTINELS):
                dve.memset(rank[0][:, NODES + n:NODES + n + 1], 4.0 + n).then_inc(S["ranked"], 1)
            dve.wait_ge(S["ranks_turned"], 1)
            dve.tensor_copy(rank[0][:, 0:4 * P], PS[0:E, 5, 0:4 * P]).then_inc(S["ranked"], 1)
            dve.tensor_copy(rank[0][:, 4 * P:NODES], PS[0:E, 6, 0:P]).then_inc(S["ranked"], 1)
            dve.wait_ge(S["ranked"], SENTINELS + 2)
            for n in range(PICKS):
                dve.max(top8[:, :], rank[n % 2][:, :]).then_inc(S["top8"], 1)
                dve.wait_ge(S["top8"], n + 1)
                dve.match_replace(rank[1 - n % 2][:, :], top8[:, :], rank[n % 2][:, :], -1.0).then_inc(S["taken"], 1)
                dve.wait_ge(S["taken"], n + 1)
            dve.tensor_scalar(picked[:, :], rank[PICKS % 2][:, 0:NODES], -1.0, None, ALU.is_equal).then_inc(S["picked"], 1)
            dve.wait_ge(S["picked_turned"], 1)
            dve.tensor_copy(sel[:, :, :], PS[0:P, 7, 0:TILES * E].rearrange("p (m e) -> p m e", m=TILES)
                            ).then_inc(S["comb"], 1)
            dve.wait_ge(S["comb"], 1)
            dve.tensor_reduce(rr[:, :], sel[:, :, :], AX.X, ALU.add).then_inc(S["comb"], 1)
            dve.scalar_tensor_tensor(w[:, :, :], T[:, :, :], 0.5, sel[:, :, :], ALU.is_gt, ALU.mult).then_inc(S["comb"], 1)
            dve.wait_ge(S["comb"], 3)
            dve.tensor_scalar(rr[:, :], rr[:, :], 1.0, None, ALU.add).then_inc(S["comb"], 1)
            dve.wait_ge(S["comb"], 4)
            dve.reciprocal(rr[:, :], rr[:, :]).then_inc(S["comb"], 1)
            dve.wait_ge(S["comb"], 5)
            dve.tensor_tensor(w[:, :, :], w[:, :, :], spread(rr[:, :], E), ALU.mult).then_inc(S["comb"], 1)
            dve.wait_ge(S["comb"], 6)
            experts_vector(dve, b, S, w, 0, E * TILES, E, parked)

        @block.scalar
        def _(act):
            parts.split_x_high(act, b, S)
            act.wait_ge(loaded, loads)
            for e in range(2):
                parts.split_w_high(act, S, W, e)
            for n in range(PARKED):
                act.wait_ge(S["expert"], n + 1)
                act.activation(parked[n], PS[0:P, n % EXPERT_BANKS, :], ACT.Copy).then_inc(S["parked"], 1)
                if n % TILES == TILES - 1:
                    parts.split_w_high(act, S, W, n // TILES + 2)
            for e in range(PARKED // TILES + 2, E):
                parts.split_w_high(act, S, W, e)
            input_columns(act, b, S, expert_turn_bank, 2)

        @block.tensor
        def _(pe):
            pe.wait_ge(loaded, loads)
            logits_tensor(pe, b, S, gate, E)
            for i in range(ROUNDS):
                pe.wait_ge(S["balanced"], i + 1)
                accumulate(pe, PS[0:P, 6, 0:E], [(b.ones[0:P, 0:P], T[:, m, :]) for m in range(TILES)]
                           ).then_inc(S["column_sums"], 1)
                experts_tensor(pe, b, S, W, i, i + 1, E, PARKED, parts)
            pe.wait_ge(S["balanced"], ROUNDS + 1)
            for m in range(TILES):
                last = pe.transpose(PS[0:E, 5 + m // 4, (m % 4) * P:(m % 4 + 1) * P], T[:, m, :], b.ident[0:P, 0:P])
            last.then_inc(S["ranks_turned"], 1)
            experts_tensor(pe, b, S, W, ROUNDS, PARKED, E, PARKED, parts)
            pe.wait_ge(S["picked"], 1)
            for m in range(TILES):
                last = pe.transpose(PS[0:P, 7, m * E:(m + 1) * E], picked[:, m * P:(m + 1) * P], b.ident[0:E, 0:E])
            last.then_inc(S["picked_turned"], 1)
            experts_tensor(pe, b, S, W, PARKED, E * TILES, E, PARKED, parts)


def attention(nc, b, t, layer, slot, loaded, loads, load_next, C, edged):
    S = Semaphores(nc, b.part)
    PS = b.psum
    HEADS, DH = 8, 64
    W, V = b.W[slot], b.V[slot]
    wq, wk, wv, wo = (W[:, n * K * D:(n + 1) * K * D].rearrange("p (k n) -> p k n", k=K) for n in range(4))
    w1 = V[:, 0:256].rearrange("p (k n) -> p k n", k=K)
    w2 = V[0:64, 256:768]
    ln_g, ln_b = V[0:P, 1024:1536], V[0:P, 1536:2048]
    cols = column_vectors(b, slot, [(n, K) for n in ("bq", "bo", "b2", "g1", "beta1", "g2", "beta2")] + [("b1", 1)])
    PAIRS = HEADS // 2
    ITEMS = TILES * PAIRS
    RING = 3

    qT = b.sb("q_columns", [128, K, Halves.WIDTH])
    kT = b.sb("k_columns", [128, K, Halves.WIDTH])
    bqs = b.sb("bq_scaled", [128, K])
    STEPS_IN = [("q", 0), ("k", 0), ("q", 1), ("k", 1), ("v", 0), ("v", 1)]
    HALF_D = D // 2
    EVEN_HALF = Halves.WIDTH // 2
    with nc.sbuf_tensor(f"{b.part}_x_high", [128, K, Halves.WIDTH], F32R) as x_high, \
            nc.sbuf_tensor(f"{b.part}_x_low", [128, K, Halves.WIDTH], F32R) as x_low, \
            nc.sbuf_tensor(f"{b.part}_w_high", [128, 2, K, HALF_D], F32R) as w_high, \
            nc.sbuf_tensor(f"{b.part}_w_low", [128, 2, K, HALF_D], F32R) as w_low:
        parts = Halves(b, [x_high, x_low], [w_high, w_low])

    def raw_step(s):
        matrix, half = STEPS_IN[s]
        return {"q": wq, "k": wk, "v": wv}[matrix][:, :, half * HALF_D:(half + 1) * HALF_D]

    v = b.XN
    ring = [b.sb(f"scores{n}", [P, 2, PADDED]) for n in range(RING - 1)]
    ring.append(V[0:P, 4 * D:4 * D + 2 * PADDED].rearrange("p (a n) -> p a n", a=2))
    pT = b.sb("probabilities_turned", [P, 2, 2, TILES, P])
    top = b.sb("score_max", [P, ITEMS, 2])
    ntop = b.sb("minus_max", [P, ITEMS, 2])
    total = b.sb("prob_sum", [P, ITEMS, 2])
    inv = b.sb("inverse_sum", [P, ITEMS, 2])
    aT = b.sb("attended_columns", [128, K, PADDED])
    fT = kT[0:64, 0, 0:PADDED]
    bs = b.sb("batch_stats", [128, K, 2, 6])
    bm = b.sb("batch_mean", [128, K, 2])
    bv = b.sb("batch_scale", [128, 4, K])
    z = qT[:, :, 0:PADDED]

    def batch_norm_vector(dve, tag, product, bias, gain, shift):
        for c in range(K + 1):
            if c < K:
                bank = 2 * (c % 4)
                dve.wait_ge(S[product], c + 1)
                dve.scalar_tensor_tensor(halves(z[:, c, :]), PS[:, bank:bank + 2, 0:HALF], bias[:, c:c + 1],
                                         halves(b.XT[:, c, :]), ALU.add, ALU.add).then_inc(S[tag + "_sums"], 1)
            if c >= 1:
                dve.wait_ge(S[tag + "_sums"], c)
                dve.bn_stats(bs[:, c - 1, 0, :], z[:, c - 1, 0:HALF]).then_inc(S[tag + "_stats"], 1)
                dve.bn_stats(bs[:, c - 1, 1, :], z[:, c - 1, HALF:NODES]).then_inc(S[tag + "_stats"], 1)
        dve.wait_ge(S[tag + "_stats"], 2 * K)
        for c in range(K):
            dve.bn_aggr(bm[:, c, :], bs[:, c, :, :].rearrange("p h s -> p (h s)")).then_inc(S[tag + "_aggr"], 1)
        dve.wait_ge(S[tag + "_aggr"], K)
        dve.tensor_scalar(bv[:, 0, :], bm[:, :, 1], 1e-5, None, ALU.add).then_inc(S[tag + "_var"], 1)
        dve.wait_ge(S[tag + "_root"], 1)
        dve.reciprocal(bv[:, 1, :], bv[:, 1, :]).then_inc(S[tag], 1)
        dve.wait_ge(S[tag], 1)
        dve.tensor_tensor(bv[:, 2, :], bv[:, 1, :], gain, ALU.mult).then_inc(S[tag], 1)
        dve.wait_ge(S[tag], 2)
        dve.tensor_tensor(bv[:, 3, :], bm[:, :, 0], bv[:, 2, :], ALU.mult).then_inc(S[tag], 1)
        dve.wait_ge(S[tag], 3)
        dve.tensor_tensor(bv[:, 3, :], shift, bv[:, 3, :], ALU.subtract).then_inc(S[tag], 1)
        dve.wait_ge(S[tag], 4)
        for c in range(0, K, 2):
            dve.tensor_scalar(b.XT[:, c, 0:NODES], z[:, c, 0:NODES], bv[:, 2, c:c + 1], bv[:, 3, c:c + 1], ALU.mult, ALU.add
                              ).then_inc(S[tag + "_even"], 1)

    def batch_norm_scalar(act, tag):
        act.wait_ge(S[tag + "_var"], 1)
        act.activation(bv[:, 1, :], bv[:, 0, :], ACT.Sqrt).then_inc(S[tag + "_root"], 1)
        act.wait_ge(S[tag], 4)
        for c in range(1, K, 2):
            act.activation(b.XT[:, c, 0:NODES], z[:, c, 0:NODES], ACT.Identity, bias=bv[:, 3, c:c + 1],
                           scale=bv[:, 2, c:c + 1]).then_inc(S[tag + "_odd"], 1)

    with nc.Block() as block:
        @block.sync
        def _(sp):
            load_next(sp)

        @block.gpsimd
        def _(pool):
            for s in range(len(STEPS_IN)):
                pool.wait_ge(S["w_high"], s + 1)
                pool.tensor_tensor(w_low[:, s % 2, :, :], raw_step(s), w_high[:, s % 2, :, :].bitcast(F32), ALU.subtract
                                   ).then_inc(S["w_low"], 1)
            for n in range(ITEMS):
                pool.wait_ge(S["inv"], n + 1)
                for e in range(2):
                    pool.tensor_scalar(ring[n % RING][:, e, :], ring[n % RING][:, e, :], inv[:, n, e:e + 1],
                                       edged[:, n // PAIRS:n // PAIRS + 1], ALU.mult, ALU.mult).then_inc(S["scaled"], 1)
            if layer == 1:
                for m in range(TILES):
                    pool.tensor_tensor(b.X[:, m, :], b.X[:, m, :], ln_b, ALU.add).then_inc(S["last_shift"], 1)
                pool.wait_ge(S["last_shift"], TILES)
                for m in range(TILES):
                    pool.wait_ge(S["last_norm"], m + 1)
                    pool.tensor_tensor(b.XN[:, m, :], b.XN[:, m, :], ln_g, ALU.mult).then_inc(S["last_gain"], 1)

        @block.vector
        def _(dve):
            parts.split_x_low(dve, b, S)

            def last_source_tile(n):
                dve.wait_ge(S["turned"], n + 1)
                if n >= 2:
                    dve.wait_ge(S["pv"], n - 1)
                dve.tensor_copy(pT[:, n % 2, :, 4, :], PS[0:P, 6, 0:2 * P].rearrange("p (e d) -> p e d", e=2)).then_inc(S["turned_last"], 1)

            dve.wait_ge(loaded, loads)
            dve.tensor_scalar(bqs[:, :], cols["bq"], float(DH) ** -0.5, None, ALU.mult).then_inc(S["bq"], 1)
            for c in range(K):
                dve.wait_ge(S["k"], c + 1)
                bank = 4 * (c % 2) + 2
                dve.tensor_copy(halves(kT[:, c, :]), PS[:, bank:bank + 2, 0:EVEN_HALF]).then_inc(S["k_out"], 1)
            for m in range(TILES):
                dve.wait_ge(S["v"], m + 1)
                dve.tensor_copy(v[:, m, :], PS[0:P, m, :]).then_inc(S["v_out"], 1)
            dve.memset(aT[:, :, NODES:], 0.0).then_inc(S["padding"], 1)
            for n in range(ITEMS + 2):
                if n < ITEMS:
                    m, pair = divmod(n, PAIRS)
                    dve.wait_ge(S["scores"], n + 1)
                    if n >= RING:
                        dve.wait_ge(S["turned"], n - RING + 1)
                    for e in range(2):
                        dve.tensor_tensor_reduce(halves(ring[n % RING][:, e, :]), PS[0:P, 2 * e:2 * e + 2, 0:HALF],
                                                 halves(C[:, m, :]), 1.0, -3e38, ALU.add, ALU.max, top[:, n, e:e + 1]
                                                 ).then_inc(S["scored"], 1)
                    dve.wait_ge(S["scored"], 2 * n + 2)
                    dve.tensor_scalar(ntop[:, n, :], top[:, n, :], -1.0, None, ALU.mult).then_inc(S["ntop"], 1)
                if 1 <= n <= ITEMS:
                    dve.wait_ge(S["probs"], 2 * n)
                    dve.reciprocal(inv[:, n - 1, :], total[:, n - 1, :]).then_inc(S["inv"], 1)
                if n >= 2:
                    last_source_tile(n - 2)
            batch_norm_vector(dve, "bn1", "wo", cols["bo"], cols["g1"], cols["beta1"])
            batch_norm_vector(dve, "bn2", "ff2", cols["b2"], cols["g2"], cols["beta2"])
            if layer == 1:
                for step in range(TILES + 4):
                    if step < TILES:
                        dve.wait_ge(S["rows"], step + 1)
                        begin_stats(dve, b, S, "last", step, [PS[0:P, step, :]])
                    if 1 <= step <= TILES:
                        m = step - 1
                        end_stats(dve, b, S, "last", m)
                        dve.scalar_tensor_tensor(b.nmr[:, m:m + 1], b.mv[:, m, 0:1], -1.0, b.rstd[:, m:m + 1],
                                                 ALU.mult, ALU.mult).then_inc(S["last_nmr"], 1)
                    if 2 <= step <= TILES + 1:
                        m = step - 2
                        dve.wait_ge(S["last_gain"], m + 1)
                        dve.tensor_tensor(b.X[:, m, :], b.X[:, m, :], b.XN[:, m, :], ALU.add).then_inc(S["last_sum"], 1)
                        dve.wait_ge(S["last_sum"], m + 1)
                        begin_stats(dve, b, S, "pre", m, [b.X[:, m, :]])
                    if 3 <= step <= TILES + 2:
                        input_scale(dve, b, S, step - 3)

        @block.scalar
        def _(act):
            def source_tiles(n):
                act.wait_ge(S["turned"], n + 1)
                if n >= 2:
                    act.wait_ge(S["pv"], n - 1)
                act.activation(pT[:, n % 2, :, 0:4, :].rearrange("p e s d -> p e (s d)"), PS[0:P, 4:6, 0:4 * P], ACT.Copy
                               ).then_inc(S["turned_first"], 1)

            def attended(m):
                act.wait_ge(S["pv"], PAIRS * (m + 1))
                act.activation(aT[:, :, m * P:(m + 1) * P], PS[:, 7, 0:K * P].rearrange("p (k n) -> p k n", k=K),
                               ACT.Copy).then_inc(S["att_columns"], 1)

            def split_high(s):
                if s >= 2:
                    matrix, half = STEPS_IN[s - 2]
                    act.wait_ge(S[matrix], 2 * (half + 1))
                act.activation(w_high[:, s % 2, :, :], raw_step(s), ACT.Copy).then_inc(S["w_high"], 1)

            act.wait_ge(loaded, loads)
            split_high(0)
            parts.split_x_high(act, b, S)
            split_high(1)
            act.wait_ge(S["bq"], 1)
            for c in range(K):
                act.wait_ge(S["q"], c + 1)
                bank = 4 * (c % 2)
                act.activation(halves(qT[:, c, :]), PS[:, bank:bank + 2, 0:EVEN_HALF], ACT.Identity, bias=bqs[:, c:c + 1],
                               scale=float(DH) ** -0.5).then_inc(S["q_out"], 1)
                if c % 2 == 1:
                    split_high(c + 1)
                    split_high(c + 2)
            for n in range(ITEMS + 2):
                if n >= 4 and (n - 4) % PAIRS == PAIRS - 1:
                    attended((n - 4) // PAIRS)
                if n < ITEMS:
                    act.wait_ge(S["ntop"], n + 1)
                    for e in range(2):
                        act.activation(ring[n % RING][:, e, :], ring[n % RING][:, e, :], ACT.Exp,
                                       bias=ntop[:, n, e:e + 1], scale=1.0, accum_out=total[:, n, e:e + 1]
                                       ).then_inc(S["probs"], 1)
                if n >= 2:
                    source_tiles(n - 2)
            attended(TILES - 1)
            batch_norm_scalar(act, "bn1")
            act.wait_ge(S["ff1"], 1)
            act.activation(halves(fT), PS[0:64, 0:2, 0:HALF], ACT.Relu, bias=cols["b1"][0:64, :]).then_inc(S["ff"], 1)
            batch_norm_scalar(act, "bn2")
            if layer == 1:
                for step in range(TILES + 4):
                    if step < TILES:
                        tile_root(act, b, S, "last", step)
                    if 1 <= step <= TILES:
                        m = step - 1
                        act.wait_ge(S["last_nmr"], m + 1)
                        act.activation(b.XN[:, m, :], PS[0:P, m, :], ACT.Identity, bias=b.nmr[:, m:m + 1],
                                       scale=b.rstd[:, m:m + 1]).then_inc(S["last_norm"], 1)
                    if 2 <= step <= TILES + 1:
                        tile_root(act, b, S, "pre", step - 2)
                    if step >= 4:
                        input_column(act, b, S, step - 4, 5 + (step - 4) % 3)

        @block.tensor
        def _(pe):
            pe.wait_ge(loaded, loads)
            pe.wait_ge(S["x_padding"], 2)
            PASSES = ((0, 0), (1, 0), (0, 1))
            for s, (matrix, half) in enumerate(STEPS_IN):
                pe.wait_ge(S["w_high"], s + 1)
                if s > 0:
                    pe.wait_ge(S["w_low"], s + 1)
                w = [part[:, s % 2, :, :] for part in parts.w]
                if matrix != "v":
                    side = "qk".index(matrix)
                    for c in (2 * half, 2 * half + 1):
                        if c >= 2:
                            pe.wait_ge(S[("q_out", "k_out")[side]], c - 1)
                        for n, (px, pw) in enumerate(PASSES):
                            if s == 0 and c == 0 and n == 2:
                                pe.wait_ge(S["w_low"], 1)
                            for k in range(K):
                                if s == 0 and c == 0 and n < 2:
                                    pe.wait_ge(S[("x_high", "x_low")[n]], k + 1)
                                for h in range(2):
                                    last = pe.matmul(PS[:, 4 * (c % 2) + 2 * side + h, 0:EVEN_HALF],
                                                     w[pw][:, k, (c % 2) * 128:(c % 2 + 1) * 128],
                                                     parts.x[px][:, k, h * EVEN_HALF:(h + 1) * EVEN_HALF],
                                                     start=(n == 0 and k == 0), stop=(n == 2 and k == K - 1))
                        last.then_inc(S[matrix], 1)
                    continue
                if half == 0:
                    pe.wait_ge(S["q_out"], K)
                    pe.wait_ge(S["k_out"], K)
                for m in range(TILES):
                    last = accumulate(pe, PS[:, m, half * HALF_D:(half + 1) * HALF_D],
                                      [(parts.x_tile(px, k, m), w[pw][:, k, :]) for k in range(K) for px, pw in PASSES])
                    if half == 1:
                        last.then_inc(S["v"], 1)
            pe.wait_ge(S["v_out"], TILES)

            def scores(n):
                m, pair = divmod(n, PAIRS)
                if n >= 1:
                    pe.wait_ge(S["scored"], 2 * n)
                for half in range(2):
                    for e in range(2):
                        rows = slice(DH * e, DH * e + DH)
                        last = pe.matmul(PS[0:P, 2 * e + half, 0:HALF], qT[rows, pair, m * P:(m + 1) * P],
                                         kT[rows, pair, half * HALF:(half + 1) * HALF], start=True, stop=True)
                last.then_inc(S["scores"], 1)

            def turn(n):
                pe.wait_ge(S["scaled"], 2 * n + 2)
                if n >= 1:
                    pe.wait_ge(S["turned_first"], n)
                    pe.wait_ge(S["turned_last"], n)
                for e in range(2):
                    for s in range(TILES):
                        bank, at = (4 + e, s * P) if s < 4 else (6, e * P)
                        last = pe.transpose(PS[0:P, bank, at:at + P], ring[n % RING][:, e, s * P:(s + 1) * P],
                                            b.ident[0:P, 0:P])
                last.then_inc(S["turned"], 1)

            def weigh(n):
                m, pair = divmod(n, PAIRS)
                if pair == 0 and m >= 1:
                    pe.wait_ge(S["att_columns"], m)
                pe.wait_ge(S["turned_first"], n + 1)
                pe.wait_ge(S["turned_last"], n + 1)
                for s in range(TILES):
                    for e in range(2):
                        at = (2 * pair + e) * DH
                        last = pe.matmul(PS[DH * e:DH * e + DH, 7, pair * P:(pair + 1) * P], v[:, s, at:at + DH],
                                         pT[:, n % 2, e, s, :], start=(s == 0), stop=(s == TILES - 1),
                                         skip_group_check=True)
                last.then_inc(S["pv"], 1)

            for n in range(ITEMS + 3):
                if n < ITEMS:
                    scores(n)
                if 2 <= n < ITEMS + 2:
                    turn(n - 2)
                if n >= 3:
                    weigh(n - 3)
            pe.wait_ge(S["att_columns"], TILES)
            pe.wait_ge(S["padding"], 1)
            for c in range(K):
                for h in range(2):
                    last = accumulate(pe, PS[:, 2 * c + h, 0:HALF],
                                      [(wo[:, k, c * 128:(c + 1) * 128], aT[:, k, h * HALF:(h + 1) * HALF])
                                       for k in range(K)])
                last.then_inc(S["wo"], 1)
            for k in range(K):
                pe.wait_ge(S[("bn1_even", "bn1_odd")[k % 2]], k // 2 + 1)
                for h in range(2):
                    last = pe.matmul(PS[0:64, h, 0:HALF], w1[:, k, :], b.XT[:, k, h * HALF:(h + 1) * HALF],
                                     start=(k == 0), stop=(k == K - 1))
            last.then_inc(S["ff1"], 1)
            pe.wait_ge(S["ff"], 1)
            for c in range(K):
                for h in range(2):
                    last = pe.matmul(PS[:, 2 * c + h, 0:HALF], w2[:, c * 128:(c + 1) * 128],
                                     fT[:, h * HALF:(h + 1) * HALF], start=True, stop=True)
                last.then_inc(S["ff2"], 1)
            if layer == 1:
                pe.wait_ge(S["bn2_even"], K // 2)
                pe.wait_ge(S["bn2_odd"], K // 2)
                for m in range(TILES):
                    for k in range(K):
                        last = pe.transpose(PS[0:P, m, k * 128:(k + 1) * 128], tile_of(b.XT, k, m), b.ident[:, :])
                    last.then_inc(S["rows"], 1)
                for m in range(TILES):
                    if m >= 3:
                        pe.wait_ge(S["pre_columns"], m - 2)
                    input_turn(pe, b, S, m, 5 + m % 3)



def relations(nc, b, t, layer, slot, loaded, loads, load_next, C2):
    S = Semaphores(nc, b.part)
    PS = b.psum
    W = b.W[slot]
    mixed = W[:, 0:STEPS * D].rearrange("p (a n) -> p a n", a=STEPS)
    root = W[:, STEPS * D:STEPS * D + K * D].rearrange("p (k n) -> p k n", k=K)
    bias = b.V[slot][0:P, 0:D]
    gate = b.U[slot][:, 0:2 * K].rearrange("p (k r) -> p k r", k=K)
    g = b.sb("gates", [P, TILES, 2])
    xg = b.sb("gated", [P, 2, TILES, D])
    yT = b.sb("gathered_columns", [128, STEPS, PADDED])

    UNITS = 4 * K

    def gathered(n, part):
        c, r, h = n // 4, n // 2 % 2, n % 2
        return yT[64 * r:64 * r + 64, 2 * c + part, h * HALF:(h + 1) * HALF], 5 + n % 3

    with nc.Block() as block:
        @block.sync
        def _(sp):
            if layer == 0:
                for r in range(2):
                    sp.dma_start(C2[:, r, :, :].rearrange("p m n -> p (m n)"), b.counts_dram[1 + r]
                                 ).then_inc(b.relations_loaded, 16)
            load_next(sp)

        @block.vector
        def _(dve):
            dve.wait_ge(S["gate_exp"], 1)
            dve.tensor_scalar(g[:, :, :], g[:, :, :], 1.0, None, ALU.add).then_inc(S["gate"], 1)
            dve.wait_ge(S["gate"], 1)
            dve.reciprocal(g[:, :, :], g[:, :, :]).then_inc(S["gate"], 1)
            dve.wait_ge(S["gate"], 2)
            for m in range(TILES):
                dve.tensor_scalar(xg[:, 1, m, :], b.XN[:, m, :], g[:, m, 1:2], None, ALU.mult).then_inc(S["gated_1"], 1)
            for n in range(UNITS):
                dve.wait_ge(S["gathered"], n + 1)
                out, bank = gathered(n, 0)
                dve.tensor_copy(out, PS[0:64, bank, 0:HALF]).then_inc(S["y_low"], 1)
            dve.wait_ge(loaded, loads)
            for m in range(TILES):
                dve.wait_ge(S["sum"], m + 1)
                if layer == 0:
                    dve.tensor_tensor(xg[:, 0, m, :], PS[0:P, m, :], bias, ALU.add).then_inc(S["biased"], 1)
                else:
                    dve.tensor_tensor(xg[:, 0, m, :], PS[0:P, m, :], bias, ALU.add).then_inc(S["biased"], 1)
                    dve.wait_ge(S["biased"], m + 1)
                    dve.tensor_tensor(b.X[:, m, :], xg[:, 0, m, :], b.X[:, m, :], ALU.add).then_inc(S["added"], 1)
                    dve.wait_ge(S["added"], m + 1)
                    input_rows(dve, b, S, m)

        @block.scalar
        def _(act):
            act.wait_ge(S["logits"], 1)
            act.activation(g[:, :, :], PS[0:P, 7, 0:2 * TILES].rearrange("p (m r) -> p m r", m=TILES), ACT.Exp, scale=-1.0
                           ).then_inc(S["gate_exp"], 1)
            act.wait_ge(S["gate"], 2)
            for m in range(TILES):
                act.activation(xg[:, 0, m, :], b.XN[:, m, :], ACT.Copy, scale=g[:, m, 0:1]).then_inc(S["gated_0"], 1)
            for n in range(UNITS):
                act.wait_ge(S["gathered"], n + 1)
                out, bank = gathered(n, 1)
                act.activation(out, PS[64:128, bank, 0:HALF], ACT.Copy).then_inc(S["y_high"], 1)
            if layer == 0:
                for m in range(TILES):
                    act.wait_ge(S["biased"], m + 1)
                    act.activation(b.XN[:, m, :], xg[:, 0, m, :], ACT.Relu).then_inc(S["x_rows"], 1)
                for m in range(TILES):
                    act.wait_ge(S["x_turned"], m + 1)
                    act.activation(b.XT[:, :, m * P:(m + 1) * P], PS[:, m, 0:K * P].rearrange("p (k n) -> p k n", k=K),
                                   ACT.Copy).then_inc(S["x_columns"], 1)
            else:
                input_columns(act, b, S, lambda m: 5 + m % 3, 2)

        @block.tensor
        def _(pe):
            pe.wait_ge(loaded, loads)
            logits_tensor(pe, b, S, gate, 2)
            for m in range(TILES):
                for k in range(K):
                    pe.matmul(PS[0:P, m, :], tile_of(b.XT, k, m), root[:, k, :], start=(k == 0), stop=False,
                              skip_group_check=True)
            pe.wait_ge(b.relations_loaded, 32)
            pe.wait_ge(S["gated_0"], TILES)
            pe.wait_ge(S["gated_1"], TILES)
            for n in range(UNITS):
                c, r, h = n // 4, n // 2 % 2, n % 2
                if n >= 3:
                    pe.wait_ge(S["y_low"], n - 2)
                    pe.wait_ge(S["y_high"], n - 2)
                accumulate(pe, PS[:, 5 + n % 3, 0:HALF],
                           [(xg[:, r, m, c * 128:(c + 1) * 128], C2[:, r, m, h * HALF:(h + 1) * HALF])
                            for m in range(TILES)]).then_inc(S["gathered"], 1)
            for m in range(TILES):
                for a in range(STEPS):
                    if m == 0 and a % 2 == 0:
                        pe.wait_ge(S["y_low"], 2 * a + 4)
                        pe.wait_ge(S["y_high"], 2 * a + 4)
                    last = pe.matmul(PS[0:P, m, :], tile_of(yT, a, m), mixed[:, a, :], start=False, stop=(a == STEPS - 1),
                                     skip_group_check=True)
                last.then_inc(S["sum"], 1)
                if layer == 1 and m >= 2:
                    input_turn(pe, b, S, m - 2, 5 + (m - 2) % 3)
            if layer == 1:
                for m in (TILES - 2, TILES - 1):
                    pe.wait_ge(S["pre_columns"], m - 2)
                    input_turn(pe, b, S, m, 5 + m % 3)
            if layer == 0:
                for m in range(TILES):
                    pe.wait_ge(S["x_rows"], m + 1)
                    for k in range(K):
                        last = pe.transpose(PS[:, m, k * P:(k + 1) * P], b.XN[:, m, k * 128:(k + 1) * 128],
                                            b.ident[0:P, 0:P])
                    last.then_inc(S["x_turned"], 1)



def ffn_top2(nc, b, t, slot, loaded, loads, load_next):
    S = Semaphores(nc, b.part)
    PS = b.psum
    E = 8
    FILL = 6
    W = b.W[slot]
    w1 = W[:, 0:K * D].rearrange("p (k n) -> p k n", k=K)
    w2 = W[:, K * D:2 * K * D].rearrange("p (k n) -> p k n", k=K)
    b2 = W[:, 2 * K * D:2 * K * D + D]
    gamma = b.V[slot][0:P, :].rearrange("p (e n) -> p e n", e=E)
    router = b.U[slot][:, 0:K * E].rearrange("p (k e) -> p k e", k=K)
    b1 = b.U[slot][:, K * E:K * E + K]
    lg = b.sb("router_logits", [P, TILES, E + FILL])
    lg2 = b.sb("router_taken", [P, TILES, E + FILL])
    top8 = b.sb("router_top8", [P, TILES, 8])
    sel = b.sb("router_sel", [P, TILES, E])
    w = b.sb("router_weights", [P, TILES, E])
    s = b.sb("router_sums", [P, TILES])
    wT = b.sb("router_columns", [E, NODES])
    beta = b.sb("beta", [E, D])
    fT = b.sb("hidden_columns", [128, K, PADDED])
    PART_ROWS = (slice(0, 32), slice(32, 64), slice(64, 128))
    b2_parts = nc.alloc_sbuf_tensor(f"{b.part}_b2_parts", [128, D], BF16)
    b2_high = nc.alloc_sbuf_tensor(f"{b.part}_b2_high", [128, 2, D], BF16)
    b2_rest = b.sb("b2_rest", [128, 2, D])
    one_row = nc.alloc_sbuf_tensor(f"{b.part}_one_row_of_b2", [128, E, P], BF16)
    PAIRS = E // 2
    y = b.sb("y", [P, 2, TILES, 2, D])
    st = b.sb("y_stats", [P, 2, TILES, 2, 6])
    mv = b.sb("y_mean", [P, 2, TILES, 2, 2])
    sd = b.sb("y_root", [P, 2, TILES, 2])
    ws = b.sb("y_scale", [P, 2, TILES, 2])
    nm = b.sb("y_shift", [P, 2, TILES, 2])
    VECTOR_GAINS = (1, 2, 4)

    def banks(n):
        slot = 2 + n % 2 if n < 2 * TILES else n % 4
        return 2 * slot, n - 1 if n < 2 * TILES + 2 else n - 3 if n >= 2 * TILES + 4 else 0

    with nc.Block() as block:
        @block.sync
        def _(sp):
            sp.dma_start(beta[:, :], t["L2_ffn_beta"]).then_inc(S["beta_in"], 16)
            load_next(sp)

        def gain(engine, q, m):
            engine.wait_ge(S["y_norm"], 2 * (q * TILES + m + 1))
            engine.tensor_tensor(y[:, q % 2, m, :, :], y[:, q % 2, m, :, :], gamma[:, 2 * q:2 * q + 2, :], ALU.mult
                                 ).then_inc(S["gained_vector" if engine is nc.vector else "gained_pool"], 1)

        @block.gpsimd
        def _(pool):
            for n, rows in enumerate(PART_ROWS):
                first = rows.start
                pool.tensor_copy(one_row[rows, :, :],
                                 b.ident[rows, first:first + E].unsqueeze(2).to_broadcast([rows.stop - first, E, P])
                                 ).then_inc(S["one_row"], 1)
                pool.wait_ge(S["one_row"], n + 1)
            pool.wait_ge(loaded, loads)
            rest = b2
            for n, rows in enumerate(PART_ROWS):
                pool.tensor_copy(b2_parts[rows, :], rest[rows, :]).then_inc(S["b2_parts"], 1)
                pool.wait_ge(S["b2_parts"], n + 1)
                if n < 2:
                    pool.tensor_copy(b2_high[:, n, :], rest).then_inc(S["b2_high"], 1)
                    pool.wait_ge(S["b2_high"], n + 1)
                    pool.tensor_tensor(b2_rest[:, n, :], rest, b2_high[:, n, :], ALU.subtract).then_inc(S["b2_rest"], 1)
                    pool.wait_ge(S["b2_rest"], n + 1)
                    rest = b2_rest[:, n, :]
            for q in range(PAIRS):
                for m in range(TILES):
                    if q < PAIRS - 1 or m not in VECTOR_GAINS:
                        gain(nc.gpsimd, q, m)
                    if q < PAIRS - 1:
                        pool.wait_ge(S["gained_pool"], q * TILES + m + 1)
                        pool.tensor_tensor(y[:, q % 2, m, 0, :], y[:, q % 2, m, 0, :], y[:, q % 2, m, 1, :], ALU.add
                                           ).then_inc(S["paired"], 1)

        @block.vector
        def _(dve):
            dve.memset(lg[:, :, E:], 3e38).then_inc(S["route"], 1)
            dve.wait_ge(S["logits"], 1)
            dve.tensor_copy(lg[:, :, 0:E], PS[0:P, 7, 0:TILES * E].rearrange("p (m e) -> p m e", m=TILES)
                            ).then_inc(S["route"], 1)
            dve.wait_ge(S["route"], 2)
            for m in range(TILES):
                dve.max(top8[:, m, :], lg[:, m, :]).then_inc(S["top8"], 1)
            for m in range(TILES):
                dve.wait_ge(S["top8"], m + 1)
                dve.match_replace(lg2[:, m, :], top8[:, m, :], lg[:, m, :], -3e38).then_inc(S["route"], 1)
            dve.wait_ge(S["route"], 2 + TILES)
            dve.tensor_tensor(sel[:, :, :], lg[:, :, 0:E], lg2[:, :, 0:E], ALU.not_equal).then_inc(S["route"], 1)
            dve.tensor_tensor(w[:, :, :], lg[:, :, 0:E], top8[:, :, FILL:FILL + 1].to_broadcast([P, TILES, E]),
                              ALU.subtract).then_inc(S["route_shifted"], 1)
            dve.wait_ge(S["route_exp"], 1)
            dve.wait_ge(S["route"], 3 + TILES)
            dve.tensor_tensor(w[:, :, :], w[:, :, :], sel[:, :, :], ALU.mult).then_inc(S["route"], 1)
            dve.wait_ge(S["route"], 4 + TILES)
            dve.tensor_reduce(s[:, :], w[:, :, :], AX.X, ALU.add).then_inc(S["route"], 1)
            dve.wait_ge(S["route"], 5 + TILES)
            dve.reciprocal(s[:, :], s[:, :]).then_inc(S["route"], 1)
            dve.wait_ge(S["route"], 6 + TILES)
            dve.tensor_tensor(w[:, :, :], w[:, :, :], spread(s[:, :], E), ALU.mult).then_inc(S["gates"], 1)
            dve.wait_ge(S["gates"], 1)

            def add_pair(q):
                for m in range(TILES):
                    dve.wait_ge(S["paired"], q * TILES + m + 1)
                    if q == 0:
                        dve.wait_ge(S["betas_out"], m + 1)
                    else:
                        dve.wait_ge(S["added"], (q - 1) * TILES + m + 1)
                    dve.tensor_tensor(b.X[:, m, :], b.X[:, m, :], y[:, q % 2, m, 0, :], ALU.add).then_inc(S["added"], 1)

            def add_last(j, m):
                if m in VECTOR_GAINS:
                    dve.wait_ge(S["gained_vector"], VECTOR_GAINS.index(m) + 1)
                else:
                    dve.wait_ge(S["gained_pool"], (PAIRS - 1) * TILES + (0, 3).index(m) + 1)
                dve.tensor_tensor(b.X[:, m, :], b.X[:, m, :], y[:, (PAIRS - 1) % 2, m, j, :], ALU.add
                                  ).then_inc(S[f"last_added{j}"], 1)

            for q in range(PAIRS):
                o = q % 2
                for m in range(TILES):
                    n = q * TILES + m
                    bank, _ = banks(n)
                    dve.wait_ge(S["expert"], n + 1)
                    if q >= 2:
                        dve.wait_ge(S["added"], (q - 2) * TILES + m + 1)
                    dve.tensor_tensor(y[:, o, m, :, :], PS[0:P, bank:bank + 2, :],
                                      b.XN[:, m:m + 1, :].to_broadcast([P, 2, D]), ALU.add).then_inc(S["y_sum"], 1)
                    dve.wait_ge(S["y_sum"], n + 1)
                    for j in range(2):
                        dve.bn_stats(st[:, o, m, j, :], y[:, o, m, j, :]).then_inc(S["y_stats"], 1)
                dve.wait_ge(S["y_stats"], 2 * TILES * (q + 1))
                for m in range(TILES):
                    for j in range(2):
                        dve.bn_aggr(mv[:, o, m, j, :], st[:, o, m, j, :]).then_inc(S["y_aggr"], 1)
                dve.wait_ge(S["y_aggr"], 2 * TILES * (q + 1))
                dve.tensor_scalar(sd[:, o, :, :], mv[:, o, :, :, 1], 1e-6, None, ALU.add).then_inc(S["y_var"], 1)
                dve.wait_ge(S["y_root"], q + 1)
                dve.reciprocal(ws[:, o, :, :], sd[:, o, :, :]).then_inc(S["y_scale"], 1)
                dve.wait_ge(S["y_scale"], 2 * q + 1)
                dve.tensor_tensor(ws[:, o, :, :], ws[:, o, :, :], w[:, :, 2 * q:2 * q + 2], ALU.mult).then_inc(S["y_scale"], 1)
                dve.wait_ge(S["y_scale"], 2 * q + 2)
                dve.scalar_tensor_tensor(nm[:, o, :, :], mv[:, o, :, :, 0], -1.0, ws[:, o, :, :], ALU.mult, ALU.mult
                                         ).then_inc(S["y_shift"], 1)
                if q == 0:
                    dve.wait_ge(S["gates_turned"], 1)
                    dve.tensor_copy(wT[:, 0:4 * P], PS[0:E, 0, 0:4 * P]).then_inc(S["gates_out"], 1)
                    dve.tensor_copy(wT[:, 4 * P:], PS[0:E, 1, 0:P]).then_inc(S["gates_out"], 1)
                if q == 1:
                    for m in range(TILES):
                        dve.wait_ge(S["betas"], m + 1)
                        dve.tensor_tensor(b.X[:, m, :], PS[0:P, 2 + m % 2, :], b.X[:, m, :], ALU.add
                                          ).then_inc(S["betas_out"], 1)
                if q >= 1:
                    add_pair(q - 1)
            dve.wait_ge(S["added"], TILES * (PAIRS - 1))
            gain(nc.vector, PAIRS - 1, 1)
            add_last(0, 0)
            add_last(0, 1)
            gain(nc.vector, PAIRS - 1, 2)
            dve.wait_ge(S["last_added0"], 2)
            add_last(1, 0)
            add_last(1, 1)
            add_last(0, 2)
            gain(nc.vector, PAIRS - 1, 4)
            dve.wait_ge(S["last_added0"], 3)
            add_last(1, 2)
            add_last(0, 3)
            add_last(0, 4)
            dve.wait_ge(S["last_added0"], 5)
            add_last(1, 3)
            add_last(1, 4)
            for m in range(TILES):
                dve.wait_ge(S["last_added1"], m + 1)
                begin_stats(dve, b, S, "pre", m, [b.X[:, m, :]])
                if m >= 1:
                    input_scale(dve, b, S, m - 1)
            input_scale(dve, b, S, TILES - 1)

        @block.scalar
        def _(act):

            def hidden_columns(c):
                act.wait_ge(S["hidden"], c + 1)
                bank = 2 * (c % 2)
                act.activation(halves(fT[:, c, :]), PS[:, bank:bank + 2, 0:HALF], ACT.Relu, bias=b1[:, c:c + 1]
                               ).then_inc(S["hidden_out"], 1)

            hidden_columns(0)
            hidden_columns(1)
            act.wait_ge(S["route_shifted"], 1)
            act.activation(w[:, :, :], w[:, :, :], ACT.Exp).then_inc(S["route_exp"], 1)
            hidden_columns(2)
            hidden_columns(3)
            for q in range(PAIRS):
                act.wait_ge(S["y_var"], q + 1)
                act.activation(sd[:, q % 2, :, :], sd[:, q % 2, :, :], ACT.Sqrt).then_inc(S["y_root"], 1)
                act.wait_ge(S["y_shift"], q + 1)
                for m in range(TILES):
                    for j in range(2):
                        act.activation(y[:, q % 2, m, j, :], y[:, q % 2, m, j, :], ACT.Identity,
                                       bias=nm[:, q % 2, m, j:j + 1], scale=ws[:, q % 2, m, j:j + 1]
                                       ).then_inc(S["y_norm"], 1)
            input_columns(act, b, S, lambda m: m % 4, 1)

        @block.tensor
        def _(pe):
            pe.wait_ge(loaded, loads)
            logits_tensor(pe, b, S, router, E)

            def hidden(c):
                if c >= 2:
                    pe.wait_ge(S["hidden_out"], c - 1)
                for h in range(2):
                    last = accumulate(pe, PS[:, 2 * (c % 2) + h, 0:HALF],
                                      [(w1[:, k, c * 128:(c + 1) * 128], b.XT[:, k, h * HALF:(h + 1) * HALF])
                                       for k in range(K)])
                last.then_inc(S["hidden"], 1)

            def expert_pair(q):
                pe.wait_ge(S["hidden_out"], q + 1)
                for m in range(TILES):
                    n = q * TILES + m
                    bank, left = banks(n)
                    if left > 0:
                        pe.wait_ge(S["y_sum"], left)
                    for j in range(2):
                        pe.matmul(PS[0:P, bank + j, :], one_row[:, 2 * q + j, :], b2_parts[:, :], start=True, stop=False)
                    for j in range(2):
                        rows = slice(64 * j, 64 * j + 64)
                        last = pe.matmul(PS[0:P, bank + j, :], fT[rows, q, m * P:(m + 1) * P], w2[rows, q, :],
                                         start=False, stop=True)
                    last.then_inc(S["expert"], 1)

            hidden(0)
            hidden(1)
            pe.wait_ge(S["route"], 2)
            pe.wait_ge(S["one_row"], 3)
            pe.wait_ge(S["b2_parts"], 3)
            expert_pair(0)
            hidden(2)
            hidden(3)
            pe.wait_ge(S["hidden_out"], K)
            pe.wait_ge(S["gates"], 1)
            for m in range(TILES):
                last = pe.transpose(PS[0:E, m // 4, (m % 4) * P:(m % 4 + 1) * P], w[:, m, :], b.ident[0:P, 0:P])
            last.then_inc(S["gates_turned"], 1)
            expert_pair(1)
            pe.wait_ge(S["gates_out"], 2)
            pe.wait_ge(S["beta_in"], 16)
            for m in range(TILES):
                if m >= 2:
                    pe.wait_ge(S["betas_out"], m - 1)
                pe.matmul(PS[0:P, 2 + m % 2, :], wT[:, m * P:(m + 1) * P], beta[:, :], start=True, stop=True
                          ).then_inc(S["betas"], 1)
            pe.wait_ge(S["betas_out"], TILES)
            expert_pair(2)
            expert_pair(3)
            for m in range(TILES):
                if m >= 4:
                    pe.wait_ge(S["pre_columns"], m - 3)
                input_turn(pe, b, S, m, m % 4)



def isomorphism(nc, b, t, slot, loaded, loads, load_next):
    S = Semaphores(nc, b.part)
    PS = b.psum
    W = b.W[slot]
    b1 = b.U[slot][:, 0:K]
    b2 = b.V[slot][0:P, 0:D]
    hT = b.sb("h_columns", [128, K, PADDED])
    fT = b.V[slot][:, D:D + K * PADDED].rearrange("p (k n) -> p k n", k=K)
    parts = Halves(b)
    EVEN_HALF = Halves.WIDTH // 2
    w1, w2 = ([part[:, n, :].rearrange("p (k n) -> p k n", k=K) for part in parts.w] for n in range(2))
    PASSES = ((0, 0), (1, 0), (0, 1))

    with nc.Block() as block:
        @block.sync
        def _(sp):
            load_next(sp)

        @block.gpsimd
        def _(pool):
            for n in range(2):
                parts.split_w_low(pool, S, W, n)

        @block.vector
        def _(dve):
            for x in parts.x:
                dve.tensor_scalar(x[:, :, NODES:], b.XT[:, :, 0:Halves.WIDTH - NODES], 0.0, None, ALU.mult
                                  ).then_inc(S["x_padding"], 1)
            dve.wait_ge(loaded, loads)
            for m in range(TILES):
                dve.tensor_tensor(b.X[:, m, :], b.X[:, m, :], b2, ALU.add).then_inc(S["b2"], 1)
            for c in range(K):
                dve.wait_ge(S["aggregated"], c + 1)
                dve.tensor_tensor(halves(hT[:, c, :]), PS[:, 2 * c:2 * c + 2, 0:HALF], halves(b.XT[:, c, :]), ALU.add
                                  ).then_inc(S["h"], 1)
                dve.wait_ge(S["h"], c + 1)
                dve.tensor_copy(parts.x[0][:, c, 0:NODES], hT[:, c, 0:NODES]).then_inc(S["h_high"], 1)
                dve.wait_ge(S["h_high"], c + 1)
                dve.tensor_tensor(parts.x[1][:, c, 0:NODES], hT[:, c, 0:NODES], parts.x[0][:, c, 0:NODES].bitcast(F32),
                                  ALU.subtract).then_inc(S["h_low"], 1)
            for c in range(K):
                dve.wait_ge(S["up"], K)
                dve.wait_ge(S["f_high"], c + 1)
                dve.tensor_tensor(parts.x[1][:, c, 0:NODES], fT[:, c, 0:NODES], parts.x[0][:, c, 0:NODES].bitcast(F32),
                                  ALU.subtract).then_inc(S["f_low"], 1)
            dve.wait_ge(S["b2"], TILES)
            for m in range(TILES):
                dve.wait_ge(S["down"], m + 1)
                dve.tensor_tensor(b.X[:, m, :], PS[0:P, m, :], b.X[:, m, :], ALU.add).then_inc(S["added"], 1)
                dve.wait_ge(S["added"], m + 1)
                input_rows(dve, b, S, m)

        @block.scalar
        def _(act):
            act.wait_ge(loaded, loads)
            for n in range(2):
                parts.split_w_high(act, S, W, n)
            for c in range(K):
                act.wait_ge(S["up"], c + 1)
                act.activation(halves(fT[:, c, :]), PS[:, 2 * c:2 * c + 2, 0:HALF], ACT.Relu, bias=b1[:, c:c + 1]
                               ).then_inc(S["up_out"], 1)
            act.wait_ge(S["up_out"], K)
            for c in range(K):
                act.activation(parts.x[0][:, c, 0:NODES], fT[:, c, 0:NODES], ACT.Copy).then_inc(S["f_high"], 1)
            input_columns(act, b, S, lambda m: 5 + m % 3, 2)

        @block.tensor
        def _(pe):
            for c in range(K):
                for h in range(2):
                    last = accumulate(pe, PS[:, 2 * c + h, 0:HALF],
                                      [(b.XN[:, m, c * 128:(c + 1) * 128], b.CT[:, m, h * HALF:(h + 1) * HALF])
                                       for m in range(TILES)])
                last.then_inc(S["aggregated"], 1)
            pe.wait_ge(S["h_low"], K)
            pe.wait_ge(S["x_padding"], 2)
            pe.wait_ge(S["w_low"], 2)
            for c in range(K):
                for h in range(2):
                    last = accumulate(pe, PS[:, 2 * c + h, 0:EVEN_HALF],
                                      [(w1[pw][:, k, c * 128:(c + 1) * 128],
                                        parts.x[px][:, k, h * HALF:h * HALF + EVEN_HALF])
                                       for px, pw in PASSES for k in range(K)])
                last.then_inc(S["up"], 1)
            for m in range(TILES):
                for n, (px, pw) in enumerate(PASSES):
                    for k in range(K):
                        if m == 0 and n < 2:
                            pe.wait_ge(S[("f_high", "f_low")[n]], k + 1)
                        last = pe.matmul(PS[:, m, :], parts.x_tile(px, k, m), w2[pw][:, k, :],
                                         start=(n == 0 and k == 0), stop=(n == 2 and k == K - 1))
                last.then_inc(S["down"], 1)
                if m >= 2:
                    input_turn(pe, b, S, m - 2, 5 + (m - 2) % 3)
            for m in (TILES - 2, TILES - 1):
                pe.wait_ge(S["pre_columns"], m - 2)
                input_turn(pe, b, S, m, 5 + m % 3)



def ffn_lora(nc, b, t, slot, loaded, loads, out):
    S = Semaphores(nc, b.part)
    PS = b.psum
    E, R = 4, 16
    W = b.W[slot]
    fc2 = b.W[1 - slot]
    gate = b.U[slot][:, 0:K * (E + 1)].rearrange("p (k e) -> p k e", k=K)
    down = b.V[slot][:, 0:E * K * R].rearrange("p (e k r) -> p e k r", e=E, k=K)
    up = b.V[slot][:, 256:256 + E * K * R].rearrange("p (e k r) -> p e k r", e=E, k=K)
    G = gate_buffers(b, E)
    ROWS = E * R
    parts = Halves(b)
    EVEN_HALF = parts.x[0].shape[2] // 2
    EVEN = 2 * EVEN_HALF
    down_wide = b.sb("down_wide", [128, E, K, ROWS])
    up_wide = b.sb("up_wide", [128, E, K, ROWS])
    rows_of = b.sb("rows_of_experts", [E, 2 * ROWS])
    up_fc2 = b.sb("up_times_fc2", [2 * ROWS, D])
    space = b.V[1 - slot]
    hT = space[:, 0:K * EVEN].rearrange("p (k n) -> p k n", k=K)
    wT = b.sb("gates_columns", [E, NODES])
    wide_w = b.sb("gates_of_rows", [2 * ROWS, EVEN])
    lT = space[:, K * EVEN:(K + 1) * EVEN]
    CHUNKS_H = E * K
    PRODUCT_BANKS = (0, 1, 2, 3, 5)

    with nc.Block() as block:
        @block.sync
        def _(sp):
            for e in range(E):
                sp.dma_start(fc2[:, e * K * D:(e + 1) * K * D].rearrange("p (k n) -> p k n", k=K),
                             t["lora_fc2"][e].rearrange("(k p) n -> p k n", p=128)).then_inc(S["fc2_in"], 16)
            for m in range(TILES):
                sp.wait_ge(S["added"], m + 1)
                sp.dma_start(out[m * P:(m + 1) * P, :], b.X[:, m, :]).then_inc(S["stored"], 16)
            sp.wait_ge(S["stored"], 16 * TILES)

        @block.gpsimd
        def _(pool):
            parts.split_w_low(pool, S, W, 0)
            pool.memset(down_wide[:, :, :, :], 0.0).then_inc(S["blank"], 1)
            pool.memset(up_wide[:, :, :, :], 0.0).then_inc(S["blank"], 1)
            pool.tensor_copy(rows_of[:, :].rearrange("e (j f r) -> e j f r", j=2, f=E),
                             b.ident[0:E, 0:E].unsqueeze(1).unsqueeze(3).to_broadcast([E, 2, E, R])
                             ).then_inc(S["rows_of"], 1)
            pool.wait_ge(loaded, loads)
            pool.wait_ge(S["blank"], 2)
            for e in range(E):
                pool.tensor_copy(down_wide[:, e, :, e * R:(e + 1) * R], down[:, e, :, :]).then_inc(S["down_wide"], 1)
            for e in range(1, E):
                parts.split_w_low(pool, S, W, e)
            for e in range(E):
                pool.tensor_copy(up_wide[:, e, :, e * R:(e + 1) * R], up[:, e, :, :]).then_inc(S["up_wide"], 1)

        @block.vector
        def _(dve):
            parts.split_x_low(dve, b, S)
            threshold_gates_vector(dve, b, S, G, E, None, 1.0 / E)
            dve.wait_ge(S["gates_turned"], 1)
            dve.tensor_copy(wT[:, 0:4 * P], PS[0:E, 4, 0:4 * P]).then_inc(S["gates_out"], 1)
            dve.tensor_copy(wT[:, 4 * P:], PS[0:E, 5, 0:P]).then_inc(S["gates_out"], 1)
            dve.wait_ge(S["gates_wide"], 1)
            dve.tensor_copy(halves(wide_w), PS[:, 4:6, 0:EVEN_HALF]).then_inc(S["wide_out"], 1)
            dve.wait_ge(S["fused"], 1)
            dve.tensor_copy(up_fc2[:, :], PS[:, 4, :]).then_inc(S["fused_out"], 1)
            dve.wait_ge(S["wide_out"], 1)
            dve.wait_ge(S["low"], CHUNKS_H // 2)
            for h in range(2):
                nodes = slice(h * EVEN_HALF, (h + 1) * EVEN_HALF)
                dve.tensor_tensor(lT[:, nodes], PS[:, 6 + h, 0:EVEN_HALF], wide_w[:, nodes], ALU.mult
                                  ).then_inc(S["low_columns"], 1)
            for m in range(TILES):
                dve.wait_ge(S["product"], m + 1)
                dve.tensor_tensor(b.X[:, m, :], PS[0:P, PRODUCT_BANKS[m], :], b.X[:, m, :], ALU.add
                                  ).then_inc(S["added"], 1)

        @block.scalar
        def _(act):
            parts.split_x_high(act, b, S)
            act.wait_ge(loaded, loads)
            parts.split_w_high(act, S, W, 0)
            threshold_gates_scalar(act, b, S, G, E)
            parts.split_w_high(act, S, W, 1)
            for n in range(CHUNKS_H):
                act.wait_ge(S["hidden"], n + 1)
                if n >= K:
                    act.wait_ge(S["low"], (n - K) // 2 + 1)
                bank = 2 * (n % 2)
                act.activation(halves(hT[:, n % K, :]), PS[:, bank:bank + 2, 0:EVEN_HALF], ACT.Relu
                               ).then_inc(S["hidden_out"], 1)
                if n % K == K - 1 and n // K + 2 < E:
                    parts.split_w_high(act, S, W, n // K + 2, "hidden", K)

        @block.tensor
        def _(pe):
            pe.wait_ge(loaded, loads)
            logits_tensor(pe, b, S, gate, E + 1)

            def hidden(n):
                e, c = divmod(n, K)
                if n >= 2:
                    pe.wait_ge(S["hidden_out"], n - 1)
                pe.wait_ge(S["x_low"], K)
                pe.wait_ge(S["x_padding"], 2)
                pe.wait_ge(S["w_low"], e + 1)
                for h in range(2):
                    last = accumulate(pe, PS[:, 2 * (n % 2) + h, 0:EVEN_HALF],
                                      [(parts.w[pw][:, e % 2, k * D + c * 128:k * D + (c + 1) * 128],
                                        parts.x[px][:, k, h * EVEN_HALF:(h + 1) * EVEN_HALF])
                                       for k in range(K) for px, pw in ((0, 0), (0, 1), (1, 0))])
                last.then_inc(S["hidden"], 1)

            def low(pair):
                pe.wait_ge(S["hidden_out"], 2 * pair + 2)
                for h in range(2):
                    for j in range(2):
                        e, c = divmod(2 * pair + j, K)
                        last = pe.matmul(PS[ROWS * j:ROWS * j + ROWS, 6 + h, 0:EVEN_HALF], down_wide[:, e, c, :],
                                         hT[:, c, h * EVEN_HALF:(h + 1) * EVEN_HALF], start=(pair == 0),
                                         stop=(pair == CHUNKS_H // 2 - 1), skip_group_check=True)
                last.then_inc(S["low"], 1)

            for n in range(CHUNKS_H):
                hidden(n)
                if n == 3:
                    pe.wait_ge(S["down_wide"], E)
                    pe.wait_ge(S["gate_shifted"], 1)
                if n >= 3 and n % 2:
                    low((n - 3) // 2)
                if n == 7:
                    pe.wait_ge(S["gates"], 1)
                    for m in range(TILES):
                        last = pe.transpose(PS[0:E, 4 + m // 4, (m % 4) * P:(m % 4 + 1) * P], G["w"][:, m, :],
                                            b.ident[0:P, 0:P])
                    last.then_inc(S["gates_turned"], 1)
                if n == 9:
                    pe.wait_ge(S["gates_out"], 2)
                    pe.wait_ge(S["rows_of"], 1)
                    pe.matmul(PS[:, 4, 0:EVEN_HALF], rows_of[:, :], wT[:, 0:EVEN_HALF], start=True, stop=True)
                    pe.matmul(PS[:, 5, 0:NODES - EVEN_HALF], rows_of[:, :], wT[:, EVEN_HALF:], start=True, stop=True
                              ).then_inc(S["gates_wide"], 1)
                if n == 11:
                    pe.wait_ge(S["fc2_in"], 16 * E)
                    pe.wait_ge(S["up_wide"], E)
                    pe.wait_ge(S["wide_out"], 1)
                    for n_term in range(E * K):
                        e, k = divmod(n_term, K)
                        for j in range(2):
                            last = pe.matmul(PS[ROWS * j:ROWS * j + ROWS, 4, :], up_wide[:, e, k, :],
                                             fc2[:, n_term * D:(n_term + 1) * D], start=(n_term == 0),
                                             stop=(n_term == E * K - 1), skip_group_check=True)
                    last.then_inc(S["fused"], 1)
            low(CHUNKS_H // 2 - 1)
            pe.wait_ge(S["fused_out"], 1)
            for m in range(TILES):
                pe.wait_ge(S["low_columns"], 1 if (m + 1) * P <= EVEN_HALF else 2)
                pe.matmul(PS[0:P, PRODUCT_BANKS[m], :], lT[:, m * P:(m + 1) * P], up_fc2[:, :], start=True, stop=True
                          ).then_inc(S["product"], 1)



class Buffers:

    def __init__(self, nc):
        self.nc, self.part = nc, "all"
        sb = self.sb

        self.ident = sb("ident", [128, 128])
        self.ones = sb("ones", [128, 128])
        self.X = sb("X", [P, TILES, D])
        self.XN = sb("XN", [P, TILES, D])
        self.XT = sb("XT", [128, K, PADDED])
        self.CT = sb("CT", [P, TILES, PADDED])
        self.W = [sb(f"W{n}", [128, 4 * K * D]) for n in range(2)]
        self.V = [sb(f"V{n}", [128, 8 * D]) for n in range(2)]
        self.U = [sb(f"U{n}", [128, 48]) for n in range(2)]
        self.stats = sb("stats", [P, TILES, 2, 6])
        self.mv = sb("mv", [P, TILES, 2])
        self.var = sb("var", [P, TILES])
        self.root = sb("root", [P, TILES])
        self.rstd = sb("rstd", [P, TILES])
        self.nmr = sb("nmr", [P, TILES])
        self.temperatures = sb("temperatures", [128, 3])
        self.extremes = sb("extremes", [P, TILES, 2])
        self.psum = nc.alloc_psum_tensor("PS", [128, 8, BANK], F32)
        self.mixed_dram = nc.dram_tensor("mixed_dram", [2, 128, STEPS * D], F32).ap()
        self.counts_dram = nc.dram_tensor("counts_dram", [3, P, TILES * PADDED], F32).ap()

    def sb(self, name, shape):
        return self.nc.alloc_sbuf_tensor(f"{self.part}_{name}", shape, F32)


def build(nc, t, out):
    b = Buffers(nc)
    loaders = ([lambda sp, s, d, n=n: load_conv(sp, b, t, s, d, n) for n in range(3)] +
               [lambda sp, s, d: load_experts(sp, b, t, s, d, "L0_ffn_W_exp", "L0_ffn_gate", "L0_ffn_gate_bias",
                                              "L0_ffn_b_exp")] +
               [lambda sp, s, d, n=n: load_attention(sp, b, t, s, d, n) for n in range(2)] +
               [lambda sp, s, d: load_experts(sp, b, t, s, d, "L1_ffn_experts", "L1_ffn_gate", None)] +
               [lambda sp, s, d, n=n: load_relations(sp, b, t, s, d, n) for n in range(2)] +
               [lambda sp, s, d: load_top2(sp, b, t, s, d),
                lambda sp, s, d: load_isomorphism(sp, b, t, s, d),
                lambda sp, s, d: load_lora(sp, b, t, s, d)])
    LOADS = [6, 7, 7, 7, 9, 9, 5, 4, 4, 5, 4, 7]
    numbers = iter(range(1 + len(loaders)))
    loaded = [nc.alloc_semaphore(f"loaded_{n}") for n in range(len(loaders))]
    b.counts_loaded = nc.alloc_semaphore("counts_loaded")
    b.relations_loaded = nc.alloc_semaphore("relations_loaded")

    def load_part(n, sp):
        if n < len(loaders):
            assert loaders[n](sp, n % 2, loaded[n]) == LOADS[n]

    def own(n):
        return n % 2, loaded[n], 16 * LOADS[n], lambda sp: load_part(n + 1, sp)

    def run(part, *args):
        with nc.cleanup_on_exit():
            b.part = f"part{next(numbers)}"
            part(nc, b, t, *args)

    def load_first(sp, rows_free):
        assert load_conv(sp, b, t, 0, loaded[0], 0, rows_free) == LOADS[0]
    run(count_edges, load_first)
    for n in range(3):
        run(conv, n, *own(n))
    with nc.sbuf_tensor("log_counts", [P, TILES, PADDED], F32) as C, nc.sbuf_tensor("edged", [P, TILES], F32) as edged:
        run(ffn_threshold, *own(3), C, edged)
        for n in range(2):
            run(attention, n, *own(4 + n), C, edged)
    run(ffn_sinkhorn, *own(6))
    with nc.sbuf_tensor("relation_counts", [P, 2, TILES, PADDED], F32) as C2:
        for n in range(2):
            run(relations, n, *own(7 + n), C2)
    run(ffn_top2, *own(9))
    run(isomorphism, *own(10))
    slot, done, loads, _ = own(11)
    run(ffn_lora, slot, done, loads, out)


def columns(v):
    import numpy as np
    v = np.asarray(v)
    v = v.reshape(len(v), -1)
    return np.ascontiguousarray(v.reshape(-1, 128, v.shape[1]).transpose(1, 0, 2).reshape(128, -1))


def laid_out(x):
    import numpy as np
    x = {n: np.ascontiguousarray(a) for n, a in x.items()}
    t = {n: x[n] for n in (
        "x", "src", "dst", "edge_type_2", "L0_gnn_cw", "L0_gnn_cb", "L0_ffn_W_exp", "L0_ffn_b_exp",
        "L1_gnn_ln_g", "L1_gnn_ln_b", "L1_ffn_experts", "L2_gnn_basis1", "L2_gnn_root1", "L2_gnn_bias1",
        "L2_gnn_basis2", "L2_gnn_root2", "L2_gnn_bias2", "L2_ffn_w2", "L2_ffn_gamma", "L2_ffn_beta",
        "L3_gnn_W1", "L3_gnn_W2", "L3_gnn_b2")}
    for i in range(3):
        for n in ("mw1", "mb1", "mw2", "mb2") + (("lng", "lnb") if i else ()):
            t[f"L0_gnn_{n}_{i}"] = x[f"L0_gnn_{n}_{i}"]
        t[f"conv_columns{i}"] = np.concatenate(
            [columns(x[f"L0_gnn_mlg_{i}"]), columns(x[f"L0_gnn_mlb_{i}"])], axis=1)
    t["L0_ffn_gate"] = columns(np.concatenate([x["L0_ffn_W_gate"], x["L0_ffn_W_thr"]], axis=1))
    t["L0_ffn_gate_bias"] = np.concatenate([x["L0_ffn_b_gate"], x["L0_ffn_b_thr"]])
    for n in "qkvo":
        t[f"att_W{n}"] = np.ascontiguousarray(x[f"L1_gnn_W{n}"].transpose(0, 2, 1))
    t["att_W1"] = np.ascontiguousarray(x["L1_gnn_W1"].transpose(0, 2, 1))
    t["att_W2"] = np.ascontiguousarray(x["L1_gnn_W2"].transpose(0, 2, 1))
    t["att_columns"] = np.stack([np.concatenate(
        [columns(x[f"L1_gnn_{n}"][i]) for n in ("bq", "bo", "b2", "g1", "beta1", "g2", "beta2")] +
        [np.tile(x["L1_gnn_b1"][i], 2)[:, None]], axis=1) for i in range(2)])
    t["L1_ffn_gate"] = columns(x["L1_ffn_gate_w"][0])
    for i in range(2):
        t[f"rel_columns{i}"] = columns(x[f"L2_gnn_gate_w{i + 1}"][:, :, 0].T)
    t["top2_w1"] = np.ascontiguousarray(x["L2_ffn_w1"].transpose(1, 0, 2).reshape(512, 512))
    t["top2_columns"] = np.concatenate([columns(x["L2_ffn_router_w"]), columns(x["L2_ffn_b1"].reshape(-1))], axis=1)
    t["top2_b2"] = np.pad(np.tile(np.pad(x["L2_ffn_b2"], ((0, 24), (0, 0))), (3, 1)), ((0, 32), (0, 0)))
    t["gin_columns"] = columns(x["L3_gnn_b1"])
    t["lora_gate"] = columns(np.concatenate([x["L3_ffn_gate_w"], x["L3_ffn_thr_w"]]).T)
    t["lora_fc1"] = np.ascontiguousarray(x["L3_ffn_fc1_w"].transpose(0, 2, 1))
    t["lora_fc2"] = np.ascontiguousarray(x["L3_ffn_fc2_w"].transpose(0, 2, 1))
    t["lora_down"] = np.concatenate([columns(a) for a in x["L3_ffn_lora_A"]], axis=1)
    t["lora_up"] = np.concatenate([columns(a.T) for a in x["L3_ffn_lora_B"]], axis=1)
    t["temperatures"] = np.tile(np.concatenate([x[f"L0_gnn_t{i}"] for i in range(3)]), (128, 1))
    t["ident"] = np.eye(128, dtype=np.float32)
    t["iota"] = np.tile(np.arange(NODES, dtype=np.float16), (P, 1))
    t["quarter"] = np.tile(np.eye(ROWS4, dtype=np.float32), (BASES, 1))
    t["atts"] = np.stack([np.repeat(x[f"L2_gnn_att{i + 1}"].T, ROWS4, axis=0) for i in range(2)], axis=1)
    return t


def kernel(**inputs):
    import numpy as np
    from concourse import bacc
    from concourse.bass_utils import run_bass_kernel_spmd

    nc = bacc.Bacc("TRN2", target_bir_lowering=False, num_devices=1)
    arrays = {f"in_{n}": np.ascontiguousarray(a) for n, a in laid_out(inputs).items()}
    t = {n[3:]: nc.dram_tensor(n, a.shape, mybir.dt.from_np(a.dtype), kind="ExternalInput").ap()
         for n, a in arrays.items()}
    out = nc.dram_tensor("out", [NODES, D], F32, kind="ExternalOutput").ap()
    build(nc, t, out)
    return run_bass_kernel_spmd(nc, [arrays], core_ids=[0]).results[0]["out"]
```
